# Optimizing a Trainium2 kernel written in Bass

```python
import numpy as np
import jax
import jax.numpy as jnp

def _softmax(x, axis=-1):
    return jax.nn.softmax(x, axis=axis)

def _gelu(x):
    return jax.nn.gelu(x, approximate=True)

def _silu(x):
    return jax.nn.silu(x)

def _sigmoid(x):
    return jax.nn.sigmoid(x)

def _layernorm(x, axis=-1, eps=1e-05):
    m = jnp.mean(x, axis=axis, keepdims=True)
    v = jnp.var(x, axis=axis, keepdims=True)
    return (x - m) / jnp.sqrt(v + eps)

def _scatter_add(tgt, idx, src, axis=0):
    return tgt.at[idx].add(src)

def _segment_sum(src, seg, n):
    return jax.ops.segment_sum(src, seg, n)
kernel_name = 'mk_decoder_postln_d1_seqx_r4_a57417'

def setup_inputs(seed: int=0):
    np.random.seed(seed)
    _w = jnp.asarray

    def _rec_inputs():
        import jax
        import jax.numpy as jnp
        _rk = jax.random.key(seed)
        x = -0.0003929 + 0.9999 * jax.random.normal(jax.random.fold_in(_rk, 1), (16, 256, 256), jnp.float32)
        _lenS = 256 - jax.random.randint(jax.random.fold_in(_rk, 7), (16,), 0, max(1, 256 // 4) + 1, jnp.int32)
        _lenS2 = 77 - jax.random.randint(jax.random.fold_in(_rk, 8), (16,), 0, max(1, 77 // 4) + 1, jnp.int32)
        _ctx_1024P = jax.random.normal(jax.random.fold_in(_rk, 11), (16, 16, 256), jnp.float32)
        _ctx_1024c = jax.random.dirichlet(jax.random.fold_in(_rk, 511), 0.3 * jnp.ones((16,), jnp.float32), (16, 77))
        _ctx_1024t = jnp.einsum('bsk,bkd->bsd', _ctx_1024c, _ctx_1024P)
        _ctx_1024t = _ctx_1024t * jax.lax.rsqrt(jnp.mean(jnp.square(_ctx_1024t)) + 1e-12) * 0.953939
        ctx_1024 = 2.81802e-05 + 1.00001 * (_ctx_1024t + 0.3 * jax.random.normal(jax.random.fold_in(_rk, 611), (16, 77, 256), jnp.float32))
        return (x, ctx_1024)
    x, ctx_1024 = _rec_inputs()

    def _L0_attn_setup():
        import jax, jax.numpy as jnp
        import numpy as np
        B, N, D, H = (4, 1024, 256, 16)
        HD = D // H

        def _kernel(x):
            return jax.nn.elu(x) + 1.0
        key = jax.random.key(seed)
        k1, k2, k3, k4 = jax.random.split(key, 4)
        x = jax.random.normal(k1, (B, N, D), dtype=jnp.float32)
        w_qkv = jax.random.normal(k2, (3 * D, D), dtype=jnp.float32) * (1.0 / np.sqrt(D))
        w_out = jax.random.normal(k3, (D, D), dtype=jnp.float32) * (1.0 / np.sqrt(D))
        b_out = jax.random.normal(k4, (D,), dtype=jnp.float32) * 0.01
        return {'x': x, 'w_qkv': w_qkv, 'w_out': w_out, 'b_out': b_out}
    _L0_attn_all = _L0_attn_setup()
    _L0_attn_in = {k: v for k, v in _L0_attn_all.items() if k in ('w_qkv', 'w_out', 'b_out')}
    del _L0_attn_all

    def _L0_xattn_setup():
        import jax, jax.numpy as jnp
        import numpy as np
        B, S, C = (8, 512, 256)
        key = jax.random.key(seed)
        ks = jax.random.split(key, 9)
        scale = 1.0 / np.sqrt(C)
        return {'x1': jax.random.normal(ks[0], (B, S, C), jnp.float32), 'x2': jax.random.normal(ks[1], (B, S, C), jnp.float32), 'x3': jax.random.normal(ks[2], (B, S, C), jnp.float32), 'Wq': jax.random.normal(ks[3], (C, C), jnp.float32) * scale, 'bq': jax.random.normal(ks[4], (C,), jnp.float32) * scale, 'Wk': jax.random.normal(ks[5], (C, C), jnp.float32) * scale, 'bk': jax.random.normal(ks[6], (C,), jnp.float32) * scale, 'Wv': jax.random.normal(ks[7], (C, C), jnp.float32) * scale, 'bv': jax.random.normal(ks[8], (C,), jnp.float32) * scale}
    _L0_xattn_all = _L0_xattn_setup()
    _L0_xattn_in = {k: v for k, v in _L0_xattn_all.items() if k in ('Wq', 'bq', 'Wk', 'bk', 'Wv', 'bv')}
    del _L0_xattn_all

    def _L0_ffn_setup():
        import jax, jax.numpy as jnp
        import numpy as np
        EPS = 1e-05
        NUM_HEADS = 16
        NUM_KV_HEADS = 4
        NUM_EXPERTS = 8
        TOP_K = 2

        def _layernorm(x, w, b):
            mu = jnp.mean(x, axis=-1, keepdims=True)
            var = jnp.mean((x - mu) ** 2, axis=-1, keepdims=True)
            return (x - mu) * jax.lax.rsqrt(var + EPS) * w + b
        key = jax.random.key(seed)
        ks = jax.random.split(key, 8)
        S, B, H = (256, 4, 256)
        F = 512
        hd = H // NUM_HEADS
        qkv_out = (NUM_HEADS + 2 * NUM_KV_HEADS) * hd
        w_scale = 0.02
        return {'hidden_states': jax.random.normal(ks[0], (S, B, H), jnp.float32), 'ln1_weight': jnp.ones((H,), jnp.float32), 'ln1_bias': jnp.zeros((H,), jnp.float32), 'ln2_weight': jnp.ones((H,), jnp.float32), 'ln2_bias': jnp.zeros((H,), jnp.float32), 'qkv_weight': jax.random.normal(ks[1], (qkv_out, H), jnp.float32) * w_scale, 'proj_weight': jax.random.normal(ks[2], (H, H), jnp.float32) * w_scale, 'router_weight': jax.random.normal(ks[3], (NUM_EXPERTS, H), jnp.float32) * w_scale, 'moe_w1': jax.random.normal(ks[4], (NUM_EXPERTS, H, F), jnp.float32) * w_scale, 'moe_w2': jax.random.normal(ks[5], (NUM_EXPERTS, F, H), jnp.float32) * w_scale}
    _L0_ffn_all = _L0_ffn_setup()
    _L0_ffn_in = {k: v for k, v in _L0_ffn_all.items() if k in ('ln1_weight', 'ln1_bias', 'ln2_weight', 'ln2_bias', 'qkv_weight', 'proj_weight', 'router_weight', 'moe_w1', 'moe_w2')}
    del _L0_ffn_all
    return {'x': x, 'ctx_1024': ctx_1024, 'L0_attn_w_qkv': _L0_attn_in['w_qkv'], 'L0_attn_w_out': _L0_attn_in['w_out'], 'L0_attn_b_out': _L0_attn_in['b_out'], 'L0_xattn_Wq': _L0_xattn_in['Wq'], 'L0_xattn_bq': _L0_xattn_in['bq'], 'L0_xattn_Wk': _L0_xattn_in['Wk'], 'L0_xattn_bk': _L0_xattn_in['bk'], 'L0_xattn_Wv': _L0_xattn_in['Wv'], 'L0_xattn_bv': _L0_xattn_in['bv'], 'L0_ffn_ln1_weight': _L0_ffn_in['ln1_weight'], 'L0_ffn_ln1_bias': _L0_ffn_in['ln1_bias'], 'L0_ffn_ln2_weight': _L0_ffn_in['ln2_weight'], 'L0_ffn_ln2_bias': _L0_ffn_in['ln2_bias'], 'L0_ffn_qkv_weight': _L0_ffn_in['qkv_weight'], 'L0_ffn_proj_weight': _L0_ffn_in['proj_weight'], 'L0_ffn_router_weight': _L0_ffn_in['router_weight'], 'L0_ffn_moe_w1': _L0_ffn_in['moe_w1'], 'L0_ffn_moe_w2': _L0_ffn_in['moe_w2']}

def reference(x, ctx_1024, L0_attn_w_qkv, L0_attn_w_out, L0_attn_b_out, L0_xattn_Wq, L0_xattn_bq, L0_xattn_Wk, L0_xattn_bk, L0_xattn_Wv, L0_xattn_bv, L0_ffn_ln1_weight, L0_ffn_ln1_bias, L0_ffn_ln2_weight, L0_ffn_ln2_bias, L0_ffn_qkv_weight, L0_ffn_proj_weight, L0_ffn_router_weight, L0_ffn_moe_w1, L0_ffn_moe_w2):
    import jax
    import jax.numpy as jnp

    def _L0_attn_ref(x, w_qkv, w_out, b_out):
        import jax, jax.numpy as jnp
        import numpy as np
        B, N, D, H = (4, 1024, 256, 16)
        HD = D // H

        def _kernel(x):
            return jax.nn.elu(x) + 1.0
        b, n, d = x.shape
        qkv = x @ w_qkv.T
        qkv = qkv.reshape(b, n, 3, H, HD)
        q, k, v = (qkv[:, :, 0], qkv[:, :, 1], qkv[:, :, 2])
        q = _kernel(q)
        k = _kernel(k)
        kv = jnp.einsum('bnhd,bnhm->bhdm', k, v)
        z = 1.0 / (jnp.einsum('bnhd,bhd->bnh', q, k.sum(axis=1)) + 1e-06)
        out = jnp.einsum('bnhd,bhdm,bnh->bnhm', q, kv, z)
        out = out.reshape(b, n, d)
        return out @ w_out.T + b_out

    def _L0_xattn_ref(x1, x2, x3, Wq, bq, Wk, bk, Wv, bv):
        import jax, jax.numpy as jnp
        import numpy as np
        B, S, C = (8, 512, 256)
        q = jnp.einsum('bsc,dc->bsd', x1, Wq) + bq
        k = jnp.einsum('bsc,dc->bsd', x2, Wk) + bk
        v = jnp.einsum('bsc,dc->bsd', x3, Wv) + bv
        scores = jnp.einsum('bqd,bkd->bqk', q, k)
        attn = jax.nn.softmax(scores, axis=-1)
        return jnp.einsum('bqk,bkd->bqd', attn, v)

    def _L0_ffn_ref(hidden_states, ln1_weight, ln1_bias, ln2_weight, ln2_bias, qkv_weight, proj_weight, router_weight, moe_w1, moe_w2):
        import jax, jax.numpy as jnp
        import numpy as np
        EPS = 1e-05
        NUM_HEADS = 16
        NUM_KV_HEADS = 4
        NUM_EXPERTS = 8
        TOP_K = 2

        def _layernorm(x, w, b):
            mu = jnp.mean(x, axis=-1, keepdims=True)
            var = jnp.mean((x - mu) ** 2, axis=-1, keepdims=True)
            return (x - mu) * jax.lax.rsqrt(var + EPS) * w + b
        S, B, H = hidden_states.shape
        hd = H // NUM_HEADS
        rep = NUM_HEADS // NUM_KV_HEADS
        scale = 1.0 / hd ** 0.5
        ln1_out = _layernorm(hidden_states, ln1_weight, ln1_bias)
        qkv = jnp.einsum('sbh,oh->sbo', ln1_out, qkv_weight)
        q = qkv[..., :NUM_HEADS * hd].reshape(S, B, NUM_HEADS, hd)
        k = qkv[..., NUM_HEADS * hd:(NUM_HEADS + NUM_KV_HEADS) * hd].reshape(S, B, NUM_KV_HEADS, hd)
        v = qkv[..., (NUM_HEADS + NUM_KV_HEADS) * hd:].reshape(S, B, NUM_KV_HEADS, hd)
        k = jnp.repeat(k, rep, axis=2)
        v = jnp.repeat(v, rep, axis=2)
        scores = jnp.einsum('sbhd,tbhd->bhst', q, k) * scale
        causal = jnp.tril(jnp.ones((S, S), bool))
        scores = jnp.where(causal, scores, jnp.finfo(scores.dtype).min)
        probs = jax.nn.softmax(scores, axis=-1)
        attn = jnp.einsum('bhst,tbhd->sbhd', probs, v).reshape(S, B, H)
        proj_out = jnp.einsum('sbh,oh->sbo', attn, proj_weight)
        hidden_after_attn = hidden_states + proj_out
        ln2_out = _layernorm(hidden_after_attn, ln2_weight, ln2_bias)
        x = ln2_out.reshape(-1, H)
        logits = jnp.einsum('th,eh->te', x, router_weight)
        gate = jax.nn.softmax(logits, axis=-1)
        top_probs, top_idx = jax.lax.top_k(gate, TOP_K)
        h_mid = jax.nn.gelu(jnp.einsum('th,ehf->etf', x, moe_w1))
        expert_out = jnp.einsum('etf,efh->eth', h_mid, moe_w2)
        e_ids = jnp.arange(NUM_EXPERTS)[:, None, None]
        weights = jnp.sum(jnp.where(top_idx[None] == e_ids, top_probs[None], 0.0), axis=-1)
        moe_out = jnp.einsum('eth,et->th', expert_out, weights).reshape(S, B, H)
        return hidden_after_attn + moe_out
    x = _layernorm(x + _L0_attn_ref(x, L0_attn_w_qkv, L0_attn_w_out, L0_attn_b_out), axis=-1)
    x = _layernorm(x + _L0_xattn_ref(x, ctx_1024, ctx_1024, L0_xattn_Wq, L0_xattn_bq, L0_xattn_Wk, L0_xattn_bk, L0_xattn_Wv, L0_xattn_bv), axis=-1)
    x = _layernorm(x + _L0_ffn_ref(x, L0_ffn_ln1_weight, L0_ffn_ln1_bias, L0_ffn_ln2_weight, L0_ffn_ln2_bias, L0_ffn_qkv_weight, L0_ffn_proj_weight, L0_ffn_router_weight, L0_ffn_moe_w1, L0_ffn_moe_w2), axis=-1)
    return x

_drawn_inputs = setup_inputs


def setup_inputs(seed=0):
    import zlib

    import numpy as np

    out = dict(_drawn_inputs(seed))
    spreads = {'L0_ffn_ln1_weight': (1.0, 0.6),
     'L0_ffn_ln1_bias': (0.0, 0.8),
     'L0_ffn_ln2_weight': (1.0, 0.6),
     'L0_ffn_ln2_bias': (0.0, 0.8)}
    factors = {'L0_xattn_bk': 8.0,
     'L0_ffn_router_weight': 6.403,
     'L0_ffn_moe_w1': 5.702,
     'L0_ffn_moe_w2': 5.519}
    for name, (base, spread) in spreads.items():
        noise = np.random.default_rng([zlib.crc32(name.encode()), seed]).standard_normal(out[name].shape)
        drawn = base * np.exp(spread * noise) if base else spread * noise
        out[name] = jnp.asarray(drawn.astype(out[name].dtype))
    for name, factor in factors.items():
        out[name] = (out[name] * factor).astype(out[name].dtype)
    return out
```

```python
from contextlib import ExitStack

import numpy as np

import concourse.bass as bass
from concourse import mybir

F32 = mybir.dt.float32
BF16 = mybir.dt.bfloat16
I32 = mybir.dt.int32
U32 = mybir.dt.uint32
ALU = mybir.AluOpType
ACT = mybir.ActivationFunctionType
AX = mybir.AxisListType.X

P = 128
B, N, D = 16, 256, 256
TOKENS = B * N
C = D // P
T = N // P
HD = 16
CTX = 77
H, KV = 16, 4
REP = H // KV
NI = 8
GROUPS = TOKENS // P // NI
TILES = TOKENS // P
E, F = 8, 512
K4 = F // P
SEGMENT = TOKENS + 2 * P
MOE_TILES = 2 * TOKENS // P + E - 1
EPS = 1e-5
BIG = 3.4028234663852886e38


class Steps:

    def __init__(self, eng, sem):
        self.eng, self.sem, self.base, self.n = eng, sem, 0, 0

    def mark(self, ins):
        ins.then_inc(self.sem, 1)
        self.n += 1
        return self.base + self.n

    def need(self, value):
        self.eng.wait_ge(self.sem, value)

    def need_apart(self, value):
        wait_apart(self.eng, self.sem, value)

    def chain(self, ins):
        self.need(self.mark(ins))

    def repeat(self, count, per):
        entry = self.base + self.n
        with self.eng.Fori(0, count) as j:
            self.base, self.n = j * per + entry, 0
            yield j
            assert self.n == per, f"{self.n} steps a turn"
        self.base, self.n = entry + count * per, 0


def wait(eng, sem, value):
    if not isinstance(value, int) or value > 0:
        eng.wait_ge(sem, value)


def wait_apart(eng, sem, value):
    eng.wait_ge(sem, value)
    eng.nop(nofuse=True)


def bcast(ap, shape):
    return ap.to_broadcast(shape)


class Memory:
    def __init__(self, nc, stack, prefix):
        self.nc, self.stack, self.prefix = nc, stack, prefix

    def sb(self, name, shape, dt=F32):
        return self.stack.enter_context(self.nc.sbuf_tensor(f"{self.prefix}_{name}", shape, dt))

    def ps(self, name, shape):
        return self.stack.enter_context(self.nc.psum_tensor(f"{self.prefix}_{name}", shape, F32))

    def sem(self, name):
        return self.stack.enter_context(self.nc.semaphore(f"{self.prefix}_{name}"))


def layer_norm_stats(steps, nc, rows, stats, mv, to_pool):
    k = rows.shape[1]
    for t in range(k):
        last = steps.mark(nc.vector.bn_stats(stats[:, t, :], rows[:, t, :]))
    steps.need_apart(last)
    for t in range(k):
        ins = nc.vector.bn_aggr(mv[:, t, :], stats[:, t, :])
        if t < k - 1:
            steps.mark(ins)
    ins.then_inc(to_pool, 1)


def linear_attention(nc, mem_all, dram, const):
    with ExitStack() as stack:
        m = Memory(nc, stack, "la")
        w_qkv = m.sb("w_qkv", [P, C, 3 * D])
        w_out = m.sb("w_out", [P, C, D])
        b_out = m.sb("b_out", [P, D])
        x_t = [m.sb(f"x_t{i}", [P, C, N]) for i in range(2)]
        x_tok = [m.sb(f"x_tok{i}", [P, T, D]) for i in range(2)]
        e_q, r_q = m.sb("e_q", [P, C * N]), m.sb("r_q", [P, C * N])
        e_k, r_k = m.sb("e_k", [P, T, D]), m.sb("r_k", [P, T, D])
        q = [m.sb(f"q{i}", [P, C, N]) for i in range(2)]
        k = [m.sb(f"k{i}", [P, T, D]) for i in range(2)]
        v = [m.sb(f"v{i}", [P, T, C, P + 1]) for i in range(2)]
        kv_diag = m.sb("kv_diag", [P, C, P])
        k_sum = m.sb("k_sum", [P, C, P])
        den = m.sb("den", [P, C * N])
        rec = m.sb("rec", [P, C * N])
        att = m.sb("att", [P, C, N])
        s = m.sb("s", [P, T, D])
        stats = m.sb("stats", [P, T, 6])
        mv = m.sb("mv", [P, T, 2])
        var = m.sb("var", [P, T])
        rstd = m.sb("rstd", [P, T])
        x1 = [m.sb(f"x1_{i}", [P, T, D]) for i in range(2)]

        p_q = m.ps("p_q", [P, C, N])
        p_kv = [m.ps(f"p_kv{t}", [P, 2 * D]) for t in range(T)]
        p_sum = m.ps("p_sum", [P, C, N])
        p_num = m.ps("p_num", [P, C, N])
        p_den = m.ps("p_den", [P, C * N])
        p_out = m.ps("p_out", [P, T, D])

        weights_in = m.sem("weights_in")
        x_t_in = [m.sem(f"x_t_in{i}") for i in range(2)]
        x_tok_in = [m.sem(f"x_tok_in{i}") for i in range(2)]
        ones_set = m.sem("ones_set")
        q_mm, kv_mm, sum_mm, num_mm, out_mm = (m.sem(n) for n in ("q_mm", "kv_mm", "sum_mm", "num_mm", "out_mm"))
        q_exp, kv_act, den_act = m.sem("q_exp"), m.sem("kv_act"), m.sem("den_act")
        q_ready, k_ready, diag_ready, att_ready, s_ready = (
            m.sem(n) for n in ("q_ready", "k_ready", "diag_ready", "att_ready", "s_ready"))
        bias_added, var_ready, rstd_ready, x1_ready = (
            m.sem(n) for n in ("bias_added", "var_ready", "rstd_ready", "x1_ready"))
        x1_out = [m.sem(f"x1_out{i}") for i in range(2)]
        dve_step, pool_step = m.sem("dve_step"), m.sem("pool_step")

        def pipeline(front, step, last, repeat):
            front(0, 0, 0)
            step(0, 0, 0)
            step(0, 1, 1)
            for j in repeat(B // 2 - 2):
                step(j + 1, j * 2 + 2, 0)
                step(j + 1, j * 2 + 3, 1)
            step(B // 2 - 1, B - 2, 0)
            last(B // 2 - 1, B - 1, 1)

        def plain_repeat(eng):
            def repeat(count):
                with eng.Fori(0, count) as j:
                    yield j
            return repeat

        with nc.Block() as block:

            @block.sync
            def _(sp):
                sp.dma_start(w_qkv[:, :, :], dram["w_qkv"]).then_inc(weights_in, 16)
                sp.dma_start(w_out[:, :, :], dram["w_out"]).then_inc(weights_in, 16)
                sp.dma_start(b_out[:, :], dram["b_out"].partition_broadcast(P)).then_inc(weights_in, 16)

                def load(j, b, par):
                    wait(sp, kv_mm, (b - 1) * T if not isinstance(b, int) or b >= 2 else 0)
                    sp.dma_start(x_t[par][:, :, :], dram["x_t"][:, :, bass.ds(b * N, N)]).then_inc(x_t_in[par], 16)
                    wait(sp, s_ready, b - 1 if not isinstance(b, int) or b >= 2 else 0)
                    sp.dma_start(x_tok[par][:, :, :], dram["x_rows"][:, bass.ds(b * T, T), :]).then_inc(x_tok_in[par], 16)

                load(0, 0, 0)
                load(0, 1, 1)
                with sp.Fori(0, B // 2 - 1) as j:
                    load(j + 1, j * 2 + 2, 0)
                    load(j + 1, j * 2 + 3, 1)

            @block.gpsimd
            def _(pool):
                for i in range(2):
                    ins = nc.gpsimd.memset(v[i][:, :, :, P:P + 1], 1.0)
                ins.then_inc(ones_set, 1)
                pool.wait_ge(weights_in, 48)

                def batch(j, b, par):
                    pool.wait_ge(x_tok_in[par], j * 16 + 16)
                    nc.gpsimd.tensor_tensor(x_tok[par][:, :, :], x_tok[par][:, :, :],
                                            bcast(b_out[:, :].unsqueeze(1), [P, T, D]), ALU.add).then_inc(bias_added, 1)
                    wait_apart(pool, var_ready, b + 1)
                    nc.gpsimd.tensor_scalar(var[:, :], mv[:, :, 1], EPS, None, ALU.add).then_inc(pool_step, 1)
                    pool.wait_ge(pool_step, b + 1)
                    nc.gpsimd.tensor_tensor(rstd[:, :], var[:, :], const["minus_half"][:, 0:T], ALU.pow).then_inc(rstd_ready, 1)

                with pool.Fori(0, B // 2) as j:
                    batch(j, j * 2, 0)
                    batch(j, j * 2 + 1, 1)

            @block.scalar
            def _(act):
                def q_features(j, b, par):
                    act.wait_ge(q_mm, b + 1)
                    wait(act, q_ready, b)
                    nc.scalar.activation(e_q[:, :], p_q[:, :, :].rearrange("p c n -> p (c n)"), ACT.Exp)
                    nc.scalar.activation(r_q[:, :], p_q[:, :, :].rearrange("p c n -> p (c n)"), ACT.Relu).then_inc(q_exp, 1)

                def kv_features(j, b, par):
                    for t in range(T):
                        act.wait_ge(kv_mm, b * T + t + 1)
                        if t == 0:
                            wait(act, k_ready, b)
                            wait(act, sum_mm, b - 1 if not isinstance(b, int) or b >= 2 else 0)
                        nc.scalar.activation(e_k[:, t, :], p_kv[t][:, 0:D], ACT.Exp)
                        nc.scalar.activation(r_k[:, t, :], p_kv[t][:, 0:D], ACT.Relu)
                        nc.scalar.activation(v[par][:, t, :, 0:P], p_kv[t][:, D:2 * D].rearrange("p (c e) -> p c e", c=C),
                                             ACT.Copy).then_inc(kv_act, 1)

                def denominator(j, b, par):
                    act.wait_ge(num_mm, b + 1)
                    wait(act, att_ready, b)
                    nc.scalar.activation(den[:, :], p_den[:, :], ACT.Copy, bias=1e-6).then_inc(den_act, 1)

                def store(j, b, par):
                    act.wait_ge(x1_ready, b + 1)
                    act.dma_start(dram["x1"][:, bass.ds(b * T, T), :], x1[par][:, :, :]).then_inc(x1_out[par], 16)

                def front(j, b, par):
                    q_features(j, b, par)
                    kv_features(j, b, par)

                def step(j, b, par):
                    q_features(j, b + 1, 1 - par)
                    denominator(j, b, par)
                    kv_features(j, b + 1, 1 - par)
                    store(j, b, par)

                def last(j, b, par):
                    denominator(j, b, par)
                    store(j, b, par)

                pipeline(front, step, last, plain_repeat(act))
                for i in range(2):
                    act.wait_ge(x1_out[i], 16 * B // 2)

            @block.vector
            def _(dve):
                steps = Steps(dve, dve_step)

                def q_combine(j, b, par):
                    dve.wait_ge(q_exp, b + 1)
                    wait(dve, num_mm, b - 1 if not isinstance(b, int) or b >= 2 else 0)
                    nc.vector.scalar_tensor_tensor(q[par][:, :, :].rearrange("p c n -> p (c n)"), e_q[:, :], 1.0, r_q[:, :],
                                                   ALU.min, ALU.add).then_inc(q_ready, 1)

                def k_combine(j, b, par):
                    dve.wait_ge(kv_act, b * T + T)
                    wait(dve, sum_mm, b - 1 if not isinstance(b, int) or b >= 2 else 0)
                    nc.vector.scalar_tensor_tensor(k[par][:, :, :], e_k[:, :, :], 1.0, r_k[:, :, :],
                                                   ALU.min, ALU.add).then_inc(k_ready, 1)

                def diagonal(j, b, par):
                    dve.wait_ge(sum_mm, b + 1)
                    wait(dve, num_mm, b)
                    blocks = bcast(const["head_mask"][:, :].unsqueeze(2), [P, 8, HD])
                    for c in range(C):
                        steps.mark(nc.vector.tensor_tensor(kv_diag[:, c, :].rearrange("p (h d) -> p h d", d=HD),
                                                           p_sum[:, c, 0:P].rearrange("p (h d) -> p h d", d=HD),
                                                           blocks, ALU.mult))
                    for c in range(C):
                        ins = nc.vector.tensor_scalar(k_sum[:, c, :].rearrange("p (h d) -> p h d", d=HD), blocks,
                                                      p_sum[:, c, P:P + 1], None, ALU.mult)
                    ins.then_inc(diag_ready, 1)

                def divide(j, b, par):
                    dve.wait_ge(den_act, b + 1)
                    steps.chain(nc.vector.reciprocal(rec[:, :], den[:, :]))
                    wait(dve, out_mm, b)
                    nc.vector.tensor_tensor(att[:, :, :].rearrange("p c n -> p (c n)"),
                                            p_num[:, :, :].rearrange("p c n -> p (c n)"), rec[:, :],
                                            ALU.mult).then_inc(att_ready, 1)

                def normalise(j, b, par):
                    dve.wait_ge(out_mm, b + 1)
                    dve.wait_ge(bias_added, b + 1)
                    nc.vector.tensor_tensor(s[:, :, :], p_out[:, :, :], x_tok[par][:, :, :], ALU.add).then_inc(s_ready, 1)
                    dve.wait_ge(s_ready, b + 1)
                    layer_norm_stats(steps, nc, s, stats, mv, var_ready)
                    dve.wait_ge(rstd_ready, b + 1)
                    wait(dve, x1_out[par], j * 16)
                    for t in range(T):
                        ins = nc.vector.tensor_scalar(x1[par][:, t, :], s[:, t, :], mv[:, t, 0:1], rstd[:, t:t + 1],
                                                      ALU.subtract, ALU.mult)
                        if t < T - 1:
                            steps.mark(ins)
                    ins.then_inc(x1_ready, 1)
                    dve.wait_ge(x1_ready, b + 1)

                def front(j, b, par):
                    q_combine(j, b, par)
                    k_combine(j, b, par)

                def step(j, b, par):
                    diagonal(j, b, par)
                    q_combine(j, b + 1, 1 - par)
                    divide(j, b, par)
                    k_combine(j, b + 1, 1 - par)
                    normalise(j, b, par)

                def last(j, b, par):
                    diagonal(j, b, par)
                    divide(j, b, par)
                    normalise(j, b, par)

                pipeline(front, step, last, lambda count: steps.repeat(count, 2 * 7))

            @block.tensor
            def _(pe):
                def project_q(j, b, par):
                    pe.wait_ge(x_t_in[par], (b // 2 if isinstance(b, int) else j) * 16 + 16)
                    wait(pe, q_exp, b)
                    for o in range(C):
                        for c in range(C):
                            ins = nc.tensor.matmul(p_q[:, o, :], w_qkv[:, c, o * P:(o + 1) * P], x_t[par][:, c, :],
                                                   start=(c == 0), stop=(c == C - 1))
                    ins.then_inc(q_mm, 1)

                def project_kv(j, b, par):
                    for t in range(T):
                        wait(pe, kv_act, (b - 1) * T + t + 1 if not isinstance(b, int) or b >= 1 else 0)
                        for c in range(C):
                            ins = nc.tensor.matmul(p_kv[t][:, :], x_t[par][:, c, t * P:(t + 1) * P],
                                                   w_qkv[:, c, D:3 * D], start=(c == 0), stop=(c == C - 1))
                        ins.then_inc(kv_mm, 1)

                def sum_kv(j, b, par):
                    pe.wait_ge(k_ready, b + 1)
                    pe.wait_ge(kv_act, b * T + T)
                    wait(pe, diag_ready, b)
                    for c in range(C):
                        for t in range(T):
                            ins = nc.tensor.matmul(p_sum[:, c, 0:P + 1], k[par][:, t, c * P:(c + 1) * P],
                                                   v[par][:, t, c, :], start=(t == 0), stop=(t == T - 1))
                    ins.then_inc(sum_mm, 1)

                def numerators(j, b, par):
                    pe.wait_ge(diag_ready, b + 1)
                    pe.wait_ge(q_ready, b + 1)
                    wait(pe, att_ready, b)
                    wait(pe, den_act, b)
                    for c in range(C):
                        nc.tensor.matmul(p_num[:, c, :], kv_diag[:, c, :], q[par][:, c, :], start=True, stop=True)
                    for c in range(C):
                        ins = nc.tensor.matmul(p_den[:, c * N:(c + 1) * N], k_sum[:, c, :], q[par][:, c, :],
                                               start=True, stop=True)
                    ins.then_inc(num_mm, 1)

                def project_out(j, b, par):
                    pe.wait_ge(att_ready, b + 1)
                    wait(pe, s_ready, b)
                    for t in range(T):
                        for c in range(C):
                            ins = nc.tensor.matmul(p_out[:, t, :], att[:, c, t * P:(t + 1) * P], w_out[:, c, :],
                                                   start=(c == 0), stop=(c == C - 1))
                    ins.then_inc(out_mm, 1)

                def front(j, b, par):
                    project_q(j, b, par)
                    project_kv(j, b, par)

                def step(j, b, par):
                    nxt = j if par == 0 else j + 1
                    sum_kv(j, b, par)
                    project_q(nxt, b + 1, 1 - par)
                    numerators(j, b, par)
                    project_kv(nxt, b + 1, 1 - par)
                    project_out(j, b, par)

                def last(j, b, par):
                    sum_kv(j, b, par)
                    numerators(j, b, par)
                    project_out(j, b, par)

                pe.wait_ge(weights_in, 48)
                pe.wait_ge(ones_set, 1)
                pipeline(front, step, last, plain_repeat(pe))


def cross_attention(nc, mem_all, dram, const):
    KEYS = B * CTX
    CH = KEYS // 4
    with ExitStack() as stack:
        m = Memory(nc, stack, "xa")
        w_q = m.sb("w_q", [P, C, D])
        w_k = m.sb("w_k", [P, C, D])
        w_v = m.sb("w_v", [P, C, D])
        b_q, b_k = m.sb("b_q", [P, C]), m.sb("b_k", [P, C])
        b_v = m.sb("b_v", [P, D])
        b_q_cols = m.sb("b_q_cols", [P, C, P])
        ctx_t = m.sb("ctx_t", [P, C, KEYS])
        k_t = m.sb("k_t", [P, C, KEYS])
        qk = m.sb("qk", [P, C, KEYS])
        k_bias = m.sb("k_bias", [P, KEYS])
        ctx_b = [m.sb(f"ctx_b{i}", [P, C, CTX]) for i in range(2)]
        x1 = [m.sb(f"x1_{i}", [P, T, D]) for i in range(2)]
        x1_t = [m.sb(f"x1_t{i}", [P, C, N]) for i in range(2)]
        v = [m.sb(f"v{i}", [CTX, D]) for i in range(2)]
        sc = m.sb("sc", [P, T, CTX])
        top = m.sb("top", [P, T])
        prob = [m.sb(f"prob{i}", [P, T, CTX]) for i in range(2)]
        total = [m.sb(f"total{i}", [P, T]) for i in range(2)]
        rec = m.sb("rec", [P, T])
        prob_t = m.sb("prob_t", [CTX, T, P])
        s = m.sb("s", [P, T, D])
        stats = m.sb("stats", [P, T, 6])
        mv = m.sb("mv", [P, T, 2])
        var = m.sb("var", [P, T])
        rstd = m.sb("rstd", [P, T])
        x2 = [m.sb(f"x2_{i}", [P, T, D]) for i in range(2)]

        p_t = m.ps("p_t", [P, C, N])
        p_v = m.ps("p_v", [P, 512])
        p_s = m.ps("p_s", [P, T, N])
        p_p = m.ps("p_p", [P, T, N])
        p_o = m.ps("p_o", [P, T, D])
        p_set = [m.ps(f"p_set{i}", [P, 512]) for i in range(2)]

        (weights_in, biases_in, bq_cols, set_mm, set_read, x1_t_mm, v_mm, s_mm, p_t_mm, o_mm, x1_t_ready, exp_done,
         prob_t_ready, v_ready, sc_ready, s_ready, var_ready, rstd_ready, x2_ready, pool_step, dve_step) = (
            m.sem(n) for n in ("weights_in", "biases_in", "bq_cols", "set_mm", "set_read", "x1_t_mm", "v_mm", "s_mm",
                               "p_t_mm", "o_mm", "x1_t_ready", "exp_done", "prob_t_ready", "v_ready", "sc_ready",
                               "s_ready", "var_ready", "rstd_ready", "x2_ready", "pool_step", "dve_step"))
        x1_in = [m.sem(f"x1_in{i}") for i in range(2)]
        ctx_in = [m.sem(f"ctx_in{i}") for i in range(2)]
        x2_out = [m.sem(f"x2_out{i}") for i in range(2)]

        def pipeline(front, step, last, repeat):
            front(0, 0, 0)
            step(0, 0, 0)
            step(0, 1, 1)
            for j in repeat(B // 2 - 2):
                step(j + 1, j * 2 + 2, 0)
                step(j + 1, j * 2 + 3, 1)
            step(B // 2 - 1, B - 2, 0)
            last(B // 2 - 1, B - 1, 1)

        def plain_repeat(eng):
            def repeat(count):
                with eng.Fori(0, count) as j:
                    yield j
            return repeat

        SET_K, SET_QK, SET_ALL = 2 * 4, 4 * 4, 5 * 4

        with nc.Block() as block:

            @block.sync
            def _(sp):
                sp.dma_start(w_k[:, :, :], dram["xw_k"]).then_inc(weights_in, 16)
                sp.dma_start(ctx_t[:, :, :], dram["ctx_t"]).then_inc(weights_in, 16)
                sp.dma_start(w_q[:, :, :], dram["xw_q"]).then_inc(weights_in, 16)
                sp.dma_start(w_v[:, :, :], dram["xw_v"]).then_inc(weights_in, 16)
                sp.dma_start(b_q[:, :], dram["xb_q"]).then_inc(biases_in, 16)
                sp.dma_start(b_k[:, :], dram["xb_k"]).then_inc(biases_in, 16)
                sp.dma_start(b_v[:, :], dram["xb_v"].partition_broadcast(P)).then_inc(biases_in, 16)

                def load(j, b, par):
                    early = isinstance(b, int) and b < 2
                    wait(sp, s_ready, 0 if early else b - 1)
                    sp.dma_start(x1[par][:, :, :], dram["x1"][:, bass.ds(b * T, T), :]).then_inc(x1_in[par], 16)
                    wait(sp, v_mm, 0 if early else b - 1)
                    sp.dma_start(ctx_b[par][:, :, :], dram["ctx_t"][:, :, bass.ds(b * CTX, CTX)]).then_inc(ctx_in[par], 16)

                load(0, 0, 0)
                load(0, 1, 1)
                with sp.Fori(0, B // 2 - 1) as j:
                    load(j + 1, j * 2 + 2, 0)
                    load(j + 1, j * 2 + 3, 1)

            @block.gpsimd
            def _(pool):
                with pool.Fori(0, B) as b:
                    wait_apart(pool, var_ready, b + 1)
                    nc.gpsimd.tensor_scalar(var[:, :], mv[:, :, 1], EPS, None, ALU.add).then_inc(pool_step, 1)
                    pool.wait_ge(pool_step, b + 1)
                    nc.gpsimd.tensor_tensor(rstd[:, :], var[:, :], const["minus_half"][:, 0:T], ALU.pow).then_inc(rstd_ready, 1)

            @block.scalar
            def _(act):
                act.wait_ge(biases_in, 48)
                for n in range(0, SET_ALL, 2):
                    act.wait_ge(set_mm, n + 1)
                    o, ch = (n % SET_K) // 4, n % 4
                    cols = slice(ch * CH, (ch + 1) * CH)
                    if n < SET_K:
                        ins = nc.scalar.activation(k_t[:, o, cols], p_set[0][:, 0:CH], ACT.Identity, bias=b_k[:, o:o + 1])
                    elif n < SET_QK:
                        ins = nc.scalar.activation(qk[:, o, cols], p_set[0][:, 0:CH], ACT.Copy)
                    else:
                        ins = nc.scalar.activation(k_bias[:, cols], p_set[0][:, 0:CH], ACT.Copy)
                    ins.then_inc(set_read, 1)

                def x1_t_copy(j, b, par):
                    act.wait_ge(x1_t_mm, b + 1)
                    wait(act, s_mm, b - 1 if not isinstance(b, int) or b >= 2 else 0)
                    nc.scalar.activation(x1_t[par][:, :, :], p_t[:, :, :], ACT.Copy).then_inc(x1_t_ready, 1)

                def exponentials(j, b, par):
                    act.wait_ge(sc_ready, b + 1)
                    wait(act, s_ready, b - 1 if not isinstance(b, int) or b >= 2 else 0)
                    for t in range(T):
                        ins = nc.scalar.activation(prob[par][:, t, :], sc[:, t, :], ACT.Exp, bias=top[:, t:t + 1],
                                                   accum_out=total[par][:, t:t + 1])
                        ins.then_inc(exp_done, 1)

                def prob_t_copy(j, b, par):
                    act.wait_ge(p_t_mm, b + 1)
                    wait(act, o_mm, b)
                    nc.scalar.activation(prob_t[:, :, :], p_p[0:CTX, :, 0:P], ACT.Copy).then_inc(prob_t_ready, 1)

                def store(j, b, par):
                    act.wait_ge(x2_ready, b + 1)
                    act.dma_start(dram["x2"][:, bass.ds(b * T, T), :], x2[par][:, :, :]).then_inc(x2_out[par], 16)

                def front(j, b, par):
                    x1_t_copy(j, b, par)
                    exponentials(j, b, par)

                def step(j, b, par):
                    x1_t_copy(j, b + 1, 1 - par)
                    prob_t_copy(j, b, par)
                    exponentials(j, b + 1, 1 - par)
                    store(j, b, par)

                def last(j, b, par):
                    prob_t_copy(j, b, par)
                    store(j, b, par)

                pipeline(front, step, last, plain_repeat(act))
                for i in range(2):
                    act.wait_ge(x2_out[i], 16 * B // 2)

            @block.vector
            def _(dve):
                steps = Steps(dve, dve_step)
                dve.wait_ge(biases_in, 48)
                nc.vector.tensor_copy(b_q_cols[:, :, :], bcast(b_q[:, :].unsqueeze(2), [P, C, P])).then_inc(bq_cols, 1)
                for n in range(1, SET_ALL, 2):
                    dve.wait_ge(set_mm, n + 1)
                    o, ch = (n % SET_K) // 4, n % 4
                    cols = slice(ch * CH, (ch + 1) * CH)
                    if n < SET_K:
                        ins = nc.vector.tensor_scalar(k_t[:, o, cols], p_set[1][:, 0:CH], b_k[:, o:o + 1], None, ALU.add)
                    elif n < SET_QK:
                        ins = nc.vector.tensor_copy(qk[:, o, cols], p_set[1][:, 0:CH])
                    else:
                        ins = nc.vector.tensor_copy(k_bias[:, cols], p_set[1][:, 0:CH])
                    ins.then_inc(set_read, 1)
                dve.wait_ge(set_read, SET_ALL)

                def values(j, b, par):
                    dve.wait_ge(v_mm, b + 1)
                    wait(dve, o_mm, b - 1 if not isinstance(b, int) or b >= 2 else 0)
                    nc.vector.tensor_tensor(v[par][:, :], p_v[0:CTX, 0:D], b_v[0:CTX, :], ALU.add).then_inc(v_ready, 1)

                def scores(j, b, par):
                    dve.wait_ge(s_mm, b + 1)
                    wait(dve, exp_done, b * T)
                    steps.chain(nc.vector.tensor_tensor(
                        sc[:, :, :], p_s[:, :, 0:CTX],
                        bcast(k_bias[:, bass.ds(b * CTX, CTX)].unsqueeze(1), [P, T, CTX]), ALU.add))
                    steps.chain(nc.vector.tensor_reduce(top[:, :], sc[:, :, :], AX, ALU.max))
                    nc.vector.tensor_scalar(top[:, :], top[:, :], -1.0, None, ALU.mult).then_inc(sc_ready, 1)

                def normalise(j, b, par):
                    dve.wait_ge(exp_done, b * T + T)
                    steps.chain(nc.vector.reciprocal(rec[:, :], total[par][:, :]))
                    dve.wait_ge(o_mm, b + 1)
                    for t in range(T):
                        ins = nc.vector.scalar_tensor_tensor(s[:, t, :], p_o[:, t, :], rec[:, t:t + 1], x1[par][:, t, :],
                                                             ALU.mult, ALU.add)
                        if t < T - 1:
                            steps.mark(ins)
                    ins.then_inc(s_ready, 1)
                    dve.wait_ge(s_ready, b + 1)
                    layer_norm_stats(steps, nc, s, stats, mv, var_ready)
                    dve.wait_ge(rstd_ready, b + 1)
                    wait(dve, x2_out[par], j * 16)
                    for t in range(T):
                        ins = nc.vector.tensor_scalar(x2[par][:, t, :], s[:, t, :], mv[:, t, 0:1], rstd[:, t:t + 1],
                                                      ALU.subtract, ALU.mult)
                        if t < T - 1:
                            steps.mark(ins)
                    ins.then_inc(x2_ready, 1)
                    dve.wait_ge(x2_ready, b + 1)

                def front(j, b, par):
                    values(j, b, par)
                    scores(j, b, par)

                def step(j, b, par):
                    values(j, b + 1, 1 - par)
                    scores(j, b + 1, 1 - par)
                    normalise(j, b, par)

                pipeline(front, step, normalise, lambda count: steps.repeat(count, 2 * 8))

            @block.tensor
            def _(pe):
                pe.wait_ge(weights_in, 64)
                n = 0

                def piece(pairs, waits):
                    nonlocal n
                    if n >= 2:
                        pe.wait_ge(set_read, waits)
                    for i, (lhs, rhs) in enumerate(pairs):
                        ins = nc.tensor.matmul(p_set[n % 2][:, 0:CH], lhs, rhs, start=(i == 0), stop=(i == len(pairs) - 1))
                    ins.then_inc(set_mm, 1)
                    n += 1

                for o in range(C):
                    for ch in range(4):
                        piece([(w_k[:, c, o * P:(o + 1) * P], ctx_t[:, c, ch * CH:(ch + 1) * CH]) for c in range(C)], n)
                pe.wait_ge(set_read, SET_K)
                for o in range(C):
                    for ch in range(4):
                        piece([(w_q[:, c, o * P:(o + 1) * P], k_t[:, c, ch * CH:(ch + 1) * CH]) for c in range(C)], n)
                pe.wait_ge(bq_cols, 1)
                for ch in range(4):
                    piece([(b_q_cols[:, c, :], k_t[:, c, ch * CH:(ch + 1) * CH]) for c in range(C)], n)
                pe.wait_ge(set_read, SET_ALL)

                def turn_x1(j, b, par):
                    pe.wait_ge(x1_in[par], j * 16 + 16)
                    wait(pe, x1_t_ready, b)
                    for t in range(T):
                        for c in range(C):
                            ins = nc.tensor.transpose(p_t[:, c, t * P:(t + 1) * P], x1[par][:, t, c * P:(c + 1) * P],
                                                      const["identity"][:, :])
                    ins.then_inc(x1_t_mm, 1)

                def project_v(j, b, par):
                    pe.wait_ge(ctx_in[par], j * 16 + 16)
                    wait(pe, v_ready, b)
                    for c in range(C):
                        ins = nc.tensor.matmul(p_v[0:CTX, 0:D], ctx_b[par][:, c, :], w_v[:, c, :],
                                               start=(c == 0), stop=(c == C - 1))
                    ins.then_inc(v_mm, 1)

                def scores(j, b, par):
                    pe.wait_ge(x1_t_ready, b + 1)
                    wait(pe, sc_ready, b)
                    for t in range(T):
                        for c in range(C):
                            ins = nc.tensor.matmul(p_s[:, t, 0:CTX], x1_t[par][:, c, t * P:(t + 1) * P],
                                                   qk[:, c, bass.ds(b * CTX, CTX)], start=(c == 0), stop=(c == C - 1))
                    ins.then_inc(s_mm, 1)

                def turn_prob(j, b, par):
                    pe.wait_ge(exp_done, b * T + T)
                    wait(pe, prob_t_ready, b)
                    for t in range(T):
                        ins = nc.tensor.transpose(p_p[0:CTX, t, 0:P], prob[par][:, t, :], const["identity"][:, :])
                    ins.then_inc(p_t_mm, 1)

                def outputs(j, b, par):
                    pe.wait_ge(prob_t_ready, b + 1)
                    pe.wait_ge(v_ready, b + 1)
                    wait(pe, s_ready, b)
                    for t in range(T):
                        ins = nc.tensor.matmul(p_o[:, t, :], prob_t[:, t, :], v[par][:, :], start=True, stop=True)
                    ins.then_inc(o_mm, 1)

                def front(j, b, par):
                    turn_x1(j, b, par)
                    project_v(j, b, par)
                    scores(j, b, par)

                def step(j, b, par):
                    nxt = j if par == 0 else j + 1
                    turn_x1(nxt, b + 1, 1 - par)
                    project_v(nxt, b + 1, 1 - par)
                    turn_prob(j, b, par)
                    scores(nxt, b + 1, 1 - par)
                    outputs(j, b, par)

                def last(j, b, par):
                    turn_prob(j, b, par)
                    outputs(j, b, par)

                pipeline(front, step, last, plain_repeat(pe))


class Ring:

    def __init__(self, m, name, banks, order):
        self.banks = [m.ps(f"{name}{i}", [P, 512]) for i in range(banks)]
        self.full = [m.sem(f"{name}_full{i}") for i in range(banks)]
        self.free = [m.sem(f"{name}_free{i}") for i in range(banks)]
        assert len(order) % banks == 0
        self.at = {what: (i % banks, i // banks) for i, what in enumerate(order)}
        self.per = len(order) // banks

    def open(self, eng):
        for sem in self.free:
            eng.sem_inc(sem, 1)

    def fill(self, pe, g, what):
        bank, turn = self.at[what]
        pe.wait_ge(self.free[bank], g * self.per + turn + 1)
        return self.banks[bank], self.full[bank]

    def read(self, eng, g, what):
        bank, turn = self.at[what]
        eng.wait_ge(self.full[bank], g * self.per + turn + 1)
        return self.banks[bank], self.free[bank]


def batch_axis_attention(nc, mem_all, dram, const, keep):
    PAIRS = NI // 2
    BLK = P // B
    QK = (H + KV) * HD
    with ExitStack() as stack:
        m = Memory(nc, stack, "ba")
        w_qk = m.sb("w_qk", [P, C, QK])
        w_v = m.sb("w_v", [P, C, KV * HD])
        w_proj = m.sb("w_proj", [P, C, D])
        w_router = m.sb("w_router", [P, C, E])
        ln1_w, ln1_b = m.sb("ln1_w", [P, C]), m.sb("ln1_b", [P, C])
        limit = m.sb("limit", [P, B])
        prefix = m.sb("prefix", [P, P], BF16)
        ones = m.sb("ones", [P, P], BF16)
        experts = m.sb("experts", [P, E])
        segments = m.sb("segments", [P, E])
        row_i, row_f, col_f = m.sb("row_i", [P, 1], I32), m.sb("row_f", [P, 1]), m.sb("col_f", [P, B])
        lim_a, lim_b = m.sb("lim_a", [P, B]), m.sb("lim_b", [P, B])
        stats = m.sb("stats", [P, NI, 6])
        mv = m.sb("mv", [P, NI, 2])
        var = m.sb("var", [P, NI])
        rstd = m.sb("rstd", [P, NI])
        xh1 = m.sb("xh1", [P, NI, D])
        xh2 = m.sb("xh2", [P, NI, D])
        xn_t = m.sb("xn_t", [P, C, NI * P])
        qk = m.sb("qk", [P, H + KV, NI, HD])
        v_diag = m.sb("v_diag", [P, BLK * KV, P])
        k_diag = m.sb("k_diag", [P, KV, BLK, P])
        q_t = m.sb("q_t", [P, H, P])
        prob = [m.sb(f"prob{i}", [P, 4 * NI, B]) for i in range(2)]
        top = [m.sb(f"top{i}", [P, 4 * NI]) for i in range(2)]
        total = [m.sb(f"total{i}", [P, 4 * NI]) for i in range(2)]
        rec = [m.sb(f"rec{i}", [P, 4 * NI]) for i in range(2)]
        prob_t = [m.sb(f"prob_t{i}", [P, 4, P]) for i in range(2)]
        o_t = qk[:, 0:H, :, :].rearrange("p h i d -> p (h i d)").rearrange("p (n b) -> p n b", b=BLK)
        att = xh1
        att_t = [m.sb(f"att_t{i}", [P, 2, C, P]) for i in range(2)]
        h_rows = m.sb("h_rows", [P, NI, D])
        xh2_t = [m.sb(f"xh2_t{i}", [P, 2, C, P]) for i in range(2)]
        logits = m.sb("logits", [P, NI, E])
        best = m.sb("best", [P, NI, 8])
        best_at = m.sb("best_at", [P, NI, 8], U32)
        chosen = m.sb("chosen", [P, NI, 2])
        shifted = m.sb("shifted", [P, NI, E + 2])
        gate_sum = m.sb("gate_sum", [P, NI])
        gate_rec = m.sb("gate_rec", [P, NI])
        picked = m.sb("picked", [P, NI + 1, E], BF16)
        place = m.sb("place", [P, NI, E])
        masked = m.sb("masked", [P, NI, E])
        slot_u = m.sb("slot_u", [P, NI, 2], U32)

        turn = Ring(m, "turn", 3, [(n, i) for n in ("x", "q", "p", "o", "a", "h") for i in range(4)])
        prod = Ring(m, "prod", 3, [("qk", i) for i in range(8)] + [("k", 0), ("s", 0), ("s", 1), ("s", 2), ("o", 0),
                                                                    ("s", 3), ("o", 1), ("o", 2), ("o", 3)]
                    + [("a", i) for i in range(4)])
        p_v = m.ps("p_v", [P, BLK * KV, HD])
        p_r = m.ps("p_r", [P, 512])

        names = ("weights_in biases_in pool_const const_ready var_ready rstd_ready xh1_ready xh2_ready xn_t_ready qk_ready "
                 "v_mm v_diag_ready q_t_ready k_diag_ready top_ready shift_done exp_done rec_ready prob_ready prob_t_ready "
                 "o_t_ready att_ready att_t_ready h_ready keep_done xh2_t_ready logits_mm shifted_ready gates_exp "
                 "picked_ready place_mm slots_ready scattered pool_step dve_step").split()
        s = {n: m.sem(n) for n in names}
        x2_in = [m.sem(f"x2_in{i}") for i in range(GROUPS)]
        resid = keep["resid"]

        with nc.Block() as block:

            @block.sync
            def _(sp):
                sp.dma_start(resid[:, 0:NI, :], dram["x2_group"][:, 0:NI, :]).then_inc(x2_in[0], 16)
                for t, name in ((ln1_w, "ln1_w"), (ln1_b, "ln1_b"), (keep["ln2_w"], "ln2_w"), (keep["ln2_b"], "ln2_b")):
                    sp.dma_start(t[:, :], dram[name]).then_inc(s["biases_in"], 16)
                for t, name in ((w_qk, "w_qk"), (w_v, "w_v"), (w_proj, "w_proj"), (w_router, "w_router")):
                    sp.dma_start(t[:, :, :], dram[name]).then_inc(s["weights_in"], 16)
                for g in range(1, GROUPS):
                    sp.dma_start(resid[:, g * NI:(g + 1) * NI, :], dram["x2_group"][:, g * NI:(g + 1) * NI, :])\
                      .then_inc(x2_in[g], 16)
                sp.dma_start(keep["w1"][:, :, :].rearrange("p (e c) f -> p e c f", c=C), dram["moe_w1"])\
                  .then_inc(keep["experts_in"], 16)
                sp.dma_start(keep["w2"][:, :, :].rearrange("p (e k) h -> p e k h", k=K4), dram["moe_w2"])\
                  .then_inc(keep["experts_in"], 16)

            @block.gpsimd
            def _(pool):
                done = s["pool_const"]
                nc.gpsimd.iota(row_i[:, :], [[0, 1]], base=0, channel_multiplier=1).then_inc(done, 1)
                nc.gpsimd.iota(col_f[:, :], [[1, B]], base=0, channel_multiplier=0,
                               allow_small_or_imprecise_dtypes=True).then_inc(done, 1)
                nc.gpsimd.iota(experts[:, :], [[1, E]], base=0, channel_multiplier=0,
                               allow_small_or_imprecise_dtypes=True).then_inc(done, 1)
                nc.gpsimd.iota(segments[:, :], [[SEGMENT, E]], base=0, channel_multiplier=0,
                               allow_small_or_imprecise_dtypes=True).then_inc(done, 1)
                nc.gpsimd.memset(ones[:, :], 1.0).then_inc(done, 1)
                nc.gpsimd.memset(prefix[:, :], 1.0).then_inc(done, 1)
                nc.gpsimd.memset(picked[:, NI, :], 0.0).then_inc(done, 1)
                nc.gpsimd.memset(keep["count"][:, :], 0.0).then_inc(done, 1)
                pool.wait_ge(done, 8)
                nc.gpsimd.affine_select(out=prefix[:, :], in_=prefix[:, :], compare_op=ALU.is_gt, fill=0.0, base=0,
                                        pattern=[[1, P]], channel_multiplier=-1).then_inc(done, 1)
                with pool.Fori(0, GROUPS) as g:
                    def rstd_of(n):
                        wait_apart(pool, s["var_ready"], g * 2 + n + 1)
                        nc.gpsimd.tensor_scalar(var[:, :], mv[:, :, 1], EPS, None, ALU.add).then_inc(s["pool_step"], 1)
                        pool.wait_ge(s["pool_step"], g * 2 + n + 1)
                        nc.gpsimd.tensor_tensor(rstd[:, :], var[:, :], const["minus_half"][:, :], ALU.pow)\
                          .then_inc(s["rstd_ready"], 1)

                    def subtract_top(i):
                        pool.wait_ge(s["top_ready"], g * 4 + i + 1)
                        nc.gpsimd.tensor_tensor(prob[i % 2][:, :, :], prob[i % 2][:, :, :],
                                                bcast(top[i % 2][:, :].unsqueeze(2), [P, 4 * NI, B]), ALU.subtract)\
                          .then_inc(s["shift_done"], 1)

                    def scale(i):
                        pool.wait_ge(s["rec_ready"], g * 4 + i + 1)
                        nc.gpsimd.tensor_tensor(prob[i % 2][:, :, :], prob[i % 2][:, :, :],
                                                bcast(rec[i % 2][:, :].unsqueeze(2), [P, 4 * NI, B]), ALU.mult)\
                          .then_inc(s["prob_ready"], 1)

                    rstd_of(0)
                    subtract_top(0)
                    for i in range(1, 4):
                        subtract_top(i)
                        scale(i - 1)
                    scale(3)
                    for i in range(PAIRS):
                        pool.wait_ge(s["h_ready"], g * PAIRS + i + 1)
                        rows = resid[:, bass.ds(g * NI + 2 * i, 2), :]
                        nc.gpsimd.tensor_tensor(rows, rows, h_rows[:, 2 * i:2 * i + 2, :], ALU.add).then_inc(s["keep_done"], 1)
                    rstd_of(1)
                    wait_apart(pool, s["slots_ready"], g + 1)
                    for u in range(NI):
                        for k in range(2):
                            nc.gpsimd.indirect_dma_start(
                                out=dram["dispatched"], out_offset=bass.IndirectOffsetOnAxis(ap=slot_u[:, u, k:k + 1], axis=0),
                                in_=xh2[:, u, :], in_offset=None).then_inc(s["scattered"], 16)
                pool.wait_ge(s["scattered"], GROUPS * NI * 2 * 16)
                pool.wait_ge(s["keep_done"], GROUPS * PAIRS)

            @block.scalar
            def _(act):
                act.wait_ge(s["biases_in"], 64)
                with act.Fori(0, GROUPS) as g:
                    def turned(what, out, ready, scale=None, bias=None):
                        bank, free = turn.read(act, g, what)
                        src = bank[:, :].rearrange("p (u c n) -> p u c n", u=2, c=C)
                        if scale is None:
                            nc.scalar.activation(out, src, ACT.Copy).then_inc(free, 1)
                            return
                        for c in range(C):
                            ins = nc.scalar.activation(out[:, :, c, :], src[:, :, c, :], ACT.Identity,
                                                       bias=bias[:, c:c + 1], scale=scale[:, c:c + 1])
                        ins.then_inc(free, 1)

                    def qk_copy(u):
                        bank, free = prod.read(act, g, ("qk", u))
                        nc.scalar.activation(qk[:, :, u, :], bank[:, 0:QK].rearrange("p (h d) -> p h d", d=HD), ACT.Copy).then_inc(free, 1)

                    xn_pairs = xn_t[:, :, :].rearrange("p c (u n) -> p u c n", n=P)
                    for i in range(PAIRS):
                        turned(("x", i), xn_pairs[:, 2 * i:2 * i + 2, :, :], None, ln1_w, ln1_b)
                        if i >= 1:
                            qk_copy(2 * i - 2)
                    qk_copy(6)
                    for i in range(4):
                        bank, free = turn.read(act, g, ("q", i))
                        nc.scalar.activation(q_t[:, 4 * i:4 * i + 4, :], bank[:, :].rearrange("p (h n) -> p h n", n=P),
                                             ACT.Copy).then_inc(free, 1)

                    def exponential(i):
                        act.wait_ge(s["shift_done"], g * 4 + i + 1)
                        nc.scalar.activation(prob[i % 2][:, :, :], prob[i % 2][:, :, :], ACT.Exp).then_inc(s["exp_done"], 1)

                    def prob_t_copy(i):
                        bank, free = turn.read(act, g, ("p", i))
                        if i >= 2:
                            act.wait_ge(prod.full[prod.at[("o", i - 2)][0]], g * prod.per + prod.at[("o", i - 2)][1] + 1)
                        nc.scalar.activation(prob_t[i % 2][:, :, :], bank[:, :].rearrange("p (u n) -> p u n", n=P),
                                             ACT.Copy).then_inc(free, 1)

                    def o_t_copy(i):
                        bank, free = prod.read(act, g, ("o", i))
                        nc.scalar.activation(o_t[:, :, 2 * i:2 * i + 2], bank[:, :].rearrange("p (b n) -> p n b", b=2),
                                             ACT.Copy).then_inc(free, 1)

                    exponential(0)
                    exponential(1)
                    prob_t_copy(0)
                    exponential(2)
                    prob_t_copy(1)
                    o_t_copy(0)
                    exponential(3)
                    prob_t_copy(2)
                    o_t_copy(1)
                    prob_t_copy(3)
                    o_t_copy(2)
                    o_t_copy(3)
                    for i in range(4):
                        bank, free = turn.read(act, g, ("o", i))
                        nc.scalar.activation(
                            att[:, :, i * 4 * HD:(i + 1) * 4 * HD].rearrange("p i (h d) -> p h i d", d=HD),
                            bank[:, :].rearrange("p (h i d) -> p h i d", h=4, d=HD), ACT.Copy).then_inc(free, 1)
                    for i in range(PAIRS):
                        if i >= 2:
                            act.wait_ge(prod.full[prod.at[("a", i - 2)][0]], g * prod.per + prod.at[("a", i - 2)][1] + 1)
                        turned(("a", i), att_t[i % 2][:, :, :, :], None)
                    for i in range(PAIRS):
                        if i >= 2:
                            act.wait_ge(s["logits_mm"], g * PAIRS + i - 1)
                        turned(("h", i), xh2_t[i % 2][:, :, :, :], None, keep["ln2_w"], keep["ln2_b"])
                    act.wait_ge(s["shifted_ready"], g + 1)
                    nc.scalar.activation(shifted[:, :, :], shifted[:, :, :], ACT.Exp).then_inc(s["gates_exp"], 1)

            @block.vector
            def _(dve):
                steps = Steps(dve, s["dve_step"])
                turn.open(dve)
                prod.open(dve)
                dve.wait_ge(s["pool_const"], 9)
                steps.chain(nc.vector.tensor_scalar(row_i[:, :], row_i[:, :], B - 1, None, ALU.bitwise_and))
                steps.chain(nc.vector.tensor_copy(row_f[:, :], row_i[:, :]))
                steps.chain(nc.vector.tensor_scalar(limit[:, :], col_f[:, :], row_f[:, 0:1], None, ALU.is_le))
                steps.mark(nc.vector.tensor_scalar(lim_a[:, :], limit[:, :], BIG, None, ALU.mult))
                steps.chain(nc.vector.tensor_scalar(lim_b[:, :], limit[:, :], -1.0, BIG, ALU.add, ALU.mult))
                steps.chain(nc.vector.tensor_tensor(limit[:, :], lim_a[:, :], lim_b[:, :], ALU.add))
                dve.wait_ge(s["biases_in"], 64)
                for i in range(GROUPS):
                    dve.wait_ge(x2_in[i], 16)

                for g in steps.repeat(GROUPS, 72):
                    def statistics(rows):
                        for u in range(NI):
                            last = steps.mark(nc.vector.bn_stats(stats[:, u, :], rows(u)))
                        steps.need_apart(last)
                        for u in range(NI):
                            ins = nc.vector.bn_aggr(mv[:, u, :], stats[:, u, :])
                            if u < NI - 1:
                                steps.mark(ins)
                        ins.then_inc(s["var_ready"], 1)

                    statistics(lambda u: resid[:, bass.ds(g * NI + u, 1), :])
                    dve.wait_ge(s["rstd_ready"], g * 2 + 1)
                    for u in range(NI):
                        nc.vector.tensor_scalar(xh1[:, u, :], resid[:, bass.ds(g * NI + u, 1), :], mv[:, u, 0:1],
                                                rstd[:, u:u + 1], ALU.subtract, ALU.mult).then_inc(s["xh1_ready"], 1)
                    for u in range(1, NI, 2):
                        bank, free = prod.read(dve, g, ("qk", u))
                        nc.vector.tensor_copy(qk[:, :, u, :], bank[:, 0:QK].rearrange("p (h d) -> p h d", d=HD)).then_inc(free, 1)
                    dve.wait_ge(s["v_mm"], g + 1)
                    nc.vector.tensor_tensor(
                        v_diag[:, :, :].rearrange("p b (i d) -> p b i d", d=HD),
                        bcast(p_v[:, :, :].unsqueeze(2), [P, BLK * KV, NI, HD]),
                        bcast(const["head_mask"][:, :].unsqueeze(1).unsqueeze(3), [P, BLK * KV, NI, HD]), ALU.mult)\
                        .then_inc(s["v_diag_ready"], 1)
                    bank, free = prod.read(dve, g, ("k", 0))
                    for kv in range(KV):
                        src = bank[:, kv * P:(kv + 1) * P].rearrange("p (t b) -> p b t", b=BLK).unsqueeze(2)
                        ins = nc.vector.tensor_tensor(
                            k_diag[:, kv, :, :].rearrange("p b (i t) -> p b i t", t=B),
                            bcast(src, [P, BLK, NI, B]),
                            bcast(const["head_mask"][:, :].unsqueeze(1).unsqueeze(3), [P, BLK, NI, B]), ALU.mult)
                        if kv < KV - 1:
                            steps.mark(ins)
                    ins.then_inc(free, 1)

                    def score_top(i):
                        bank, free = prod.read(dve, g, ("s", i))
                        if i >= 2:
                            b2, t2 = turn.at[("p", i - 2)]
                            dve.wait_ge(turn.full[b2], g * turn.per + t2 + 1)
                        nc.vector.scalar_tensor_tensor(prob[i % 2][:, :, :], bank[:, :].rearrange("p (n t) -> p n t", t=B),
                                                       HD ** -0.5, bcast(limit[:, :].unsqueeze(1), [P, 4 * NI, B]),
                                                       ALU.mult, ALU.min).then_inc(free, 1)
                        b1, t1 = prod.at[("s", i)]
                        dve.wait_ge(prod.free[b1], g * prod.per + t1 + 2)
                        nc.vector.tensor_reduce(top[i % 2][:, :], prob[i % 2][:, :, :], AX, ALU.max).then_inc(s["top_ready"], 1)

                    def reciprocal_sum(i):
                        dve.wait_ge(s["exp_done"], g * 4 + i + 1)
                        steps.chain(nc.vector.tensor_reduce(total[i % 2][:, :], prob[i % 2][:, :, :], AX, ALU.add))
                        nc.vector.reciprocal(rec[i % 2][:, :], total[i % 2][:, :]).then_inc(s["rec_ready"], 1)

                    score_top(0)
                    score_top(1)
                    reciprocal_sum(0)
                    score_top(2)
                    reciprocal_sum(1)
                    score_top(3)
                    reciprocal_sum(2)
                    reciprocal_sum(3)

                    for i in range(PAIRS):
                        bank, free = prod.read(dve, g, ("a", i))
                        steps.mark(nc.vector.tensor_tensor(
                            h_rows[:, 2 * i:2 * i + 2, :], bank[:, :].rearrange("p (u d) -> p u d", u=2),
                            resid[:, bass.ds(g * NI + 2 * i, 2), :], ALU.add))
                        steps.need(steps.base + steps.n)
                        dve.sem_inc(free, 1)
                        dve.sem_inc(s["h_ready"], 1)
                    statistics(lambda u: h_rows[:, u, :])
                    dve.wait_ge(s["rstd_ready"], g * 2 + 2)
                    for u in range(NI):
                        nc.vector.tensor_scalar(xh2[:, u, :], h_rows[:, u, :], mv[:, u, 0:1],
                                                rstd[:, u:u + 1], ALU.subtract, ALU.mult).then_inc(s["xh2_ready"], 1)
                    dve.wait_ge(s["logits_mm"], g * PAIRS + PAIRS)
                    steps.need_apart(steps.mark(nc.vector.tensor_copy(logits[:, :, :],
                                                                      p_r[:, 0:NI * E].rearrange("p (u e) -> p u e", e=E))))
                    for u in range(NI):
                        last = steps.mark(nc.vector.max(best[:, u, :], logits[:, u, :]))
                    steps.need_apart(last)
                    for u in range(NI):
                        steps.mark(nc.vector.max_index(best_at[:, u, :], best[:, u, :], logits[:, u, :]))
                    leader = best[:, :, 0:1]
                    steps.mark(nc.vector.tensor_tensor(shifted[:, :, 0:E], logits[:, :, :], bcast(leader, [P, NI, E]),
                                                       ALU.subtract))
                    nc.vector.tensor_tensor(shifted[:, :, E:E + 2], best[:, :, 0:2], bcast(leader, [P, NI, 2]),
                                            ALU.subtract).then_inc(s["shifted_ready"], 1)
                    steps.need(steps.base + steps.n)
                    steps.chain(nc.vector.tensor_copy(chosen[:, :, :], best_at[:, :, 0:2]))
                    hot = []
                    for k in range(2):
                        one = keep["hot"][:, k, bass.ds(g * NI, NI), :]
                        hot.append(one)
                        steps.mark(nc.vector.tensor_tensor(one, bcast(chosen[:, :, k:k + 1], [P, NI, E]),
                                                           bcast(experts[:, :].unsqueeze(1), [P, NI, E]), ALU.is_equal))
                    steps.need(steps.base + steps.n)
                    nc.vector.tensor_tensor(picked[:, 0:NI, :], hot[0], hot[1], ALU.add).then_inc(s["picked_ready"], 1)
                    dve.wait_ge(s["gates_exp"], g + 1)
                    steps.chain(nc.vector.tensor_reduce(gate_sum[:, :], shifted[:, :, 0:E], AX, ALU.add))
                    steps.chain(nc.vector.reciprocal(gate_rec[:, :], gate_sum[:, :]))
                    steps.mark(nc.vector.tensor_tensor(keep["gate"][:, bass.ds(g * NI, NI), :], shifted[:, :, E:E + 2],
                                                       bcast(gate_rec[:, :].unsqueeze(2), [P, NI, 2]), ALU.mult))
                    dve.wait_ge(s["place_mm"], g + 1)
                    places = p_r[:, NI * E:(2 * NI + 1) * E].rearrange("p (u e) -> p u e", e=E)
                    steps.chain(nc.vector.tensor_tensor(place[:, :, :], places[:, 0:NI, :],
                                                        bcast(keep["count"][:, :].unsqueeze(1), [P, NI, E]), ALU.add))
                    steps.mark(nc.vector.tensor_tensor(keep["count"][:, :], places[:, NI, :], keep["count"][:, :], ALU.add))
                    steps.chain(nc.vector.tensor_tensor(place[:, :, :], place[:, :, :],
                                                        bcast(segments[:, :].unsqueeze(1), [P, NI, E]), ALU.add))
                    for k in range(2):
                        steps.chain(nc.vector.tensor_tensor(masked[:, :, :], place[:, :, :], hot[k], ALU.mult))
                        summed = steps.mark(nc.vector.tensor_reduce(keep["slot"][:, bass.ds(g * NI, NI), k:k + 1], masked[:, :, :],
                                                            AX, ALU.add))
                        steps.need_apart(summed)
                    nc.vector.tensor_copy(slot_u[:, :, :], keep["slot"][:, bass.ds(g * NI, NI), :]).then_inc(s["slots_ready"], 1)
                    dve.wait_ge(s["scattered"], g * (NI * 2 * 16) + NI * 2 * 16)
                    dve.wait_ge(s["keep_done"], g * PAIRS + PAIRS)

            @block.tensor
            def _(pe):
                ident = const["identity"]
                pe.wait_ge(s["weights_in"], 64)
                pe.wait_ge(s["pool_const"], 9)
                with pe.Fori(0, GROUPS) as g:
                    def turn_pair(what, ready, per_pair, rows, i):
                        pe.wait_ge(ready, g * NI + 2 * i + 2)
                        bank, full = turn.fill(pe, g, (what, i))
                        for u in range(2):
                            for c in range(C):
                                ins = nc.tensor.transpose(bank[:, (u * C + c) * P:(u * C + c + 1) * P],
                                                          rows[:, 2 * i + u, c * P:(c + 1) * P], ident[:, :])
                        ins.then_inc(full, 1)

                    def turn_read(what, i):
                        b, t = turn.at[(what, i)]
                        pe.wait_ge(turn.free[b], g * turn.per + t + 2)

                    def prod_read(what, i):
                        b, t = prod.at[(what, i)]
                        pe.wait_ge(prod.free[b], g * prod.per + t + 2)

                    def project_qk(i):
                        turn_read("x", i)
                        for u in (2 * i, 2 * i + 1):
                            bank, full = prod.fill(pe, g, ("qk", u))
                            for c in range(C):
                                ins = nc.tensor.matmul(bank[:, 0:QK], xn_t[:, c, u * P:(u + 1) * P], w_qk[:, c, :],
                                                       start=(c == 0), stop=(c == C - 1))
                            ins.then_inc(full, 1)

                    turn_pair("x", s["xh1_ready"], 2, xh1, 0)
                    for i in range(1, PAIRS):
                        turn_pair("x", s["xh1_ready"], 2, xh1, i)
                        project_qk(i - 1)
                    project_qk(PAIRS - 1)
                    for b in range(BLK):
                        for c in range(C):
                            tokens = xn_t[:, c, :].rearrange("p (n b) -> p n b", b=BLK)[:, :, b]
                            ins = nc.tensor.matmul(p_v[:, b * KV:(b + 1) * KV, :].rearrange("p k d -> p (k d)"), tokens,
                                                   w_v[:, c, :], start=(c == 0), stop=(c == C - 1))
                    ins.then_inc(s["v_mm"], 1)
                    for u in range(NI):
                        prod_read("qk", u)
                    for i in range(4):
                        bank, full = turn.fill(pe, g, ("q", i))
                        for h in range(4):
                            ins = nc.tensor.transpose(bank[:, h * P:(h + 1) * P],
                                                      qk[:, 4 * i + h, :, :].rearrange("p i d -> p (i d)"), ident[:, :])
                        ins.then_inc(full, 1)
                    bank, full = prod.fill(pe, g, ("k", 0))
                    for kv in range(KV):
                        ins = nc.tensor.transpose(bank[:, kv * P:(kv + 1) * P],
                                                  qk[:, H + kv, :, :].rearrange("p i d -> p (i d)"), ident[:, :])
                    ins.then_inc(full, 1)

                    def scores(i):
                        bank, full = prod.fill(pe, g, ("s", i))
                        for b2 in range(2):
                            for kv in range(KV):
                                b = 2 * i + b2
                                tile = 2 * b2 + kv // 2
                                rows = slice(64 * (kv % 2), 64 * (kv % 2) + 64)
                                queries = q_t[:, kv * REP:(kv + 1) * REP, :].rearrange("p h n -> p (h n)")\
                                    .rearrange("p (n b) -> p n b", b=BLK)[:, :, b]
                                ins = nc.tensor.matmul(bank[rows, tile * P:(tile + 1) * P], queries, k_diag[:, kv, b, :],
                                                       start=True, stop=True)
                        ins.then_inc(full, 1)

                    def turn_prob(i):
                        pe.wait_ge(s["prob_ready"], g * 4 + i + 1)
                        bank, full = turn.fill(pe, g, ("p", i))
                        for t in range(4):
                            ins = nc.tensor.transpose(bank[:, t * P:(t + 1) * P],
                                                      prob[i % 2][:, t * NI:(t + 1) * NI, :].rearrange("p n t -> p (n t)"),
                                                      ident[:, :])
                        ins.then_inc(full, 1)

                    def outputs(i):
                        turn_read("p", i)
                        bank, full = prod.fill(pe, g, ("o", i))
                        for b2 in range(2):
                            for kv in range(KV):
                                tile = 2 * b2 + kv // 2
                                ins = nc.tensor.matmul(bank[:, (b2 * KV + kv) * 64:(b2 * KV + kv + 1) * 64],
                                                       v_diag[:, (2 * i + b2) * KV + kv, :],
                                                       prob_t[i % 2][:, tile, 64 * (kv % 2):64 * (kv % 2) + 64],
                                                       start=True, stop=True)
                        ins.then_inc(full, 1)

                    for i in range(4):
                        turn_read("q", i)
                    prod_read("k", 0)
                    pe.wait_ge(s["v_diag_ready"], g + 1)
                    scores(0)
                    scores(1)
                    turn_prob(0)
                    scores(2)
                    outputs(0)
                    turn_prob(1)
                    scores(3)
                    outputs(1)
                    turn_prob(2)
                    outputs(2)
                    turn_prob(3)
                    outputs(3)
                    for i in range(4):
                        prod_read("o", i)
                    for i in range(4):
                        bank, full = turn.fill(pe, g, ("o", i))
                        for h in range(4):
                            head = o_t[:, (4 * i + h) * B:(4 * i + h + 1) * B, :].rearrange("p s b -> p (s b)")
                            ins = nc.tensor.transpose(bank[:, h * P:(h + 1) * P], head, ident[:, :])
                        ins.then_inc(full, 1)
                    for i in range(4):
                        turn_read("o", i)

                    def turn_att(i):
                        bank, full = turn.fill(pe, g, ("a", i))
                        for u in range(2):
                            for c in range(C):
                                ins = nc.tensor.transpose(bank[:, (u * C + c) * P:(u * C + c + 1) * P],
                                                          att[:, 2 * i + u, c * P:(c + 1) * P], ident[:, :])
                        ins.then_inc(full, 1)

                    def project(i):
                        turn_read("a", i)
                        bank, full = prod.fill(pe, g, ("a", i))
                        for u in range(2):
                            for c in range(C):
                                ins = nc.tensor.matmul(bank[:, u * D:(u + 1) * D], att_t[i % 2][:, u, c, :], w_proj[:, c, :],
                                                       start=(c == 0), stop=(c == C - 1))
                        ins.then_inc(full, 1)

                    turn_att(0)
                    for i in range(1, PAIRS):
                        turn_att(i)
                        project(i - 1)
                    project(PAIRS - 1)

                    def route(i):
                        turn_read("h", i)
                        for u in range(2):
                            for c in range(C):
                                ins = nc.tensor.matmul(p_r[:, (2 * i + u) * E:(2 * i + u + 1) * E], xh2_t[i % 2][:, u, c, :],
                                                       w_router[:, c, :], start=(c == 0), stop=(c == C - 1))
                        ins.then_inc(s["logits_mm"], 1)

                    turn_pair("h", s["xh2_ready"], 2, xh2, 0)
                    for i in range(1, PAIRS):
                        turn_pair("h", s["xh2_ready"], 2, xh2, i)
                        route(i - 1)
                    route(PAIRS - 1)
                    pe.wait_ge(s["picked_ready"], g + 1)
                    places = p_r[:, NI * E:(2 * NI + 1) * E]
                    nc.tensor.matmul(places, prefix[:, :], picked[:, :, :].rearrange("p u e -> p (u e)"), start=True, stop=False)
                    for u in range(NI):
                        ins = nc.tensor.matmul(places[:, (u + 1) * E:(NI + 1) * E], ones[:, :],
                                               bcast(picked[:, u:u + 1, :], [P, NI - u, E]), start=False, stop=(u == NI - 1))
                    ins.then_inc(s["place_mm"], 1)
                    pe.wait_ge(s["slots_ready"], g + 1)


def experts_and_end(nc, mem_all, dram, const, keep):
    HALF = TILES // 2
    with ExitStack() as stack:
        m = Memory(nc, stack, "ex")
        count_i = m.sb("count_i", [P, E], I32)
        tiles_i = m.sb("tiles_i", [P, E], I32)
        n_tiles = m.sb("n_tiles", [P, E])
        up_to = m.sb("up_to", [P, E])
        before = m.sb("before", [P, E])
        one_e = m.sb("one_e", [P, E])
        experts = m.sb("experts", [P, E])
        segments = m.sb("segments", [P, E])
        offset = m.sb("offset", [P, E])
        tail_row = m.sb("tail_row", [P, E])
        tail_i = m.sb("tail_i", [P, E], I32)
        tile_no = m.sb("tile_no", [P, MOE_TILES])
        wide = m.sb("wide", [P, MOE_TILES, E])
        hot_t = m.sb("hot_t", [P, MOE_TILES, E])
        expert_f = m.sb("expert_f", [P, MOE_TILES])
        skip_f = m.sb("skip_f", [P, MOE_TILES])
        own_f = m.sb("own_f", [P, MOE_TILES])
        row_f = m.sb("row_f", [P, MOE_TILES])
        expert_i = m.sb("expert_i", [P, MOE_TILES], I32)
        first_i = m.sb("first_i", [P, MOE_TILES], I32)
        moved = m.sb("moved", [P, TILES, E])
        result_f = m.sb("result_f", [P, TILES, 2])
        result_u = m.sb("result_u", [P, TILES, 2], U32)
        zeros = m.sb("zeros", [P, 2, D])
        xm = [m.sb(f"xm{i}", [P, D]) for i in range(2)]
        xm_t = [m.sb(f"xm_t{i}", [P, C, P]) for i in range(2)]
        hid = [m.sb(f"hid{i}", [P, F]) for i in range(2)]
        hid_t = [m.sb(f"hid_t{i}", [P, K4, P]) for i in range(2)]
        ym = [m.sb(f"ym{i}", [P, D]) for i in range(2)]

        p_x = m.ps("p_x", [P, C, P])
        p_h = [m.ps(f"p_h{i}", [P, F]) for i in range(2)]
        p_t = [m.ps(f"p_t{i}", [P, K4, P]) for i in range(2)]
        p_y = [m.ps(f"p_y{i}", [P, 512]) for i in range(2)]

        names = ("pool_const table_ready tails_zero x_mm x_ready h_mm hid_ready t_mm t_ready y_mm y_ready dve_step").split()
        s = {n: m.sem(n) for n in names}
        xm_in = [m.sem(f"xm_in{i}") for i in range(2)]
        ym_out = [m.sem(f"ym_out{i}") for i in range(2)]
        w1, w2 = keep["w1"], keep["w2"]
        LAST = MOE_TILES - 1
        assert MOE_TILES % 2 == 1

        with nc.Block() as block:

            @block.sync
            def _(sp):
                sp.wait_ge(s["table_ready"], 1)
                with sp.Fori(0, E) as e:
                    row = sp.value_load(tail_i[0:1, bass.ds(e, 1)], min_val=0, max_val=E * SEGMENT - 2 * P)
                    sp.dma_start(dram["dispatched"][bass.ds(row, 2 * P), :].rearrange("(t p) d -> p t d", p=P),
                                 zeros[:, :, :]).then_inc(s["tails_zero"], 16)
                sp.wait_ge(s["tails_zero"], 16 * E)

                def load(j, t, par):
                    wait(sp, s["x_mm"], t - 1 if not isinstance(t, int) or t >= 2 else 0)
                    sp.nop(nofuse=True)
                    row = sp.value_load(first_i[0:1, bass.ds(t, 1)], min_val=0, max_val=E * SEGMENT - P)
                    sp.dma_start(xm[par][:, :], dram["dispatched"][bass.ds(row, P), :]).then_inc(xm_in[par], 16)

                load(0, 0, 0)
                load(0, 1, 1)
                with sp.Fori(0, (MOE_TILES - 3) // 2) as j:
                    load(j + 1, j * 2 + 2, 0)
                    load(j + 1, j * 2 + 3, 1)
                load(LAST // 2, LAST, 0)

            @block.gpsimd
            def _(pool):
                done = s["pool_const"]
                nc.gpsimd.memset(zeros[:, :, :], 0.0).then_inc(done, 1)
                nc.gpsimd.memset(one_e[:, :], 1.0).then_inc(done, 1)
                nc.gpsimd.iota(experts[:, :], [[1, E]], base=0, channel_multiplier=0,
                               allow_small_or_imprecise_dtypes=True).then_inc(done, 1)
                nc.gpsimd.iota(segments[:, :], [[SEGMENT, E]], base=0, channel_multiplier=0,
                               allow_small_or_imprecise_dtypes=True).then_inc(done, 1)
                nc.gpsimd.iota(tile_no[:, :], [[1, MOE_TILES]], base=0, channel_multiplier=0,
                               allow_small_or_imprecise_dtypes=True).then_inc(done, 1)

            def moe_pipeline(first, step, end, repeat):
                first(0, 0, 0)
                step(0, 1, 1)
                step(1, 2, 0)
                for j in repeat((MOE_TILES - 5) // 2):
                    step(j + 1, j * 2 + 3, 1)
                    step(j + 2, j * 2 + 4, 0)
                step(LAST // 2 - 1, LAST - 1, 1)
                end(LAST // 2, LAST, 0)

            def plain_repeat(eng):
                def repeat(count):
                    with eng.Fori(0, count) as j:
                        yield j
                return repeat

            @block.scalar
            def _(act):
                def x_copy(t, par):
                    act.wait_ge(s["x_mm"], t + 1)
                    wait(act, s["h_mm"], t - 1 if not isinstance(t, int) or t >= 2 else 0)
                    for c in range(C):
                        ins = nc.scalar.activation(xm_t[par][:, c, :], p_x[:, c, :], ACT.Identity,
                                                   bias=keep["ln2_b"][:, c:c + 1], scale=keep["ln2_w"][:, c:c + 1])
                    ins.then_inc(s["x_ready"], 1)

                def gelu(t, par):
                    act.wait_ge(s["h_mm"], t + 1)
                    wait(act, s["t_mm"], t - 1 if not isinstance(t, int) or t >= 2 else 0)
                    nc.scalar.activation(hid[par][:, :], p_h[par][:, :], ACT.Gelu_apprx_tanh).then_inc(s["hid_ready"], 1)

                def store(t, par):
                    act.wait_ge(s["y_ready"], t + 1)
                    act.dma_start(dram["results"][bass.ds(t * P, P), :], ym[par][:, :]).then_inc(ym_out[par], 16)

                def first(turn, t, par):
                    x_copy(0, 0)
                    gelu(t, par)
                    x_copy(t + 1, 1 - par)

                def step(turn, t, par):
                    gelu(t, par)
                    x_copy(t + 1, 1 - par)
                    store(t - 1, 1 - par)

                def end(turn, t, par):
                    gelu(t, par)
                    store(t - 1, 1 - par)
                    store(t, par)

                moe_pipeline(first, step, end, plain_repeat(act))
                act.wait_ge(ym_out[0], 16 * (MOE_TILES // 2 + 1))
                act.wait_ge(ym_out[1], 16 * (MOE_TILES // 2))

            @block.vector
            def _(dve):
                steps = Steps(dve, s["dve_step"])
                V = nc.vector
                dve.wait_ge(s["pool_const"], 5)
                steps.chain(V.tensor_scalar(count_i[:, :], keep["count"][:, :], float(P - 1), None, ALU.add))
                steps.chain(V.tensor_scalar(tiles_i[:, :], count_i[:, :], 7, None, ALU.logical_shift_right))
                steps.chain(V.tensor_copy(n_tiles[:, :], tiles_i[:, :]))
                steps.chain(V.tensor_tensor_scan(up_to[:, :], one_e[:, :], n_tiles[:, :], 0.0, ALU.mult, ALU.add))
                steps.chain(V.tensor_tensor(before[:, :], up_to[:, :], n_tiles[:, :], ALU.subtract))
                steps.chain(V.tensor_tensor(tail_row[:, :], keep["count"][:, :], segments[:, :], ALU.add))
                steps.chain(V.tensor_copy(tail_i[:, :], tail_row[:, :]))
                wide_shape = [P, MOE_TILES, E]
                steps.chain(V.tensor_tensor(wide[:, :, :], bcast(tile_no[:, :].unsqueeze(2), wide_shape),
                                            bcast(up_to[:, :].unsqueeze(1), wide_shape), ALU.is_ge))
                steps.chain(V.tensor_reduce(expert_f[:, :], wide[:, :, :], AX, ALU.add))
                steps.chain(V.tensor_scalar(expert_f[:, :], expert_f[:, :], float(E - 1), None, ALU.min))
                steps.chain(V.tensor_tensor(hot_t[:, :, :], bcast(expert_f[:, :].unsqueeze(2), wide_shape),
                                            bcast(experts[:, :].unsqueeze(1), wide_shape), ALU.is_equal))
                for table, out in ((before, skip_f), (n_tiles, own_f)):
                    steps.chain(V.tensor_tensor(wide[:, :, :], hot_t[:, :, :], bcast(table[:, :].unsqueeze(1), wide_shape),
                                                ALU.mult))
                    steps.chain(V.tensor_reduce(out[:, :], wide[:, :, :], AX, ALU.add))
                steps.chain(V.tensor_tensor(skip_f[:, :], tile_no[:, :], skip_f[:, :], ALU.subtract))
                steps.chain(V.tensor_tensor(skip_f[:, :], skip_f[:, :], own_f[:, :], ALU.min))
                steps.chain(V.tensor_scalar(skip_f[:, :], skip_f[:, :], float(P), None, ALU.mult))
                steps.chain(V.scalar_tensor_tensor(row_f[:, :], expert_f[:, :], float(SEGMENT), skip_f[:, :],
                                                   ALU.mult, ALU.add))
                steps.chain(V.tensor_copy(expert_i[:, :], expert_f[:, :]))
                V.tensor_copy(first_i[:, :], row_f[:, :]).then_inc(s["table_ready"], 1)
                steps.chain(V.scalar_tensor_tensor(offset[:, :], before[:, :], float(P), segments[:, :],
                                                   ALU.mult, ALU.subtract))
                for k in range(2):
                    steps.chain(V.tensor_tensor(moved[:, :, :], keep["hot"][:, k, :, :],
                                                bcast(offset[:, :].unsqueeze(1), [P, TILES, E]), ALU.mult))
                    steps.chain(V.tensor_reduce(result_f[:, :, k:k + 1], moved[:, :, :], AX, ALU.add))
                steps.chain(V.tensor_tensor(result_f[:, :, :], result_f[:, :, :], keep["slot"][:, :, :], ALU.add))
                steps.chain(V.tensor_copy(keep["result"][:, :, :], result_f[:, :, :]))

                def hid_t_copy(t, par):
                    dve.wait_ge(s["t_mm"], t + 1)
                    wait(dve, s["y_mm"], t - 1 if not isinstance(t, int) or t >= 2 else 0)
                    V.tensor_copy(hid_t[par][:, :, :], p_t[par][:, :, :]).then_inc(s["t_ready"], 1)

                def y_copy(turn, t, par):
                    dve.wait_ge(s["y_mm"], t + 1)
                    wait(dve, ym_out[par], turn * 16)
                    V.tensor_copy(ym[par][:, :], p_y[par][:, 0:D]).then_inc(s["y_ready"], 1)

                def first(turn, t, par):
                    hid_t_copy(t, par)

                def step(turn, t, par):
                    y_copy(turn if par else turn - 1, t - 1, 1 - par)
                    hid_t_copy(t, par)

                def end(turn, t, par):
                    step(turn, t, par)
                    y_copy(turn, t, par)

                moe_pipeline(first, step, end, plain_repeat(dve))

            @block.tensor
            def _(pe):
                def turn_x(turn, t, par):
                    pe.wait_ge(xm_in[par], turn * 16 + 16)
                    wait(pe, s["x_ready"], t)
                    for c in range(C):
                        ins = nc.tensor.transpose(p_x[:, c, :], xm[par][:, c * P:(c + 1) * P], const["identity"][:, :])
                    ins.then_inc(s["x_mm"], 1)

                def up(t, par, expert):
                    pe.wait_ge(s["x_ready"], t + 1)
                    wait(pe, s["hid_ready"], t - 1 if not isinstance(t, int) or t >= 2 else 0)
                    for c in range(C):
                        ins = nc.tensor.matmul(p_h[par][:, :], xm_t[par][:, c, :], w1[:, bass.ds(expert * C + c, 1), :],
                                               start=(c == 0), stop=(c == C - 1))
                    ins.then_inc(s["h_mm"], 1)

                def turn_hidden(t, par):
                    pe.wait_ge(s["hid_ready"], t + 1)
                    wait(pe, s["t_ready"], t - 1 if not isinstance(t, int) or t >= 2 else 0)
                    for c in range(K4):
                        ins = nc.tensor.transpose(p_t[par][:, c, :], hid[par][:, c * P:(c + 1) * P], const["identity"][:, :])
                    ins.then_inc(s["t_mm"], 1)

                def down(t, par, expert):
                    pe.wait_ge(s["t_ready"], t + 1)
                    wait(pe, s["y_ready"], t - 1 if not isinstance(t, int) or t >= 2 else 0)
                    for c in range(K4):
                        ins = nc.tensor.matmul(p_y[par][:, 0:D], hid_t[par][:, c, :], w2[:, bass.ds(expert * K4 + c, 1), :],
                                               start=(c == 0), stop=(c == K4 - 1))
                    ins.then_inc(s["y_mm"], 1)

                def expert_of(t):
                    return pe.value_load(expert_i[0:1, bass.ds(t, 1)], min_val=0, max_val=E - 1)

                def first(turn, t, par):
                    turn_x(0, 0, 0)
                    up(t, par, expert_of(t))
                    turn_x(0, 1, 1)
                    turn_hidden(t, par)

                def step(turn, t, par):
                    up(t, par, expert_of(t))
                    turn_x(turn + 1 if par else turn, t + 1, 1 - par)
                    down(t - 1, 1 - par, expert_of(t - 1))
                    turn_hidden(t, par)

                def end(turn, t, par):
                    up(t, par, expert_of(t))
                    down(t - 1, 1 - par, expert_of(t - 1))
                    turn_hidden(t, par)
                    down(t, par, expert_of(t))

                pe.wait_ge(s["table_ready"], 1)
                pe.wait_ge(keep["experts_in"], 32)
                moe_pipeline(first, step, end, plain_repeat(pe))


def gather_and_end(nc, mem_all, dram, const, keep):
    with ExitStack() as stack:
        m = Memory(nc, stack, "en")
        at = [m.sb(f"at{i}", [P, 2], U32) for i in range(2)]
        y = [[m.sb(f"y{i}{k}", [P, D]) for k in range(2)] for i in range(2)]
        acc = m.sb("acc", [P, 2, D])
        stats, mv = m.sb("stats", [P, 2, 6]), m.sb("mv", [P, 2, 2])
        var, rstd = m.sb("var", [P, 2]), m.sb("rstd", [P, 2])
        out = [m.sb(f"out{i}", [P, 2, D]) for i in range(2)]
        names = "at_ready at_read y_read var_ready rstd_ready out_ready pool_step dve_step".split()
        s = {n: m.sem(n) for n in names}
        out_stored = [m.sem(f"out_stored{i}") for i in range(2)]
        y_in = [m.sem(f"y_in{i}") for i in range(2)]
        resid = keep["resid"]

        with nc.Block() as block:

            @block.gpsimd
            def _(pool):
                def gather(j, par):
                    wait_apart(pool, s["at_ready"], j * 2 + par + 1)
                    for k in range(2):
                        nc.gpsimd.indirect_dma_start(
                            out=y[par][k][:, :], out_offset=None, in_=dram["results"],
                            in_offset=bass.IndirectOffsetOnAxis(ap=at[par][:, k:k + 1], axis=0)).then_inc(y_in[par], 16)

                def root(j):
                    wait_apart(pool, s["var_ready"], j + 1)
                    nc.gpsimd.tensor_scalar(var[:, :], mv[:, :, 1], EPS, None, ALU.add).then_inc(s["pool_step"], 1)
                    pool.wait_ge(s["pool_step"], j + 1)
                    nc.gpsimd.tensor_tensor(rstd[:, :], var[:, :], const["minus_half"][:, 0:2], ALU.pow)\
                      .then_inc(s["rstd_ready"], 1)

                gather(0, 0)
                gather(0, 1)
                with pool.Fori(0, TILES // 2 - 1) as j:
                    gather(j + 1, 0)
                    gather(j + 1, 1)
                    root(j)
                root(TILES // 2 - 1)

            @block.sync
            def _(sp):
                def store(q, par):
                    sp.wait_ge(s["out_ready"], q * 4 + 2 * par + 2)
                    sp.dma_start(dram["out_group"][:, bass.ds(q * 4 + 2 * par, 2), :], out[par][:, :, :])\
                      .then_inc(out_stored[par], 16)

                with sp.Fori(0, TILES // 4) as q:
                    store(q, 0)
                    store(q, 1)
                for par in range(2):
                    sp.wait_ge(out_stored[par], TILES // 4 * 16)

            @block.vector
            def _(dve):
                V = nc.vector
                steps = Steps(dve, s["dve_step"])

                def indices(j, par):
                    V.tensor_copy(at[par][:, :], keep["result"][:, bass.ds(j * 2 + par, 1), :].rearrange("p a k -> p (a k)"))\
                     .then_inc(s["at_ready"], 1)

                def combine(q, pair, last):
                    j = q * 2 + pair
                    for par in range(2):
                        dve.wait_ge(y_in[par], j * 32 + 32)
                        gate = keep["gate"][:, bass.ds(j * 2 + par, 1), :].rearrange("p a k -> p (a k)")
                        steps.chain(V.scalar_tensor_tensor(acc[:, par, :], y[par][0][:, :], gate[:, 0:1],
                                                           resid[:, bass.ds(j * 2 + par, 1), :].rearrange("p a d -> p (a d)"),
                                                           ALU.mult, ALU.add))
                        steps.need_apart(steps.mark(V.scalar_tensor_tensor(acc[:, par, :], y[par][1][:, :], gate[:, 1:2],
                                                                           acc[:, par, :], ALU.mult, ALU.add)))
                        if not last:
                            indices(j + 1, par)
                    layer_norm_stats(steps, nc, acc, stats, mv, s["var_ready"])
                    dve.wait_ge(s["rstd_ready"], j + 1)
                    wait(dve, out_stored[pair], q * 16)
                    for t in range(2):
                        V.tensor_scalar(out[pair][:, t, :], acc[:, t, :], mv[:, t, 0:1], rstd[:, t:t + 1],
                                        ALU.subtract, ALU.mult).then_inc(s["out_ready"], 1)
                    dve.wait_ge(s["out_ready"], j * 2 + 2)

                indices(0, 0)
                indices(0, 1)
                combine(0, 0, False)
                combine(0, 1, False)
                for q in steps.repeat(TILES // 4 - 2, 14):
                    combine(q + 1, 0, False)
                    combine(q + 1, 1, False)
                combine(TILES // 4 - 1, 0, False)
                combine(TILES // 4 - 1, 1, True)


def constants(nc, m, dram):
    const = {
        "identity": m.sb("identity", [P, P]),
        "head_mask": m.sb("head_mask", [P, 8]),
        "minus_half": m.sb("minus_half", [P, NI]),
    }
    step = m.sem("const_step")
    with nc.Block() as block:

        @block.gpsimd
        def _(pool):
            nc.gpsimd.memset(const["identity"][:, :], 0.0).then_inc(step, 1)
            nc.gpsimd.memset(const["head_mask"][:, :], 1.0).then_inc(step, 1)
            nc.gpsimd.memset(const["minus_half"][:, :], -0.5).then_inc(step, 1)
            pool.wait_ge(step, 3)
            nc.gpsimd.affine_select(out=const["identity"][:, :], in_=const["identity"][:, :], compare_op=ALU.not_equal,
                                    fill=1.0, base=0, pattern=[[-1, P]], channel_multiplier=1).then_inc(step, 1)
            nc.gpsimd.affine_select(out=const["head_mask"][:, :], in_=const["head_mask"][:, :], compare_op=ALU.is_ge,
                                    fill=0.0, base=0, pattern=[[-HD, 8]], channel_multiplier=1).then_inc(step, 1)
            pool.wait_ge(step, 5)
            nc.gpsimd.affine_select(out=const["head_mask"][:, :], in_=const["head_mask"][:, :], compare_op=ALU.is_ge,
                                    fill=0.0, base=HD - 1, pattern=[[HD, 8]], channel_multiplier=-1).then_inc(step, 1)
            pool.wait_ge(step, 6)
    return const


def decoder_kernel(nc, dram):
    with ExitStack() as stack:
        m = Memory(nc, stack, "all")
        def scratch(name, shape):
            return nc.dram_tensor(name, shape, F32, kind="Internal").ap()
        rows = "(t p) d -> p t d"
        dram = dict(dram)
        dram["x_rows"] = dram["x"].rearrange(rows, p=P)
        x1 = scratch("x1_rows", [TOKENS, D])
        x2 = scratch("x2_rows", [TOKENS, D])
        dram["x1"], dram["x2"] = x1.rearrange(rows, p=P), x2.rearrange(rows, p=P)
        dram["x2_group"] = x2.rearrange("(p i) d -> p i d", p=P)
        dram["dispatched"] = scratch("dispatched", [E * SEGMENT, D])
        dram["results"] = scratch("results", [MOE_TILES * P, D])
        dram["out_group"] = dram["out"].rearrange("(p i) d -> p i d", p=P)
        const = constants(nc, m, dram)
        linear_attention(nc, m, dram, const)
        cross_attention(nc, m, dram, const)
        keep = {
            "resid": m.sb("resid", [P, TILES, D]),
            "w1": m.sb("w1", [P, E * C, F]),
            "w2": m.sb("w2", [P, E * K4, D]),
            "ln2_w": m.sb("ln2_w", [P, C]),
            "ln2_b": m.sb("ln2_b", [P, C]),
            "hot": m.sb("hot", [P, 2, TILES, E]),
            "gate": m.sb("gate", [P, TILES, 2]),
            "slot": m.sb("slot", [P, TILES, 2]),
            "result": m.sb("result", [P, TILES, 2], U32),
            "count": m.sb("count", [P, E]),
            "experts_in": m.sem("experts_in"),
        }
        batch_axis_attention(nc, m, dram, const, keep)
        experts_and_end(nc, m, dram, const, keep)
        gather_and_end(nc, m, dram, const, keep)


def kernel(x, ctx_1024, L0_attn_w_qkv, L0_attn_w_out, L0_attn_b_out, L0_xattn_Wq, L0_xattn_bq, L0_xattn_Wk, L0_xattn_bk,
           L0_xattn_Wv, L0_xattn_bv, L0_ffn_ln1_weight, L0_ffn_ln1_bias, L0_ffn_ln2_weight, L0_ffn_ln2_bias,
           L0_ffn_qkv_weight, L0_ffn_proj_weight, L0_ffn_router_weight, L0_ffn_moe_w1, L0_ffn_moe_w2):
    from concourse import bacc
    from concourse.bass_utils import run_bass_kernel_spmd

    def dense(a):
        return np.ascontiguousarray(a)

    def features_first(a):
        return dense(np.asarray(a).T.reshape(C, P, -1).transpose(1, 0, 2))

    def columns(a):
        return dense(np.asarray(a).reshape(C, P).T)

    x_rows = np.asarray(x).reshape(TOKENS, D)
    qk_rows = (H + KV) * HD
    arrays = {
        "x": dense(x_rows),
        "x_t": features_first(x_rows),
        "w_qkv": features_first(L0_attn_w_qkv),
        "w_out": features_first(L0_attn_w_out),
        "b_out": dense(L0_attn_b_out),
        "ctx_t": features_first(np.asarray(ctx_1024).reshape(-1, D)),
        "xw_q": dense(np.asarray(L0_xattn_Wq).reshape(C, P, D).transpose(1, 0, 2)),
        "xw_k": features_first(L0_xattn_Wk),
        "xw_v": features_first(L0_xattn_Wv),
        "xb_q": columns(L0_xattn_bq),
        "xb_k": columns(L0_xattn_bk),
        "xb_v": dense(L0_xattn_bv),
        "w_qk": features_first(np.asarray(L0_ffn_qkv_weight)[:qk_rows]),
        "w_v": features_first(np.asarray(L0_ffn_qkv_weight)[qk_rows:]),
        "w_proj": features_first(L0_ffn_proj_weight),
        "w_router": features_first(L0_ffn_router_weight),
        "moe_w1": dense(np.asarray(L0_ffn_moe_w1).reshape(E, C, P, F).transpose(2, 0, 1, 3)),
        "moe_w2": dense(np.asarray(L0_ffn_moe_w2).reshape(E, K4, P, D).transpose(2, 0, 1, 3)),
        "ln1_w": columns(L0_ffn_ln1_weight),
        "ln1_b": columns(L0_ffn_ln1_bias),
        "ln2_w": columns(L0_ffn_ln2_weight),
        "ln2_b": columns(L0_ffn_ln2_bias),
    }
    nc = bacc.Bacc("TRN2", target_bir_lowering=False, num_devices=1)
    dram = {
        name: nc.dram_tensor(f"in_{name}_dram", a.shape, mybir.dt.from_np(a.dtype), kind="ExternalInput").ap()
        for name, a in arrays.items()
    }
    dram["out"] = nc.dram_tensor("out_0_dram", (TOKENS, D), F32, kind="ExternalOutput").ap()
    decoder_kernel(nc, dram)
    r = run_bass_kernel_spmd(nc, [{f"in_{name}_dram": a for name, a in arrays.items()}], core_ids=[0])
    return r.results[0]["out_0_dram"].reshape(B, N, D)
```

```python
from contextlib import ExitStack

import numpy as np

import concourse.bass as bass
from concourse import mybir

F32 = mybir.dt.float32
BF16 = mybir.dt.bfloat16
I32 = mybir.dt.int32
U32 = mybir.dt.uint32
ALU = mybir.AluOpType
ACT = mybir.ActivationFunctionType
AX = mybir.AxisListType.X

P = 128
B, N, D = 16, 256, 256
TOKENS = B * N
C = D // P
T = N // P
HD = 16
CTX = 77
H, KV = 16, 4
REP = H // KV
NI = 8
GROUPS = TOKENS // P // NI
TILES = TOKENS // P
E, F = 8, 512
K4 = F // P
SEGMENT = TOKENS + 2 * P
ROW = D + 5
MOE_TILES = 2 * TOKENS // P + E - 1
EPS = 1e-5
BIG = 3.4028234663852886e38


class Steps:

    def __init__(self, eng, sem):
        self.eng, self.sem, self.base, self.n = eng, sem, 0, 0

    def mark(self, ins):
        ins.then_inc(self.sem, 1)
        self.n += 1
        return self.base + self.n

    def need(self, value):
        self.eng.wait_ge(self.sem, value)

    def need_apart(self, value):
        wait_apart(self.eng, self.sem, value)

    def chain(self, ins):
        self.need(self.mark(ins))

    def repeat(self, count, per):
        entry = self.base + self.n
        with self.eng.Fori(0, count) as j:
            self.base, self.n = j * per + entry, 0
            yield j
            assert self.n == per, f"{self.n} steps a turn"
        self.base, self.n = entry + count * per, 0


def wait(eng, sem, value):
    if not isinstance(value, int) or value > 0:
        eng.wait_ge(sem, value)


def wait_apart(eng, sem, value):
    eng.wait_ge(sem, value)
    eng.nop(nofuse=True)


def bcast(ap, shape):
    return ap.to_broadcast(shape)


class Batch:

    def __init__(self, turn, par):
        self.turn, self.par, self.n = turn, par, turn * 2 + par

    def off(self, d):
        return Batch(self.turn + (self.par + d) // 2, (self.par + d) % 2)

    @property
    def there(self):
        return not isinstance(self.n, int) or 0 <= self.n < B


def upto(n):
    return min(n, B) if isinstance(n, int) else n


class Memory:
    def __init__(self, nc, stack, prefix):
        self.nc, self.stack, self.prefix = nc, stack, prefix

    def sb(self, name, shape, dt=F32):
        return self.stack.enter_context(self.nc.sbuf_tensor(f"{self.prefix}_{name}", shape, dt))

    def ps(self, name, shape):
        return self.stack.enter_context(self.nc.psum_tensor(f"{self.prefix}_{name}", shape, F32))

    def sem(self, name):
        return self.stack.enter_context(self.nc.semaphore(f"{self.prefix}_{name}"))


def layer_norm_stats(steps, nc, rows, stats, mv, to_pool):
    k = rows.shape[1]
    for t in range(k):
        last = steps.mark(nc.vector.bn_stats(stats[:, t, :], rows[:, t, :]))
    steps.need_apart(last)
    for t in range(k):
        ins = nc.vector.bn_aggr(mv[:, t, :], stats[:, t, :])
        if t < k - 1:
            steps.mark(ins)
    ins.then_inc(to_pool, 1)


def context_keys(nc, mem_all, dram, const, kept):
    KEYS = B * CTX
    PIECES = 4
    CH = KEYS // PIECES
    qk, k_bias = kept["qk"], kept["k_bias"]
    with ExitStack() as stack:
        m = Memory(nc, stack, "ck")
        w_q, w_k = m.sb("w_q", [P, C, D]), m.sb("w_k", [P, C, D])
        b_q, b_k = m.sb("b_q", [P, C]), m.sb("b_k", [P, C])
        b_q_cols = m.sb("b_q_cols", [P, C, P])
        ctx_t = m.sb("ctx_t", [P, C, KEYS])
        k_t = m.sb("k_t", [P, C, KEYS])
        p_set = [m.ps(f"p_set{i}", [P, 512]) for i in range(4)]
        wk_in, wq_in, biases_in = m.sem("wk_in"), m.sem("wq_in"), m.sem("biases_in")
        ctx_in = [m.sem(f"ctx_in{i}") for i in range(PIECES)]
        bq_cols, piece_mm = m.sem("bq_cols"), m.sem("piece_mm")
        act_read, dve_read = m.sem("act_read"), m.sem("dve_read")

        pieces = [("k", o, ch) for ch in range(PIECES) for o in range(C)]
        for ch in range(PIECES):
            pieces += [("qk", o, ch) for o in range(C)] + [("bias", 0, ch)]

        def wait_read(eng, n):
            eng.wait_ge(dve_read if n % 2 else act_read, n // 2 + 1)

        with nc.Block() as block:

            @block.sync
            def _(sp):
                sp.dma_start(w_k[:, :, :], dram["xw_k"]).then_inc(wk_in, 16)
                for ch in range(PIECES):
                    cols = slice(ch * CH, (ch + 1) * CH)
                    sp.dma_start(ctx_t[:, :, cols], dram["ctx_t"][:, :, cols]).then_inc(ctx_in[ch], 16)
                sp.dma_start(w_q[:, :, :], dram["xw_q"]).then_inc(wq_in, 16)
                for t, name in (("w_qkv", "w_qkv"), ("w_out", "w_out"), ("w_v", "xw_v")):
                    sp.dma_start(kept[t][:, :, :], dram[name]).then_inc(kept["weights_in"], 16)

            @block.scalar
            def _(act):
                act.dma_start(b_k[:, :], dram["xb_k"]).then_inc(biases_in, 16)
                act.dma_start(b_q[:, :], dram["xb_q"]).then_inc(biases_in, 16)
                act.dma_start(kept["b_out"][:, :], dram["b_out"].partition_broadcast(P)).then_inc(kept["weights_in"], 16)
                act.dma_start(kept["b_v"][:, :], dram["xb_v"].partition_broadcast(P)).then_inc(kept["weights_in"], 16)
                act.wait_ge(biases_in, 32)
                for n in range(0, len(pieces), 2):
                    kind, o, ch = pieces[n]
                    cols = slice(ch * CH, (ch + 1) * CH)
                    act.wait_ge(piece_mm, n + 1)
                    src = p_set[n % 4][:, 0:CH]
                    if kind == "k":
                        ins = nc.scalar.activation(k_t[:, o, cols], src, ACT.Identity, bias=b_k[:, o:o + 1])
                    else:
                        ins = nc.scalar.activation(qk[:, o, cols] if kind == "qk" else k_bias[:, cols], src, ACT.Copy)
                    ins.then_inc(act_read, 1)

            @block.vector
            def _(dve):
                dve.wait_ge(biases_in, 32)
                nc.vector.tensor_copy(b_q_cols[:, :, :], bcast(b_q[:, :].unsqueeze(2), [P, C, P])).then_inc(bq_cols, 1)
                for n in range(1, len(pieces), 2):
                    kind, o, ch = pieces[n]
                    cols = slice(ch * CH, (ch + 1) * CH)
                    dve.wait_ge(piece_mm, n + 1)
                    src = p_set[n % 4][:, 0:CH]
                    if kind == "k":
                        ins = nc.vector.tensor_scalar(k_t[:, o, cols], src, b_k[:, o:o + 1], None, ALU.add)
                    else:
                        ins = nc.vector.tensor_copy(qk[:, o, cols] if kind == "qk" else k_bias[:, cols], src)
                    ins.then_inc(dve_read, 1)

            @block.tensor
            def _(pe):
                pe.wait_ge(wk_in, 16)
                for n, (kind, o, ch) in enumerate(pieces):
                    cols = slice(ch * CH, (ch + 1) * CH)
                    if n >= 4:
                        wait_read(pe, n - 4)
                    if kind == "k":
                        pe.wait_ge(ctx_in[ch], 16)
                        pairs = [(w_k[:, c, o * P:(o + 1) * P], ctx_t[:, c, cols]) for c in range(C)]
                    else:
                        if kind == "qk" and o == 0:
                            pe.wait_ge(wq_in, 16)
                            pe.wait_ge(bq_cols, 1)
                            for c in range(C):
                                wait_read(pe, ch * C + c)
                        pairs = [(w_q[:, c, o * P:(o + 1) * P] if kind == "qk" else b_q_cols[:, c, :], k_t[:, c, cols])
                                 for c in range(C)]
                    for i, (lhs, rhs) in enumerate(pairs):
                        ins = nc.tensor.matmul(p_set[n % 4][:, 0:CH], lhs, rhs, start=(i == 0), stop=(i == C - 1))
                    ins.then_inc(piece_mm, 1)
                wait_read(pe, len(pieces) - 1)
                wait_read(pe, len(pieces) - 2)


def two_attentions(nc, mem_all, dram, const, kept, keep):
    with ExitStack() as stack:
        m = Memory(nc, stack, "at")
        w_qkv, w_out, b_out, w_v, b_v = (kept[n] for n in ("w_qkv", "w_out", "b_out", "w_v", "b_v"))
        qk, k_bias, weights_in = kept["qk"], kept["k_bias"], kept["weights_in"]
        resid, x2_in = keep["resid"], keep["x2_in"]
        x_t = [m.sb(f"x_t{i}", [P, C, N]) for i in range(2)]
        x_tok = [m.sb(f"x_tok{i}", [P, T, D]) for i in range(2)]
        e_q, r_q = m.sb("e_q", [P, C * N]), m.sb("r_q", [P, C * N])
        e_k, r_k = m.sb("e_k", [P, T, D]), m.sb("r_k", [P, T, D])
        q = [m.sb(f"q{i}", [P, C, N]) for i in range(2)]
        k = [m.sb(f"k{i}", [P, T, D]) for i in range(2)]
        v = [m.sb(f"v{i}", [P, T, C, P + 1]) for i in range(2)]
        kv_sum = m.sb("kv_sum", [P, C, P + P // HD])
        den = m.sb("den", [P, T, H])
        rec = m.sb("rec", [P, T, H])
        att = m.sb("att", [P, T, D])
        att_t = m.sb("att_t", [P, C, N])
        x1 = [m.sb(f"x1_{i}", [P, T, D]) for i in range(2)]
        x1_bv = [m.sb(f"x1_bv{i}", [P, T, D]) for i in range(2)]
        ctx_b = [m.sb(f"ctx_b{i}", [P, C, CTX]) for i in range(2)]
        x1_t = m.sb("x1_t", [P, C, N])
        xv = m.sb("xv", [CTX, D])
        sc = m.sb("sc", [P, T, CTX])
        top = m.sb("top", [P, T])
        prob = m.sb("prob", [P, T, CTX])
        total = m.sb("total", [P, T])
        total_rec = m.sb("total_rec", [P, T])
        prob_t = m.sb("prob_t", [CTX, T, P])
        x2 = [m.sb(f"x2_{i}", [P, T, D]) for i in range(2)]
        s = [m.sb(f"s{i}", [P, T, D]) for i in range(2)]
        stats = [m.sb(f"stats{i}", [P, T, 6]) for i in range(2)]
        mv = [m.sb(f"mv{i}", [P, T, 2]) for i in range(2)]
        var = [m.sb(f"var{i}", [P, T]) for i in range(2)]
        rstd = [m.sb(f"rstd{i}", [P, T]) for i in range(2)]

        p_sum = p_x1 = m.ps("p_sum_x1", [P, C, N])
        p_q = p_s = m.ps("p_q_s", [P, C, N])
        p_kv = [m.ps(f"p_kv{t}", [P, 2 * D]) for t in range(T)]
        p_num = [m.ps("p_num_v", [P, 2 * D]), m.ps("p_num_p", [P, 2 * D])]
        p_v, p_p = p_num
        p_out = p_att = m.ps("p_out_att", [P, 2, D])
        p_o = m.ps("p_o", [P, T, D])

        x_t_in, x_tok_in, ctx_in, x2_out = ([m.sem(f"{n}{i}") for i in range(2)] for n in ("x_t_in", "x_tok_in", "ctx_in", "x2_out"))
        s_ready, var_ready, var_done, rstd_ready = (
            [m.sem(f"{n}{i}") for i in range(2)] for n in ("s_ready", "var_ready", "var_done", "rstd_ready"))
        (ones_set, q_mm, kv_mm, sum_mm, num_mm, out_mm, q_exp, kv_act, att_mm, q_ready, k_ready, diag_ready, att_ready, att_t_ready,
         bias_added, x1_ready, x1_bv_ready, x1_t_mm, s_mm, p_t_mm, v_mm, o_mm, x1_t_ready, sc_ready, exp_done,
         prob_t_ready, xv_ready, x2_ready, dve_step) = (m.sem(n) for n in (
             "ones_set", "q_mm", "kv_mm", "sum_mm", "num_mm", "out_mm", "q_exp", "kv_act", "att_mm", "q_ready", "k_ready",
             "diag_ready", "att_ready", "att_t_ready", "bias_added", "x1_ready", "x1_bv_ready", "x1_t_mm", "s_mm", "p_t_mm", "v_mm",
             "o_mm", "x1_t_ready", "sc_ready", "exp_done", "prob_t_ready", "xv_ready", "x2_ready", "dve_step"))

        def pipeline(step, repeat):
            for b in range(-1, 4):
                step(Batch(b // 2, b % 2))
            for j in repeat(B // 2 - 3):
                step(Batch(j + 2, 0))
                step(Batch(j + 2, 1))
            for b in range(B - 2, B + 2):
                step(Batch(b // 2, b % 2))

        def plain_repeat(eng):
            def repeat(count):
                with eng.Fori(0, count) as j:
                    yield j
            return repeat

        with nc.Block() as block:

            @block.sync
            def _(sp):
                def load_x_t(k):
                    wait(sp, kv_mm, (k.n - 1) * T)
                    sp.dma_start(x_t[k.par][:, :, :], dram["x_t"][:, :, bass.ds(k.n * N, N)]).then_inc(x_t_in[k.par], 16)

                def load(k):
                    load_x_t(k.off(1))
                    wait(sp, s_ready[0], k.n - 1)
                    sp.dma_start(x_tok[k.par][:, :, :], dram["x_rows"][:, bass.ds(k.n * T, T), :])\
                      .then_inc(x_tok_in[k.par], 16)
                    wait(sp, v_mm, k.n - 1)
                    sp.dma_start(ctx_b[k.par][:, :, :], dram["ctx_t"][:, :, bass.ds(k.n * CTX, CTX)])\
                      .then_inc(ctx_in[k.par], 16)

                load_x_t(Batch(0, 0))
                load(Batch(0, 0))
                load(Batch(0, 1))
                with sp.Fori(0, B // 2 - 2) as j:
                    load(Batch(j + 1, 0))
                    load(Batch(j + 1, 1))
                load(Batch(B // 2 - 1, 0))
                sp.wait_ge(s_ready[0], B - 2)
                sp.dma_start(x_tok[1][:, :, :], dram["x_rows"][:, (B - 1) * T:, :]).then_inc(x_tok_in[1], 16)
                sp.wait_ge(v_mm, B - 2)
                sp.dma_start(ctx_b[1][:, :, :], dram["ctx_t"][:, :, (B - 1) * CTX:]).then_inc(ctx_in[1], 16)
                for first, end in ((0, B - 2), (B - 2, B - 1), (B - 1, B)):
                    for par in range(2):
                        sp.wait_ge(x2_out[par], (end + 1 - par) // 2 * 16)
                    rows = slice(first * P // B, end * P // B)
                    sp.dma_start(resid[rows, :, :], dram["x2_group"][rows, :, :]).then_inc(x2_in, 16)
                sp.wait_ge(x2_in, 48)

            @block.gpsimd
            def _(pool):
                for i in range(2):
                    ins = nc.gpsimd.memset(v[i][:, :, :, P:P + 1], 1.0)
                ins.then_inc(ones_set, 1)
                pool.wait_ge(weights_in, 80)

                def root(which, turns):
                    wait_apart(pool, var_ready[which], turns)
                    nc.gpsimd.tensor_scalar(var[which][:, :], mv[which][:, :, 1], EPS, None, ALU.add).then_inc(var_done[which], 1)
                    pool.wait_ge(var_done[which], turns)
                    nc.gpsimd.tensor_tensor(rstd[which][:, :], var[which][:, :], const["minus_half"][:, 0:T], ALU.pow)\
                      .then_inc(rstd_ready[which], 1)

                def step(k):
                    nxt, pre, old = k.off(1), k.off(-1), k.off(-2)
                    if pre.there:
                        root(0, pre.n + 1)
                        pool.wait_ge(x1_ready, pre.n + 1)
                        wait(pool, s_ready[1], pre.n - 1)
                        nc.gpsimd.tensor_tensor(x1_bv[pre.par][:, :, :], x1[pre.par][:, :, :],
                                                bcast(b_v[:, :].unsqueeze(1), [P, T, D]), ALU.add).then_inc(x1_bv_ready, 1)
                    if old.there:
                        root(1, old.n + 1)
                    if nxt.there:
                        pool.wait_ge(x_tok_in[nxt.par], nxt.turn * 16 + 16)
                        nc.gpsimd.tensor_tensor(x_tok[nxt.par][:, :, :], x_tok[nxt.par][:, :, :],
                                                bcast(b_out[:, :].unsqueeze(1), [P, T, D]), ALU.add).then_inc(bias_added, 1)

                pipeline(step, plain_repeat(pool))

            @block.scalar
            def _(act):
                def q_features(k):
                    act.wait_ge(q_mm, k.n + 1)
                    wait(act, q_ready, k.n)
                    nc.scalar.activation(e_q[:, :], p_q[:, :, :].rearrange("p c n -> p (c n)"), ACT.Exp)
                    nc.scalar.activation(r_q[:, :], p_q[:, :, :].rearrange("p c n -> p (c n)"), ACT.Relu).then_inc(q_exp, 1)

                def kv_features(k, t):
                    act.wait_ge(kv_mm, k.n * T + t + 1)
                    if t == 0:
                        wait(act, k_ready, k.n)
                        wait(act, sum_mm, k.n - 1)
                    nc.scalar.activation(e_k[:, t, :], p_kv[t][:, 0:D], ACT.Exp)
                    nc.scalar.activation(r_k[:, t, :], p_kv[t][:, 0:D], ACT.Relu)
                    nc.scalar.activation(v[k.par][:, t, :, 0:P], p_kv[t][:, D:2 * D].rearrange("p (c e) -> p c e", c=C),
                                         ACT.Copy).then_inc(kv_act, 1)

                def att_t_copy(k):
                    act.wait_ge(att_mm, k.n + 1)
                    wait(act, out_mm, k.n)
                    nc.scalar.activation(att_t[:, :, :], p_att[:, :, :], ACT.Copy).then_inc(att_t_ready, 1)

                def x1_t_copy(k):
                    act.wait_ge(x1_t_mm, k.n + 1)
                    wait(act, s_mm, k.n)
                    nc.scalar.activation(x1_t[:, :, :], p_x1[:, :, :], ACT.Copy).then_inc(x1_t_ready, 1)

                def exponentials(k):
                    act.wait_ge(sc_ready, k.n + 1)
                    wait(act, p_t_mm, k.n)
                    for t in range(T):
                        nc.scalar.activation(prob[:, t, :], sc[:, t, :], ACT.Exp, bias=top[:, t:t + 1],
                                             accum_out=total[:, t:t + 1]).then_inc(exp_done, 1)

                def prob_t_copy(k):
                    act.wait_ge(p_t_mm, k.n + 1)
                    wait(act, o_mm, k.n)
                    nc.scalar.activation(prob_t[:, :, :], p_p[0:CTX, 0:T * P].rearrange("p (t n) -> p t n", t=T),
                                         ACT.Copy).then_inc(prob_t_ready, 1)

                def xv_copy(k):
                    act.wait_ge(v_mm, k.n + 1)
                    nc.scalar.activation(xv[:, :], p_v[0:CTX, 0:D], ACT.Copy).then_inc(xv_ready, 1)

                def store(k):
                    act.wait_ge(x2_ready, k.n + 1)
                    act.dma_start(dram["x2"][:, bass.ds(k.n * T, T), :], x2[k.par][:, :, :]).then_inc(x2_out[k.par], 16)

                def step(k):
                    nxt, pre, old = k.off(1), k.off(-1), k.off(-2)
                    if old.there:
                        prob_t_copy(old)
                        xv_copy(old)
                    if nxt.there:
                        q_features(nxt)
                    if pre.there:
                        x1_t_copy(pre)
                    if nxt.there:
                        kv_features(nxt, 0)
                    if k.there:
                        att_t_copy(k)
                    if pre.there:
                        exponentials(pre)
                    if nxt.there:
                        kv_features(nxt, 1)
                    if old.there:
                        store(old)

                pipeline(step, plain_repeat(act))
                for i in range(2):
                    act.wait_ge(x2_out[i], 16 * B // 2)

            @block.vector
            def _(dve):
                steps = Steps(dve, dve_step)

                def q_combine(k):
                    dve.wait_ge(q_exp, k.n + 1)
                    wait(dve, num_mm, k.n - 1)
                    nc.vector.scalar_tensor_tensor(q[k.par][:, :, :].rearrange("p c n -> p (c n)"), e_q[:, :], 1.0, r_q[:, :],
                                                   ALU.min, ALU.add).then_inc(q_ready, 1)

                def k_combine(n):
                    dve.wait_ge(kv_act, n.n * T + T)
                    wait(dve, sum_mm, n.n - 1)
                    nc.vector.scalar_tensor_tensor(k[n.par][:, :, :], e_k[:, :, :], 1.0, r_k[:, :, :],
                                                   ALU.min, ALU.add).then_inc(k_ready, 1)

                def diagonal(n):
                    dve.wait_ge(sum_mm, n.n + 1)
                    wait(dve, num_mm, n.n)
                    blocks = bcast(const["head_mask"][:, :].unsqueeze(2), [P, 8, HD])
                    for c in range(C):
                        steps.mark(nc.vector.tensor_tensor(kv_sum[:, c, 0:P].rearrange("p (h d) -> p h d", d=HD),
                                                           p_sum[:, c, 0:P].rearrange("p (h d) -> p h d", d=HD),
                                                           blocks, ALU.mult))
                    for c in range(C):
                        ins = nc.vector.tensor_scalar(kv_sum[:, c, P:], const["head_mask"][:, :], p_sum[:, c, P:P + 1],
                                                      None, ALU.mult)
                    ins.then_inc(diag_ready, 1)

                def divide(n):
                    dve.wait_ge(num_mm, n.n + 1)
                    products = [p_num[t][:, 0:C * (P + P // HD)].rearrange("p (c e) -> p c e", c=C) for t in range(T)]
                    for t in range(T):
                        last = steps.mark(nc.vector.tensor_scalar(den[:, t, :].rearrange("p (c h) -> p c h", c=C),
                                                                  products[t][:, :, P:], 1e-6, None, ALU.add))
                    steps.need(last)
                    steps.chain(nc.vector.reciprocal(rec[:, :, :], den[:, :, :]))
                    wait(dve, att_mm, n.n)
                    for t in range(T):
                        for c in range(C):
                            ins = nc.vector.tensor_tensor(
                                att[:, t, c * P:(c + 1) * P].rearrange("p (h d) -> p h d", d=HD),
                                products[t][:, c, 0:P].rearrange("p (h d) -> p h d", d=HD),
                                bcast(rec[:, t, c * 8:(c + 1) * 8].unsqueeze(2), [P, 8, HD]), ALU.mult)
                            if (t, c) != (T - 1, C - 1):
                                steps.mark(ins)
                    ins.then_inc(att_ready, 1)

                def sum_1(n):
                    dve.wait_ge(out_mm, n.n + 1)
                    dve.wait_ge(bias_added, n.n + 1)
                    nc.vector.tensor_tensor(s[0][:, :, :], p_out[:, :, :], x_tok[n.par][:, :, :], ALU.add)\
                      .then_inc(s_ready[0], 1)
                    dve.wait_ge(s_ready[0], n.n + 1)
                    layer_norm_stats(steps, nc, s[0], stats[0], mv[0], var_ready[0])

                def sum_2(n):
                    dve.wait_ge(exp_done, n.n * T + T)
                    steps.chain(nc.vector.reciprocal(total_rec[:, :], total[:, :]))
                    dve.wait_ge(o_mm, n.n + 1)
                    dve.wait_ge(x1_bv_ready, n.n + 1)
                    for t in range(T):
                        ins = nc.vector.scalar_tensor_tensor(s[1][:, t, :], p_o[:, t, :], total_rec[:, t:t + 1],
                                                             x1_bv[n.par][:, t, :], ALU.mult, ALU.add)
                        if t < T - 1:
                            steps.mark(ins)
                    ins.then_inc(s_ready[1], 1)
                    dve.wait_ge(s_ready[1], n.n + 1)
                    layer_norm_stats(steps, nc, s[1], stats[1], mv[1], var_ready[1])

                def normalise(which, n, out, ready):
                    dve.wait_ge(rstd_ready[which], n.n + 1)
                    for t in range(T):
                        ins = nc.vector.tensor_scalar(out[:, t, :], s[which][:, t, :], mv[which][:, t, 0:1],
                                                      rstd[which][:, t:t + 1], ALU.subtract, ALU.mult)
                        if t < T - 1:
                            steps.mark(ins)
                    ins.then_inc(ready, 1)

                def scores(n):
                    dve.wait_ge(s_mm, n.n + 1)
                    wait(dve, exp_done, n.n * T)
                    steps.chain(nc.vector.tensor_tensor(
                        sc[:, :, :], p_s[:, :, 0:CTX],
                        bcast(k_bias[:, bass.ds(n.n * CTX, CTX)].unsqueeze(1), [P, T, CTX]), ALU.add))
                    steps.chain(nc.vector.tensor_reduce(top[:, :], sc[:, :, :], AX, ALU.max))
                    nc.vector.tensor_scalar(top[:, :], top[:, :], -1.0, None, ALU.mult).then_inc(sc_ready, 1)

                def step(n):
                    nxt, pre, old = n.off(1), n.off(-1), n.off(-2)
                    if pre.there:
                        sum_1(pre)
                    if n.there:
                        diagonal(n)
                    if pre.there:
                        wait(dve, x1_t_mm, pre.n - 1)
                        wait(dve, x1_bv_ready, pre.n - 1)
                        normalise(0, pre, x1[pre.par], x1_ready)
                    if nxt.there:
                        q_combine(nxt)
                    if n.there:
                        divide(n)
                    if old.there:
                        sum_2(old)
                    if pre.there:
                        scores(pre)
                    if old.there:
                        wait(dve, x2_out[old.par], old.turn * 16)
                        normalise(1, old, x2[old.par], x2_ready)
                    if nxt.there:
                        k_combine(nxt)

                pipeline(step, lambda count: steps.repeat(count, 2 * 20))

            @block.tensor
            def _(pe):
                def project_q(n):
                    pe.wait_ge(x_t_in[n.par], n.turn * 16 + 16)
                    wait(pe, q_exp, n.n)
                    wait(pe, sc_ready, n.n - 2)
                    for o in range(C):
                        for c in range(C):
                            ins = nc.tensor.matmul(p_q[:, o, :], w_qkv[:, c, o * P:(o + 1) * P], x_t[n.par][:, c, :],
                                                   start=(c == 0), stop=(c == C - 1))
                    ins.then_inc(q_mm, 1)

                def project_kv(n, t):
                    wait(pe, kv_act, (n.n - 1) * T + t + 1)
                    for c in range(C):
                        ins = nc.tensor.matmul(p_kv[t][:, :], x_t[n.par][:, c, t * P:(t + 1) * P],
                                               w_qkv[:, c, D:3 * D], start=(c == 0), stop=(c == C - 1))
                    ins.then_inc(kv_mm, 1)

                def sum_kv(n):
                    pe.wait_ge(k_ready, n.n + 1)
                    pe.wait_ge(kv_act, n.n * T + T)
                    wait(pe, diag_ready, n.n)
                    wait(pe, x1_t_ready, n.n - 1)
                    for c in range(C):
                        for t in range(T):
                            ins = nc.tensor.matmul(p_sum[:, c, 0:P + 1], k[n.par][:, t, c * P:(c + 1) * P],
                                                   v[n.par][:, t, c, :], start=(t == 0), stop=(t == T - 1))
                    ins.then_inc(sum_mm, 1)

                def numerators(n):
                    pe.wait_ge(diag_ready, n.n + 1)
                    pe.wait_ge(q_ready, n.n + 1)
                    wait(pe, att_ready, n.n)
                    wait(pe, xv_ready, n.n - 1)
                    wait(pe, prob_t_ready, n.n - 1)
                    for t in range(T):
                        for c in range(C):
                            ins = nc.tensor.matmul(p_num[t][:, c * (P + P // HD):(c + 1) * (P + P // HD)],
                                                   q[n.par][:, c, t * P:(t + 1) * P], kv_sum[:, c, :], start=True, stop=True)
                    ins.then_inc(num_mm, 1)

                def turn_att(n):
                    pe.wait_ge(att_ready, n.n + 1)
                    wait(pe, s_ready[0], n.n)
                    for t in range(T):
                        for c in range(C):
                            ins = nc.tensor.transpose(p_att[:, c, t * P:(t + 1) * P], att[:, t, c * P:(c + 1) * P],
                                                      const["identity"][:, :])
                    ins.then_inc(att_mm, 1)

                def project_out(n):
                    pe.wait_ge(att_t_ready, n.n + 1)
                    for t in range(T):
                        for c in range(C):
                            ins = nc.tensor.matmul(p_out[:, t, :], att_t[:, c, t * P:(t + 1) * P], w_out[:, c, :],
                                                   start=(c == 0), stop=(c == C - 1))
                    ins.then_inc(out_mm, 1)

                def turn_x1(n):
                    pe.wait_ge(x1_ready, n.n + 1)
                    pe.wait_ge(diag_ready, upto(n.n + 2))
                    for t in range(T):
                        for c in range(C):
                            ins = nc.tensor.transpose(p_x1[:, c, t * P:(t + 1) * P], x1[n.par][:, t, c * P:(c + 1) * P],
                                                      const["identity"][:, :])
                    ins.then_inc(x1_t_mm, 1)

                def scores(n):
                    pe.wait_ge(x1_t_ready, n.n + 1)
                    pe.wait_ge(q_exp, upto(n.n + 3))
                    wait(pe, sc_ready, n.n)
                    for t in range(T):
                        for c in range(C):
                            ins = nc.tensor.matmul(p_s[:, t, 0:CTX], x1_t[:, c, t * P:(t + 1) * P],
                                                   qk[:, c, bass.ds(n.n * CTX, CTX)], start=(c == 0), stop=(c == C - 1))
                    ins.then_inc(s_mm, 1)

                def turn_prob(n):
                    pe.wait_ge(exp_done, n.n * T + T)
                    pe.wait_ge(att_ready, upto(n.n + 2))
                    wait(pe, prob_t_ready, n.n)
                    for t in range(T):
                        ins = nc.tensor.transpose(p_p[0:CTX, t * P:(t + 1) * P], prob[:, t, :], const["identity"][:, :])
                    ins.then_inc(p_t_mm, 1)

                def project_v(n):
                    pe.wait_ge(ctx_in[n.par], n.turn * 16 + 16)
                    pe.wait_ge(att_ready, upto(n.n + 2))
                    wait(pe, xv_ready, n.n)
                    for c in range(C):
                        ins = nc.tensor.matmul(p_v[0:CTX, 0:D], ctx_b[n.par][:, c, :], w_v[:, c, :],
                                               start=(c == 0), stop=(c == C - 1))
                    ins.then_inc(v_mm, 1)

                def outputs(n):
                    pe.wait_ge(prob_t_ready, n.n + 1)
                    pe.wait_ge(xv_ready, n.n + 1)
                    wait(pe, s_ready[1], n.n)
                    for t in range(T):
                        ins = nc.tensor.matmul(p_o[:, t, :], prob_t[:, t, :], xv[:, :], start=True, stop=True)
                    ins.then_inc(o_mm, 1)

                def step(n):
                    nxt, pre, old = n.off(1), n.off(-1), n.off(-2)
                    if n.there:
                        sum_kv(n)
                    if nxt.there:
                        project_q(nxt)
                    if old.there:
                        outputs(old)
                    if n.there:
                        numerators(n)
                    if pre.there:
                        turn_x1(pre)
                    if nxt.there:
                        project_kv(nxt, 0)
                    if pre.there:
                        scores(pre)
                    if n.there:
                        turn_att(n)
                    if nxt.there:
                        project_kv(nxt, 1)
                    if n.there:
                        project_out(n)
                    if pre.there:
                        turn_prob(pre)
                        project_v(pre)

                pe.wait_ge(weights_in, 80)
                pe.wait_ge(ones_set, 1)
                pipeline(step, plain_repeat(pe))


class Ring:

    def __init__(self, m, name, banks, body, ahead):
        self.banks = [m.ps(f"{name}{i}", [P, 512]) for i in range(banks)]
        self.full = [m.sem(f"{name}_full{i}") for i in range(banks)]
        self.free = [m.sem(f"{name}_free{i}") for i in range(banks)]
        before = [what for what in body if what[0] in ahead]
        after = [what for what in body if what[0] not in ahead]
        assert len(body) % banks == 0
        self.first = {what: i for i, what in enumerate(before)}
        self.at = {what: len(before) + i for i, what in enumerate(body)}
        self.last = {what: len(before) + (GROUPS - 1) * len(body) + i for i, what in enumerate(after)}
        self.ahead, self.per = ahead, len(body) // banks

    def open(self, eng):
        for sem in self.free:
            eng.sem_inc(sem, 1)

    def turn(self, g, what):
        count = len(self.banks)
        if what[0] in self.ahead:
            if isinstance(g, int) and g == 0:
                return self.first[what] % count, self.first[what] // count
            return self.at[what] % count, (g - 1) * self.per + self.at[what] // count
        if isinstance(g, int) and g == GROUPS - 1:
            return self.last[what] % count, self.last[what] // count
        return self.at[what] % count, g * self.per + self.at[what] // count

    def fill(self, pe, g, what):
        bank, turn = self.turn(g, what)
        pe.wait_ge(self.free[bank], turn + 1)
        return self.banks[bank], self.full[bank]

    def read(self, eng, g, what):
        self.wait_full(eng, g, what)
        bank, _ = self.turn(g, what)
        return self.banks[bank], self.free[bank]

    def wait_full(self, eng, g, what):
        bank, turn = self.turn(g, what)
        eng.wait_ge(self.full[bank], turn + 1)

    def wait_read(self, eng, g, what):
        bank, turn = self.turn(g, what)
        eng.wait_ge(self.free[bank], turn + 2)


def batch_axis_attention(nc, mem_all, dram, const, keep):
    PAIRS = NI // 2
    BLK = P // B
    QK = (H + KV) * HD
    with ExitStack() as stack:
        m = Memory(nc, stack, "ba")
        w_qk = m.sb("w_qk", [P, C, QK])
        w_v = m.sb("w_v", [P, C, KV * HD])
        w_proj = m.sb("w_proj", [P, C, D])
        w_router = m.sb("w_router", [P, C, E])
        ln1_w, ln1_b = m.sb("ln1_w", [P, C]), m.sb("ln1_b", [P, C])
        limit = m.sb("limit", [P, B])
        prefix = m.sb("prefix", [P, P], BF16)
        ones = m.sb("ones", [P, P], BF16)
        experts = m.sb("experts", [P, E])
        segments = m.sb("segments", [P, E])
        row_i, row_f, col_f = m.sb("row_i", [P, 1], I32), m.sb("row_f", [P, 1]), m.sb("col_f", [P, B])
        lim_a, lim_b = m.sb("lim_a", [P, B]), m.sb("lim_b", [P, B])
        stats = m.sb("stats", [P, NI, 6])
        mv = m.sb("mv", [P, NI, 2])
        var = m.sb("var", [P, NI])
        rstd = m.sb("rstd", [P, NI])
        xh1 = m.sb("xh1", [P, NI, D])
        att = m.sb("att", [P, NI, D])
        xh2 = m.sb("xh2", [P, NI, ROW])
        xn_t = m.sb("xn_t", [P, C, NI * P])
        qk = m.sb("qk", [P, H + KV, NI, HD])
        v_diag = m.sb("v_diag", [P, BLK * KV, P])
        k_diag = m.sb("k_diag", [P, KV, BLK, P])
        q_t = m.sb("q_t", [P, H, P])
        prob = [m.sb(f"prob{i}", [P, 4 * NI, B]) for i in range(2)]
        top = [m.sb(f"top{i}", [P, 4 * NI]) for i in range(2)]
        total = [m.sb(f"total{i}", [P, 4 * NI]) for i in range(2)]
        rec = [m.sb(f"rec{i}", [P, 4 * NI]) for i in range(2)]
        prob_t = [m.sb(f"prob_t{i}", [P, 4, P]) for i in range(2)]
        o_t = qk[:, 0:H, :, :].rearrange("p h i d -> p (h i d)").rearrange("p (n b) -> p n b", b=BLK)
        h_rows = att
        att_t = [m.sb(f"att_t{i}", [P, 2, C, P]) for i in range(2)]
        xh2_t = att_t
        logits = m.sb("logits", [P, NI, E])
        best = m.sb("best", [P, NI, 8])
        best_at = m.sb("best_at", [P, NI, 8], U32)
        shifted = m.sb("shifted", [P, NI, E + 2])
        gate_sum = m.sb("gate_sum", [P, NI])
        gate_rec = m.sb("gate_rec", [P, NI])
        picked = m.sb("picked", [P, NI + 1, E], BF16)
        place = m.sb("place", [P, NI, E])
        masked = m.sb("masked", [P, NI, E])
        hot = m.sb("hot", [P, 2, NI, E])
        slot = m.sb("slot", [P, NI, 2])
        slot_u = m.sb("slot_u", [P, NI, 2], U32)
        count = m.sb("count", [P, E])
        tokens = m.sb("tokens", [P, TILES])
        tail = m.sb("tail", [P, 2, ROW])
        tail_no = m.sb("tail_no", [P, 2])
        one_e = m.sb("one_e", [P, E])
        tile_no = m.sb("tile_no", [P, MOE_TILES])
        n_tiles, up_to, before = m.sb("n_tiles", [P, E]), m.sb("up_to", [P, E]), m.sb("before", [P, E])
        tail_row, tail_i = m.sb("tail_row", [P, E]), m.sb("tail_i", [P, E], I32)
        count_i, tiles_i = m.sb("count_i", [P, E], I32), m.sb("tiles_i", [P, E], I32)
        spare, per_tile = k_diag[:, :, :, :].rearrange("p k b n -> p (k b n)"), MOE_TILES * E
        wide, hot_t = (spare[:, i * per_tile:(i + 1) * per_tile].rearrange("p (t e) -> p t e", e=E) for i in range(2))
        skip_f, own_f, row_at = (spare[:, 2 * per_tile + i * MOE_TILES:2 * per_tile + (i + 1) * MOE_TILES] for i in range(3))

        turn = Ring(m, "turn", 3, [(n, i) for n in ("p", "o", "a", "x", "q", "h") for i in range(4)], ("x", "q"))
        prod = Ring(m, "prod", 3, [("s", 0), ("s", 1), ("s", 2), ("o", 0), ("s", 3), ("o", 1), ("o", 2), ("o", 3)]
                    + [("a", i) for i in range(4)] + [("qk", i) for i in range(8)] + [("k", 0)], ("qk", "k"))
        p_v = m.ps("p_v", [P, BLK * KV, HD])
        p_r = m.ps("p_r", [P, 512])

        names = ("weights_in biases_in pool_const xh1_ready xh2_ready "
                 "v_mm v_diag_ready top_ready shift_done exp_done rec_ready prob_ready prob_t_ready "
                 "h_ready keep_done logits_mm shifted_ready gates_exp "
                 "picked_ready place_mm slots_ready scattered table_ready tails_out dve_step").split()
        s = {n: m.sem(n) for n in names}
        var_ready, var_done, rstd_ready = ([m.sem(f"{n}{i}") for i in range(2)] for n in ("var_ready", "var_done", "rstd_ready"))
        resid = keep["resid"]

        def groups(first, body, repeat):
            first(0)
            body(0)
            for j in repeat(GROUPS - 2):
                body(j + 1)
            body(GROUPS - 1)

        def there(g):
            return not isinstance(g, int) or 0 <= g < GROUPS

        def plain_repeat(eng):
            def repeat(count):
                with eng.Fori(0, count) as j:
                    yield j
            return repeat

        with nc.Block() as block:

            @block.sync
            def _(sp):
                for t, name in ((ln1_w, "ln1_w"), (ln1_b, "ln1_b"), (keep["ln2_w"], "ln2_w"), (keep["ln2_b"], "ln2_b")):
                    sp.dma_start(t[:, :], dram[name]).then_inc(s["biases_in"], 16)
                for t, name in ((w_qk, "w_qk"), (w_v, "w_v"), (w_proj, "w_proj"), (w_router, "w_router")):
                    sp.dma_start(t[:, :, :], dram[name]).then_inc(s["weights_in"], 16)
                sp.dma_start(keep["w1"][:, :, :].rearrange("p (e c) f -> p e c f", c=C), dram["moe_w1"])\
                  .then_inc(keep["experts_in"], 16)
                sp.dma_start(keep["w2"][:, :, :].rearrange("p (e k) h -> p e k h", k=K4), dram["moe_w2"])\
                  .then_inc(keep["experts_in"], 16)
                sp.wait_ge(s["table_ready"], 1)
                with sp.Fori(0, E) as e:
                    row = sp.value_load(tail_i[0:1, bass.ds(e, 1)], min_val=0, max_val=E * SEGMENT - 2 * P)
                    sp.dma_start(dram["dispatched"][bass.ds(row, 2 * P), :].rearrange("(t p) d -> p t d", p=P),
                                 tail[:, :, :]).then_inc(s["tails_out"], 16)
                sp.wait_ge(s["tails_out"], 16 * E)

            @block.gpsimd
            def _(pool):
                done = s["pool_const"]
                nc.gpsimd.iota(row_i[:, :], [[0, 1]], base=0, channel_multiplier=1).then_inc(done, 1)
                nc.gpsimd.iota(col_f[:, :], [[1, B]], base=0, channel_multiplier=0,
                               allow_small_or_imprecise_dtypes=True).then_inc(done, 1)
                nc.gpsimd.iota(experts[:, :], [[1, E]], base=0, channel_multiplier=0,
                               allow_small_or_imprecise_dtypes=True).then_inc(done, 1)
                nc.gpsimd.iota(segments[:, :], [[SEGMENT, E]], base=0, channel_multiplier=0,
                               allow_small_or_imprecise_dtypes=True).then_inc(done, 1)
                nc.gpsimd.memset(ones[:, :], 1.0).then_inc(done, 1)
                nc.gpsimd.memset(prefix[:, :], 1.0).then_inc(done, 1)
                nc.gpsimd.memset(picked[:, NI, :], 0.0).then_inc(done, 1)
                nc.gpsimd.memset(count[:, :], 0.0).then_inc(done, 1)
                nc.gpsimd.memset(one_e[:, :], 1.0).then_inc(done, 1)
                nc.gpsimd.memset(tail[:, :, :], 0.0).then_inc(done, 1)
                nc.gpsimd.iota(tail_no[:, :], [[P, 2]], base=2 * TOKENS, channel_multiplier=1,
                               allow_small_or_imprecise_dtypes=True).then_inc(done, 1)
                nc.gpsimd.iota(tile_no[:, :], [[1, MOE_TILES]], base=0, channel_multiplier=0,
                               allow_small_or_imprecise_dtypes=True).then_inc(done, 1)
                nc.gpsimd.iota(tokens[:, :], [[1, TILES]], base=0, channel_multiplier=TILES,
                               allow_small_or_imprecise_dtypes=True).then_inc(done, 1)
                pool.wait_ge(done, 13)
                nc.gpsimd.memset(tail[:, :, D + 1:D + 3], -1.0).then_inc(done, 1)
                nc.gpsimd.tensor_copy(tail[:, :, D:D + 1], tail_no[:, :].unsqueeze(2)).then_inc(done, 1)
                nc.gpsimd.affine_select(out=prefix[:, :], in_=prefix[:, :], compare_op=ALU.is_gt, fill=0.0, base=0,
                                        pattern=[[1, P]], channel_multiplier=-1).then_inc(done, 1)

                def rstd_of(which, g):
                    wait_apart(pool, var_ready[which], g + 1)
                    nc.gpsimd.tensor_scalar(var[:, :], mv[:, :, 1], EPS, None, ALU.add).then_inc(var_done[which], 1)
                    pool.wait_ge(var_done[which], g + 1)
                    nc.gpsimd.tensor_tensor(rstd[:, :], var[:, :], const["minus_half"][:, :], ALU.pow)\
                      .then_inc(rstd_ready[which], 1)

                def subtract_top(g, i):
                    pool.wait_ge(s["top_ready"], g * 4 + i + 1)
                    nc.gpsimd.tensor_tensor(prob[i % 2][:, :, :], prob[i % 2][:, :, :],
                                            bcast(top[i % 2][:, :].unsqueeze(2), [P, 4 * NI, B]), ALU.subtract)\
                      .then_inc(s["shift_done"], 1)

                def scale(g, i):
                    pool.wait_ge(s["rec_ready"], g * 4 + i + 1)
                    nc.gpsimd.tensor_tensor(prob[i % 2][:, :, :], prob[i % 2][:, :, :],
                                            bcast(rec[i % 2][:, :].unsqueeze(2), [P, 4 * NI, B]), ALU.mult)\
                      .then_inc(s["prob_ready"], 1)

                def scatter(g):
                    wait_apart(pool, s["slots_ready"], g + 1)
                    for u in range(NI):
                        for k in range(2):
                            nc.gpsimd.indirect_dma_start(
                                out=dram["dispatched"], out_offset=bass.IndirectOffsetOnAxis(ap=slot_u[:, u, k:k + 1], axis=0),
                                in_=xh2[:, u, :], in_offset=None).then_inc(s["scattered"], 16)

                def residual(g):
                    for i in range(PAIRS):
                        pool.wait_ge(s["h_ready"], g * PAIRS + i + 1)
                        rows = resid[:, bass.ds(g * NI + 2 * i, 2), :]
                        nc.gpsimd.tensor_tensor(rows, rows, h_rows[:, 2 * i:2 * i + 2, :], ALU.add).then_inc(s["keep_done"], 1)

                def body(g):
                    subtract_top(g, 0)
                    for i in range(1, 4):
                        subtract_top(g, i)
                        scale(g, i - 1)
                    scale(g, 3)
                    if there(g + 1):
                        rstd_of(0, g + 1)
                    if there(g - 1):
                        scatter(g - 1)
                    rstd_of(1, g)
                    residual(g)

                groups(lambda g: rstd_of(0, g), body, plain_repeat(pool))
                scatter(GROUPS - 1)
                pool.wait_ge(s["scattered"], GROUPS * NI * 2 * 16)
                pool.wait_ge(s["keep_done"], GROUPS * PAIRS)

            @block.scalar
            def _(act):
                act.wait_ge(s["biases_in"], 64)

                def turned(g, what, out, scale=None, bias=None):
                    bank, free = turn.read(act, g, what)
                    src = bank[:, :].rearrange("p (u c n) -> p u c n", u=2, c=C)
                    if scale is None:
                        nc.scalar.activation(out, src, ACT.Copy).then_inc(free, 1)
                        return
                    for c in range(C):
                        ins = nc.scalar.activation(out[:, :, c, :], src[:, :, c, :], ACT.Identity,
                                                   bias=bias[:, c:c + 1], scale=scale[:, c:c + 1])
                    ins.then_inc(free, 1)

                def qk_copy(g, u):
                    bank, free = prod.read(act, g, ("qk", u))
                    nc.scalar.activation(qk[:, :, u, :], bank[:, 0:QK].rearrange("p (h d) -> p h d", d=HD), ACT.Copy)\
                      .then_inc(free, 1)

                def first(g):
                    xn_pairs = xn_t[:, :, :].rearrange("p c (u n) -> p u c n", n=P)
                    for i in range(PAIRS):
                        turned(g, ("x", i), xn_pairs[:, 2 * i:2 * i + 2, :, :], ln1_w, ln1_b)
                        if i >= 1:
                            qk_copy(g, 2 * i - 2)
                            qk_copy(g, 2 * i - 1)
                    qk_copy(g, NI - 2)
                    qk_copy(g, NI - 1)
                    for i in range(4):
                        bank, free = turn.read(act, g, ("q", i))
                        nc.scalar.activation(q_t[:, 4 * i:4 * i + 4, :], bank[:, :].rearrange("p (h n) -> p h n", n=P),
                                             ACT.Copy).then_inc(free, 1)

                def exponential(g, i):
                    act.wait_ge(s["shift_done"], g * 4 + i + 1)
                    nc.scalar.activation(prob[i % 2][:, :, :], prob[i % 2][:, :, :], ACT.Exp).then_inc(s["exp_done"], 1)

                def prob_t_copy(g, i):
                    bank, free = turn.read(act, g, ("p", i))
                    if i >= 2:
                        prod.wait_full(act, g, ("o", i - 2))
                    nc.scalar.activation(prob_t[i % 2][:, :, :], bank[:, :].rearrange("p (u n) -> p u n", n=P),
                                         ACT.Copy).then_inc(free, 1)

                def o_t_copy(g, i):
                    bank, free = prod.read(act, g, ("o", i))
                    nc.scalar.activation(o_t[:, :, 2 * i:2 * i + 2], bank[:, :].rearrange("p (b n) -> p n b", b=2),
                                         ACT.Copy).then_inc(free, 1)

                def body(g):
                    exponential(g, 0)
                    exponential(g, 1)
                    prob_t_copy(g, 0)
                    exponential(g, 2)
                    prob_t_copy(g, 1)
                    if there(g - 1):
                        act.wait_ge(s["shifted_ready"], g)
                        nc.scalar.activation(shifted[:, :, :], shifted[:, :, :], ACT.Exp).then_inc(s["gates_exp"], 1)
                    o_t_copy(g, 0)
                    exponential(g, 3)
                    prob_t_copy(g, 2)
                    o_t_copy(g, 1)
                    prob_t_copy(g, 3)
                    o_t_copy(g, 2)
                    o_t_copy(g, 3)
                    wait(act, s["xh2_ready"], g * NI)
                    wait(act, s["keep_done"], g * PAIRS)
                    for i in range(4):
                        bank, free = turn.read(act, g, ("o", i))
                        nc.scalar.activation(
                            att[:, :, i * 4 * HD:(i + 1) * 4 * HD].rearrange("p i (h d) -> p h i d", d=HD),
                            bank[:, :].rearrange("p (h i d) -> p h i d", h=4, d=HD), ACT.Copy).then_inc(free, 1)
                    for i in range(PAIRS):
                        if i >= 2:
                            prod.wait_full(act, g, ("a", i - 2))
                        turned(g, ("a", i), att_t[i % 2][:, :, :, :])
                    if there(g + 1):
                        first(g + 1)
                    for i in range(PAIRS):
                        if i >= 2:
                            act.wait_ge(s["logits_mm"], g * PAIRS + i - 1)
                        turned(g, ("h", i), xh2_t[i % 2][:, :, :, :], keep["ln2_w"], keep["ln2_b"])

                groups(first, body, plain_repeat(act))
                act.wait_ge(s["shifted_ready"], GROUPS)
                nc.scalar.activation(shifted[:, :, :], shifted[:, :, :], ACT.Exp).then_inc(s["gates_exp"], 1)

            @block.vector
            def _(dve):
                steps = Steps(dve, s["dve_step"])
                turn.open(dve)
                prod.open(dve)
                dve.wait_ge(s["pool_const"], 16)
                steps.chain(nc.vector.tensor_scalar(row_i[:, :], row_i[:, :], B - 1, None, ALU.bitwise_and))
                steps.chain(nc.vector.tensor_copy(row_f[:, :], row_i[:, :]))
                steps.chain(nc.vector.tensor_scalar(limit[:, :], col_f[:, :], row_f[:, 0:1], None, ALU.is_le))
                steps.mark(nc.vector.tensor_scalar(lim_a[:, :], limit[:, :], BIG, None, ALU.mult))
                steps.chain(nc.vector.tensor_scalar(lim_b[:, :], limit[:, :], -1.0, BIG, ALU.add, ALU.mult))
                steps.chain(nc.vector.tensor_tensor(limit[:, :], lim_a[:, :], lim_b[:, :], ALU.add))
                dve.wait_ge(s["biases_in"], 64)
                dve.wait_ge(keep["x2_in"], 48)


                def statistics(rows, ready):
                    for u in range(NI):
                        last = steps.mark(nc.vector.bn_stats(stats[:, u, :], rows(u)))
                    steps.need_apart(last)
                    for u in range(NI):
                        ins = nc.vector.bn_aggr(mv[:, u, :], stats[:, u, :])
                        if u < NI - 1:
                            steps.mark(ins)
                    ins.then_inc(ready, 1)

                def normalise(rows, g, which, out, ready):
                    dve.wait_ge(rstd_ready[which], g + 1)
                    for u in range(NI):
                        nc.vector.tensor_scalar(out[:, u, :], rows(u), mv[:, u, 0:1], rstd[:, u:u + 1],
                                                ALU.subtract, ALU.mult).then_inc(ready, 1)

                def x2_rows(g):
                    return lambda u: resid[:, bass.ds(g * NI + u, 1), :]

                def first(g):
                    bank, free = prod.read(dve, g, ("k", 0))
                    for kv in range(KV):
                        src = bank[:, kv * P:(kv + 1) * P].rearrange("p (t b) -> p b t", b=BLK).unsqueeze(2)
                        ins = nc.vector.tensor_tensor(
                            k_diag[:, kv, :, :].rearrange("p b (i t) -> p b i t", t=B),
                            bcast(src, [P, BLK, NI, B]),
                            bcast(const["head_mask"][:, :].unsqueeze(1).unsqueeze(3), [P, BLK, NI, B]), ALU.mult)
                        if kv < KV - 1:
                            steps.mark(ins)
                    ins.then_inc(free, 1)
                    dve.wait_ge(s["v_mm"], g + 1)
                    nc.vector.tensor_tensor(
                        v_diag[:, :, :].rearrange("p b (i d) -> p b i d", d=HD),
                        bcast(p_v[:, :, :].unsqueeze(2), [P, BLK * KV, NI, HD]),
                        bcast(const["head_mask"][:, :].unsqueeze(1).unsqueeze(3), [P, BLK * KV, NI, HD]), ALU.mult)\
                        .then_inc(s["v_diag_ready"], 1)

                def score_top(g, i):
                    bank, free = prod.read(dve, g, ("s", i))
                    if i >= 2:
                        turn.wait_full(dve, g, ("p", i - 2))
                    nc.vector.scalar_tensor_tensor(prob[i % 2][:, :, :], bank[:, :].rearrange("p (n t) -> p n t", t=B),
                                                   HD ** -0.5, bcast(limit[:, :].unsqueeze(1), [P, 4 * NI, B]),
                                                   ALU.mult, ALU.min).then_inc(free, 1)
                    prod.wait_read(dve, g, ("s", i))
                    nc.vector.tensor_reduce(top[i % 2][:, :], prob[i % 2][:, :, :], AX, ALU.max).then_inc(s["top_ready"], 1)

                def reciprocal_sum(g, i):
                    dve.wait_ge(s["exp_done"], g * 4 + i + 1)
                    steps.chain(nc.vector.tensor_reduce(total[i % 2][:, :], prob[i % 2][:, :, :], AX, ALU.add))
                    nc.vector.reciprocal(rec[i % 2][:, :], total[i % 2][:, :]).then_inc(s["rec_ready"], 1)

                def route_best(g):
                    dve.wait_ge(s["logits_mm"], g * PAIRS + PAIRS)
                    steps.need_apart(steps.mark(nc.vector.tensor_copy(logits[:, :, :],
                                                                      p_r[:, 0:NI * E].rearrange("p (u e) -> p u e", e=E))))
                    for u in range(NI):
                        last = steps.mark(nc.vector.max(best[:, u, :], logits[:, u, :]))
                    return last

                def route_shift(last):
                    steps.need_apart(last)
                    leader = best[:, :, 0:1]
                    steps.mark(nc.vector.tensor_tensor(shifted[:, :, 0:E], logits[:, :, :], bcast(leader, [P, NI, E]),
                                                       ALU.subtract))
                    nc.vector.tensor_tensor(shifted[:, :, E:E + 2], best[:, :, 0:2], bcast(leader, [P, NI, 2]),
                                            ALU.subtract).then_inc(s["shifted_ready"], 1)
                    for u in range(NI):
                        last = steps.mark(nc.vector.max_index(best_at[:, u, :], best[:, u, :], logits[:, u, :]))
                    return last

                def route_pick(g, last):
                    steps.need(last)
                    chosen = xh2[:, :, D + 1:D + 3]
                    steps.mark(nc.vector.tensor_copy(xh2[:, :, D:D + 1], tokens[:, bass.ds(g * NI, NI)].unsqueeze(2)))
                    steps.chain(nc.vector.tensor_copy(chosen, best_at[:, :, 0:2]))
                    for k in range(2):
                        last = steps.mark(nc.vector.tensor_tensor(hot[:, k, :, :], bcast(chosen[:, :, k:k + 1], [P, NI, E]),
                                                                  bcast(experts[:, :].unsqueeze(1), [P, NI, E]), ALU.is_equal))
                    steps.need(last)
                    nc.vector.tensor_tensor(picked[:, 0:NI, :], hot[:, 0, :, :], hot[:, 1, :, :], ALU.add)\
                        .then_inc(s["picked_ready"], 1)

                def route_slots(g):
                    dve.wait_ge(s["gates_exp"], g + 1)
                    steps.chain(nc.vector.tensor_reduce(gate_sum[:, :], shifted[:, :, 0:E], AX, ALU.add))
                    steps.chain(nc.vector.reciprocal(gate_rec[:, :], gate_sum[:, :]))
                    steps.mark(nc.vector.tensor_tensor(xh2[:, :, D + 3:D + 5], shifted[:, :, E:E + 2],
                                                       bcast(gate_rec[:, :].unsqueeze(2), [P, NI, 2]), ALU.mult))
                    dve.wait_ge(s["place_mm"], g + 1)
                    places = p_r[:, NI * E:(2 * NI + 1) * E].rearrange("p (u e) -> p u e", e=E)
                    steps.chain(nc.vector.tensor_tensor(place[:, :, :], places[:, 0:NI, :],
                                                        bcast(count[:, :].unsqueeze(1), [P, NI, E]), ALU.add))
                    steps.mark(nc.vector.tensor_tensor(count[:, :], places[:, NI, :], count[:, :], ALU.add))
                    steps.chain(nc.vector.tensor_tensor(place[:, :, :], place[:, :, :],
                                                        bcast(segments[:, :].unsqueeze(1), [P, NI, E]), ALU.add))
                    for k in range(2):
                        steps.chain(nc.vector.tensor_tensor(masked[:, :, :], place[:, :, :], hot[:, k, :, :], ALU.mult))
                        summed = steps.mark(nc.vector.tensor_reduce(slot[:, :, k:k + 1], masked[:, :, :], AX, ALU.add))
                        steps.need(summed)
                    nc.vector.tensor_copy(slot_u[:, :, :], slot[:, :, :]).then_inc(s["slots_ready"], 1)

                def tile_table():
                    V = nc.vector
                    steps.chain(V.tensor_scalar(count_i[:, :], count[:, :], float(P - 1), None, ALU.add))
                    steps.chain(V.tensor_scalar(tiles_i[:, :], count_i[:, :], 7, None, ALU.logical_shift_right))
                    steps.chain(V.tensor_copy(n_tiles[:, :], tiles_i[:, :]))
                    steps.chain(V.tensor_tensor_scan(up_to[:, :], one_e[:, :], n_tiles[:, :], 0.0, ALU.mult, ALU.add))
                    steps.chain(V.tensor_tensor(before[:, :], up_to[:, :], n_tiles[:, :], ALU.subtract))
                    steps.chain(V.tensor_tensor(tail_row[:, :], count[:, :], segments[:, :], ALU.add))
                    V.tensor_copy(tail_i[:, :], tail_row[:, :]).then_inc(s["table_ready"], 1)
                    expert_f, wide_shape = keep["expert_f"], [P, MOE_TILES, E]
                    steps.chain(V.tensor_tensor(wide, bcast(tile_no[:, :].unsqueeze(2), wide_shape),
                                                bcast(up_to[:, :].unsqueeze(1), wide_shape), ALU.is_ge))
                    steps.chain(V.tensor_reduce(expert_f[:, :], wide, AX, ALU.add))
                    steps.chain(V.tensor_scalar(expert_f[:, :], expert_f[:, :], float(E - 1), None, ALU.min))
                    steps.chain(V.tensor_tensor(hot_t, bcast(expert_f[:, :].unsqueeze(2), wide_shape),
                                                bcast(experts[:, :].unsqueeze(1), wide_shape), ALU.is_equal))
                    for table, out in ((before, skip_f), (n_tiles, own_f)):
                        steps.chain(V.tensor_tensor(wide, hot_t, bcast(table[:, :].unsqueeze(1), wide_shape), ALU.mult))
                        steps.chain(V.tensor_reduce(out[:, :], wide, AX, ALU.add))
                    steps.chain(V.tensor_tensor(skip_f[:, :], tile_no[:, :], skip_f[:, :], ALU.subtract))
                    steps.chain(V.tensor_tensor(skip_f[:, :], skip_f[:, :], own_f[:, :], ALU.min))
                    steps.chain(V.tensor_scalar(skip_f[:, :], skip_f[:, :], float(P), None, ALU.mult))
                    steps.chain(V.scalar_tensor_tensor(row_at[:, :], expert_f[:, :], float(SEGMENT), skip_f[:, :],
                                                       ALU.mult, ALU.add))
                    steps.mark(V.tensor_copy(keep["expert_i"][:, :], expert_f[:, :]))
                    steps.chain(V.tensor_copy(keep["first_i"][:, :], row_at[:, :]))

                def body(g):
                    score_top(g, 0)
                    score_top(g, 1)
                    if there(g - 1):
                        last = route_best(g - 1)
                    reciprocal_sum(g, 0)
                    score_top(g, 2)
                    if there(g - 1):
                        last = route_shift(last)
                    reciprocal_sum(g, 1)
                    score_top(g, 3)
                    if there(g - 1):
                        route_pick(g - 1, last)
                    reciprocal_sum(g, 2)
                    reciprocal_sum(g, 3)
                    if there(g + 1):
                        statistics(x2_rows(g + 1), var_ready[0])
                    if there(g - 1):
                        route_slots(g - 1)
                    if there(g + 1):
                        normalise(x2_rows(g + 1), g + 1, 0, xh1, s["xh1_ready"])
                    for i in range(PAIRS):
                        bank, free = prod.read(dve, g, ("a", i))
                        added = steps.mark(nc.vector.tensor_tensor(
                            h_rows[:, 2 * i:2 * i + 2, :], bank[:, :].rearrange("p (u d) -> p u d", u=2),
                            resid[:, bass.ds(g * NI + 2 * i, 2), :], ALU.add))
                        steps.need(added)
                        dve.sem_inc(free, 1)
                        dve.sem_inc(s["h_ready"], 1)
                    statistics(lambda u: h_rows[:, u, :], var_ready[1])
                    wait(dve, s["scattered"], g * (NI * 2 * 16))
                    normalise(lambda u: h_rows[:, u, :], g, 1, xh2[:, :, 0:D], s["xh2_ready"])
                    if there(g + 1):
                        first(g + 1)

                def start(g):
                    statistics(x2_rows(g), var_ready[0])
                    normalise(x2_rows(g), g, 0, xh1, s["xh1_ready"])
                    first(g)

                groups(start, body, lambda count: steps.repeat(count, 73))
                route_pick(GROUPS - 1, route_shift(route_best(GROUPS - 1)))
                route_slots(GROUPS - 1)
                tile_table()
                dve.wait_ge(s["keep_done"], GROUPS * PAIRS)

            @block.tensor
            def _(pe):
                ident = const["identity"]
                pe.wait_ge(s["weights_in"], 64)
                pe.wait_ge(s["pool_const"], 16)

                def turn_pair(g, what, ready, rows, i):
                    pe.wait_ge(ready, g * NI + 2 * i + 2)
                    bank, full = turn.fill(pe, g, (what, i))
                    for u in range(2):
                        for c in range(C):
                            ins = nc.tensor.transpose(bank[:, (u * C + c) * P:(u * C + c + 1) * P],
                                                      rows[:, 2 * i + u, c * P:(c + 1) * P], ident[:, :])
                    ins.then_inc(full, 1)

                def project_qk(g, i):
                    turn.wait_read(pe, g, ("x", i))
                    for u in (2 * i, 2 * i + 1):
                        bank, full = prod.fill(pe, g, ("qk", u))
                        for c in range(C):
                            ins = nc.tensor.matmul(bank[:, 0:QK], xn_t[:, c, u * P:(u + 1) * P], w_qk[:, c, :],
                                                   start=(c == 0), stop=(c == C - 1))
                        ins.then_inc(full, 1)

                def first(g):
                    turn_pair(g, "x", s["xh1_ready"], xh1, 0)
                    for i in range(1, PAIRS):
                        turn_pair(g, "x", s["xh1_ready"], xh1, i)
                        project_qk(g, i - 1)
                    project_qk(g, PAIRS - 1)
                    wait(pe, s["v_diag_ready"], g)
                    for b in range(BLK):
                        for c in range(C):
                            tokens = xn_t[:, c, :].rearrange("p (n b) -> p n b", b=BLK)[:, :, b]
                            ins = nc.tensor.matmul(p_v[:, b * KV:(b + 1) * KV, :].rearrange("p k d -> p (k d)"), tokens,
                                                   w_v[:, c, :], start=(c == 0), stop=(c == C - 1))
                    ins.then_inc(s["v_mm"], 1)
                    for u in range(NI):
                        prod.wait_read(pe, g, ("qk", u))
                    bank, full = prod.fill(pe, g, ("k", 0))
                    for kv in range(KV):
                        ins = nc.tensor.transpose(bank[:, kv * P:(kv + 1) * P],
                                                  qk[:, H + kv, :, :].rearrange("p i d -> p (i d)"), ident[:, :])
                    ins.then_inc(full, 1)
                    for i in range(4):
                        bank, full = turn.fill(pe, g, ("q", i))
                        for h in range(4):
                            ins = nc.tensor.transpose(bank[:, h * P:(h + 1) * P],
                                                      qk[:, 4 * i + h, :, :].rearrange("p i d -> p (i d)"), ident[:, :])
                        ins.then_inc(full, 1)

                def scores(g, i):
                    bank, full = prod.fill(pe, g, ("s", i))
                    for b2 in range(2):
                        for kv in range(KV):
                            b = 2 * i + b2
                            tile = 2 * b2 + kv // 2
                            rows = slice(64 * (kv % 2), 64 * (kv % 2) + 64)
                            queries = q_t[:, kv * REP:(kv + 1) * REP, :].rearrange("p h n -> p (h n)")\
                                .rearrange("p (n b) -> p n b", b=BLK)[:, :, b]
                            ins = nc.tensor.matmul(bank[rows, tile * P:(tile + 1) * P], queries, k_diag[:, kv, b, :],
                                                   start=True, stop=True)
                    ins.then_inc(full, 1)

                def turn_prob(g, i):
                    pe.wait_ge(s["prob_ready"], g * 4 + i + 1)
                    bank, full = turn.fill(pe, g, ("p", i))
                    for t in range(4):
                        ins = nc.tensor.transpose(bank[:, t * P:(t + 1) * P],
                                                  prob[i % 2][:, t * NI:(t + 1) * NI, :].rearrange("p n t -> p (n t)"),
                                                  ident[:, :])
                    ins.then_inc(full, 1)

                def outputs(g, i):
                    turn.wait_read(pe, g, ("p", i))
                    bank, full = prod.fill(pe, g, ("o", i))
                    for b2 in range(2):
                        for kv in range(KV):
                            tile = 2 * b2 + kv // 2
                            ins = nc.tensor.matmul(bank[:, (b2 * KV + kv) * 64:(b2 * KV + kv + 1) * 64],
                                                   v_diag[:, (2 * i + b2) * KV + kv, :],
                                                   prob_t[i % 2][:, tile, 64 * (kv % 2):64 * (kv % 2) + 64],
                                                   start=True, stop=True)
                    ins.then_inc(full, 1)

                def turn_att(g, i):
                    bank, full = turn.fill(pe, g, ("a", i))
                    for u in range(2):
                        for c in range(C):
                            ins = nc.tensor.transpose(bank[:, (u * C + c) * P:(u * C + c + 1) * P],
                                                      att[:, 2 * i + u, c * P:(c + 1) * P], ident[:, :])
                    ins.then_inc(full, 1)

                def project(g, i):
                    turn.wait_read(pe, g, ("a", i))
                    bank, full = prod.fill(pe, g, ("a", i))
                    for u in range(2):
                        for c in range(C):
                            ins = nc.tensor.matmul(bank[:, u * D:(u + 1) * D], att_t[i % 2][:, u, c, :], w_proj[:, c, :],
                                                   start=(c == 0), stop=(c == C - 1))
                    ins.then_inc(full, 1)

                def route(g, i):
                    turn.wait_read(pe, g, ("h", i))
                    for u in range(2):
                        for c in range(C):
                            ins = nc.tensor.matmul(p_r[:, (2 * i + u) * E:(2 * i + u + 1) * E], xh2_t[i % 2][:, u, c, :],
                                                   w_router[:, c, :], start=(c == 0), stop=(c == C - 1))
                    ins.then_inc(s["logits_mm"], 1)

                def count_places(g):
                    pe.wait_ge(s["picked_ready"], g + 1)
                    places = p_r[:, NI * E:(2 * NI + 1) * E]
                    nc.tensor.matmul(places, prefix[:, :], picked[:, :, :].rearrange("p u e -> p (u e)"), start=True, stop=False)
                    for u in range(NI):
                        ins = nc.tensor.matmul(places[:, (u + 1) * E:(NI + 1) * E], ones[:, :],
                                               bcast(picked[:, u:u + 1, :], [P, NI - u, E]), start=False, stop=(u == NI - 1))
                    ins.then_inc(s["place_mm"], 1)

                def body(g):
                    for i in range(4):
                        turn.wait_read(pe, g, ("q", i))
                    prod.wait_read(pe, g, ("k", 0))
                    pe.wait_ge(s["v_diag_ready"], g + 1)
                    scores(g, 0)
                    scores(g, 1)
                    turn_prob(g, 0)
                    scores(g, 2)
                    outputs(g, 0)
                    turn_prob(g, 1)
                    scores(g, 3)
                    outputs(g, 1)
                    turn_prob(g, 2)
                    outputs(g, 2)
                    if there(g - 1):
                        count_places(g - 1)
                    turn_prob(g, 3)
                    outputs(g, 3)
                    for i in range(4):
                        prod.wait_read(pe, g, ("o", i))
                    for i in range(4):
                        bank, full = turn.fill(pe, g, ("o", i))
                        for h in range(4):
                            head = o_t[:, (4 * i + h) * B:(4 * i + h + 1) * B, :].rearrange("p s b -> p (s b)")
                            ins = nc.tensor.transpose(bank[:, h * P:(h + 1) * P], head, ident[:, :])
                        ins.then_inc(full, 1)
                    for i in range(4):
                        turn.wait_read(pe, g, ("o", i))
                    turn_att(g, 0)
                    for i in range(1, PAIRS):
                        turn_att(g, i)
                        project(g, i - 1)
                    project(g, PAIRS - 1)
                    if there(g + 1):
                        first(g + 1)
                    turn_pair(g, "h", s["xh2_ready"], xh2, 0)
                    for i in range(1, PAIRS):
                        turn_pair(g, "h", s["xh2_ready"], xh2, i)
                        route(g, i - 1)
                    route(g, PAIRS - 1)

                groups(first, body, plain_repeat(pe))
                count_places(GROUPS - 1)


def experts(nc, mem_all, dram, const, keep):
    with ExitStack() as stack:
        m = Memory(nc, stack, "ex")
        xm = [m.sb(f"xm{i}", [P, ROW]) for i in range(2)]
        xm_t = [m.sb(f"xm_t{i}", [P, C, P]) for i in range(2)]
        hid = [m.sb(f"hid{i}", [P, F]) for i in range(2)]
        hid_t = [m.sb(f"hid_t{i}", [P, K4, P]) for i in range(2)]
        ym = [m.sb(f"ym{i}", [P, D]) for i in range(2)]
        hit = m.sb("hit", [P, 2])
        hit_gate = m.sb("hit_gate", [P, 2])
        gate = [m.sb(f"gate{i}", [P, 1]) for i in range(2)]
        home_f = [m.sb(f"home_f{i}", [P, 1]) for i in range(2)]
        home = [m.sb(f"home{i}", [P, 1], U32) for i in range(2)]

        p_x = m.ps("p_x", [P, C, P])
        p_h = [m.ps(f"p_h{i}", [P, F]) for i in range(2)]
        p_t = [m.ps(f"p_t{i}", [P, K4, P]) for i in range(2)]
        p_y = [m.ps(f"p_y{i}", [P, 512]) for i in range(2)]

        names = "x_mm x_ready h_mm hid_ready t_mm t_ready y_mm y_ready home_ready dve_step".split()
        s = {n: m.sem(n) for n in names}
        xm_in = [m.sem(f"xm_in{i}") for i in range(2)]
        ym_out = [m.sem(f"ym_out{i}") for i in range(2)]
        w1, w2 = keep["w1"], keep["w2"]
        LAST = MOE_TILES - 1
        assert MOE_TILES % 2 == 1

        def moe_pipeline(first, step, end, repeat):
            first(0, 0, 0)
            step(0, 1, 1)
            step(1, 2, 0)
            for j in repeat((MOE_TILES - 5) // 2):
                step(j + 1, j * 2 + 3, 1)
                step(j + 2, j * 2 + 4, 0)
            step(LAST // 2 - 1, LAST - 1, 1)
            end(LAST // 2, LAST, 0)

        def plain_repeat(eng):
            def repeat(count):
                with eng.Fori(0, count) as j:
                    yield j
            return repeat

        with nc.Block() as block:

            @block.sync
            def _(sp):
                def load(t, par):
                    row = sp.value_load(keep["first_i"][0:1, bass.ds(t, 1)], min_val=0, max_val=E * SEGMENT - P)
                    wait(sp, s["x_mm"], t - 1)
                    wait(sp, s["home_ready"], t - 1)
                    sp.dma_start(xm[par][:, :], dram["dispatched"][bass.ds(row, P), :]).then_inc(xm_in[par], 16)

                load(0, 0)
                load(1, 1)
                with sp.Fori(0, (MOE_TILES - 3) // 2) as j:
                    load(j * 2 + 2, 0)
                    load(j * 2 + 3, 1)
                load(LAST, 0)

            @block.gpsimd
            def _(pool):
                def send(turn, par):
                    wait(pool, ym_out[1 - par], (turn + par) * 16)
                    wait_apart(pool, s["y_ready"], turn * 2 + par + 1)
                    nc.gpsimd.indirect_dma_start(
                        out=dram["results"], out_offset=bass.IndirectOffsetOnAxis(ap=home[par][:, 0:1], axis=0),
                        in_=ym[par][:, :], in_offset=None).then_inc(ym_out[par], 16)

                send(0, 0)
                send(0, 1)
                with pool.Fori(0, LAST // 2 - 1) as j:
                    send(j + 1, 0)
                    send(j + 1, 1)
                send(LAST // 2, 0)
                pool.wait_ge(ym_out[0], 16 * (LAST // 2 + 1))
                pool.wait_ge(ym_out[1], 16 * (LAST // 2))

            @block.scalar
            def _(act):
                def x_copy(t, par):
                    act.wait_ge(s["x_mm"], t + 1)
                    wait(act, s["h_mm"], t - 1)
                    for c in range(C):
                        ins = nc.scalar.activation(xm_t[par][:, c, :], p_x[:, c, :], ACT.Identity,
                                                   bias=keep["ln2_b"][:, c:c + 1], scale=keep["ln2_w"][:, c:c + 1])
                    ins.then_inc(s["x_ready"], 1)

                def gelu(t, par):
                    act.wait_ge(s["h_mm"], t + 1)
                    wait(act, s["t_mm"], t - 1)
                    nc.scalar.activation(hid[par][:, :], p_h[par][:, :], ACT.Gelu_apprx_tanh).then_inc(s["hid_ready"], 1)

                def first(turn, t, par):
                    x_copy(0, 0)
                    step(turn, t, par)

                def step(turn, t, par):
                    gelu(t, par)
                    x_copy(t + 1, 1 - par)

                moe_pipeline(first, step, lambda turn, t, par: gelu(t, par), plain_repeat(act))

            @block.vector
            def _(dve):
                V = nc.vector
                steps = Steps(dve, s["dve_step"])

                def gates_and_homes(turn, t, par):
                    dve.wait_ge(xm_in[par], turn * 16 + 16)
                    steps.chain(V.tensor_tensor(hit[:, :], xm[par][:, D + 1:D + 3],
                                                bcast(keep["expert_f"][:, bass.ds(t, 1)], [P, 2]), ALU.is_equal))
                    steps.mark(V.tensor_tensor(hit_gate[:, :], hit[:, :], xm[par][:, D + 3:D + 5], ALU.mult))
                    steps.chain(V.scalar_tensor_tensor(home_f[par][:, :], hit[:, 1:2], float(TOKENS), xm[par][:, D:D + 1],
                                                       ALU.mult, ALU.add))
                    V.tensor_tensor(gate[par][:, :], hit_gate[:, 0:1], hit_gate[:, 1:2], ALU.add)\
                     .then_inc(s["home_ready"], 1)

                def hid_t_copy(t, par):
                    dve.wait_ge(s["t_mm"], t + 1)
                    wait(dve, s["y_mm"], t - 1)
                    V.tensor_copy(hid_t[par][:, :, :], p_t[par][:, :, :]).then_inc(s["t_ready"], 1)

                def y_gated(turn, t, par):
                    wait(dve, ym_out[par], turn * 16)
                    dve.wait_ge(s["home_ready"], t + 1)
                    steps.mark(V.tensor_copy(home[par][:, :], home_f[par][:, :]))
                    dve.wait_ge(s["y_mm"], t + 1)
                    V.tensor_scalar(ym[par][:, :], p_y[par][:, 0:D], gate[par][:, 0:1], None, ALU.mult)\
                     .then_inc(s["y_ready"], 1)

                def first(turn, t, par):
                    gates_and_homes(turn, t, par)
                    hid_t_copy(t, par)

                def step(turn, t, par):
                    gates_and_homes(turn, t, par)
                    y_gated(turn if par else turn - 1, t - 1, 1 - par)
                    hid_t_copy(t, par)

                def end(turn, t, par):
                    step(turn, t, par)
                    y_gated(turn, t, par)

                moe_pipeline(first, step, end, lambda count: steps.repeat(count, 2 * 4))

            @block.tensor
            def _(pe):
                def turn_x(turn, t, par):
                    pe.wait_ge(xm_in[par], turn * 16 + 16)
                    wait(pe, s["x_ready"], t)
                    for c in range(C):
                        ins = nc.tensor.transpose(p_x[:, c, :], xm[par][:, c * P:(c + 1) * P], const["identity"][:, :])
                    ins.then_inc(s["x_mm"], 1)

                def up(t, par, expert):
                    pe.wait_ge(s["x_ready"], t + 1)
                    wait(pe, s["hid_ready"], t - 1)
                    for c in range(C):
                        ins = nc.tensor.matmul(p_h[par][:, :], xm_t[par][:, c, :], w1[:, bass.ds(expert * C + c, 1), :],
                                               start=(c == 0), stop=(c == C - 1))
                    ins.then_inc(s["h_mm"], 1)

                def turn_hidden(t, par):
                    pe.wait_ge(s["hid_ready"], t + 1)
                    wait(pe, s["t_ready"], t - 1)
                    for c in range(K4):
                        ins = nc.tensor.transpose(p_t[par][:, c, :], hid[par][:, c * P:(c + 1) * P], const["identity"][:, :])
                    ins.then_inc(s["t_mm"], 1)

                def down(t, par, expert):
                    pe.wait_ge(s["t_ready"], t + 1)
                    wait(pe, s["y_ready"], t - 1)
                    for c in range(K4):
                        ins = nc.tensor.matmul(p_y[par][:, 0:D], hid_t[par][:, c, :], w2[:, bass.ds(expert * K4 + c, 1), :],
                                               start=(c == 0), stop=(c == K4 - 1))
                    ins.then_inc(s["y_mm"], 1)

                def expert_of(t):
                    return pe.value_load(keep["expert_i"][0:1, bass.ds(t, 1)], min_val=0, max_val=E - 1)

                def first(turn, t, par):
                    turn_x(0, 0, 0)
                    up(t, par, expert_of(t))
                    turn_x(0, 1, 1)
                    turn_hidden(t, par)

                def step(turn, t, par):
                    up(t, par, expert_of(t))
                    turn_x(turn + 1 if par else turn, t + 1, 1 - par)
                    down(t - 1, 1 - par, expert_of(t - 1))
                    turn_hidden(t, par)

                def end(turn, t, par):
                    up(t, par, expert_of(t))
                    down(t - 1, 1 - par, expert_of(t - 1))
                    turn_hidden(t, par)
                    down(t, par, expert_of(t))

                pe.wait_ge(keep["experts_in"], 32)
                moe_pipeline(first, step, end, plain_repeat(pe))


def add_up_and_end(nc, mem_all, dram, const, keep):
    DEPTH = 4
    TURNS = TILES // 2 // DEPTH
    with ExitStack() as stack:
        m = Memory(nc, stack, "en")
        y = [[m.sb(f"y{i}{k}", [P, 2, D]) for k in range(2)] for i in range(DEPTH)]
        out = [m.sb(f"out{i}", [P, 2, D]) for i in range(2)]
        stats, mv, var, rstd = ([m.sb(f"{n}{i}", shape) for i in range(2)] for n, shape in (
            ("stats", [P, 2, 6]), ("mv", [P, 2, 2]), ("var", [P, 2]), ("rstd", [P, 2])))
        sum_0, sum_1, var_ready, var_done, rstd_ready, out_ready, dve_step = (
            m.sem(n) for n in ("sum_0", "sum_1", "var_ready", "var_done", "rstd_ready", "out_ready", "dve_step"))
        y_in = [m.sem(f"y_in{i}") for i in range(DEPTH)]
        out_stored = [m.sem(f"out_stored{i}") for i in range(2)]
        resid = keep["resid"]

        def turns(step, repeat):
            for i in range(DEPTH):
                step(0, i, i)
            for turn in repeat(TURNS - 1):
                for i in range(DEPTH):
                    step(turn + 1, (turn + 1) * DEPTH + i, i)

        def plain_repeat(eng):
            def repeat(count):
                with eng.Fori(0, count) as j:
                    yield j
            return repeat

        with nc.Block() as block:

            @block.sync
            def _(sp):
                def load(turn, j, i):
                    wait(sp, out_ready, j - DEPTH + 1)
                    for k in range(2):
                        sp.dma_start(y[i][k][:, :, :], dram["results_of"][k][:, bass.ds(j * 2, 2), :]).then_inc(y_in[i], 16)

                turns(load, plain_repeat(sp))

            @block.scalar
            def _(act):
                def store(turn, j, i):
                    act.wait_ge(out_ready, j + 1)
                    act.dma_start(dram["out_group"][:, bass.ds(j * 2, 2), :], out[i % 2][:, :, :]).then_inc(out_stored[i % 2], 16)

                turns(store, plain_repeat(act))
                for i in range(2):
                    act.wait_ge(out_stored[i], TILES // 4 * 16)

            @block.gpsimd
            def _(pool):
                def root(j, par):
                    wait_apart(pool, var_ready, j + 1)
                    nc.gpsimd.tensor_scalar(var[par][:, :], mv[par][:, :, 1], EPS, None, ALU.add).then_inc(var_done, 1)
                    pool.wait_ge(var_done, j + 1)
                    nc.gpsimd.tensor_tensor(rstd[par][:, :], var[par][:, :], const["minus_half"][:, 0:2], ALU.pow)\
                      .then_inc(rstd_ready, 1)

                def step(turn, j, i):
                    pool.wait_ge(y_in[i], turn * 32 + 32)
                    nc.gpsimd.tensor_tensor(y[i][0][:, :, :], y[i][0][:, :, :], resid[:, bass.ds(j * 2, 2), :], ALU.add)\
                      .then_inc(sum_0, 1)
                    if not isinstance(j, int) or j > 0:
                        root(j - 1, (i - 1) % 2)

                turns(step, plain_repeat(pool))
                root(TILES // 2 - 1, 1)

            @block.vector
            def _(dve):
                V = nc.vector
                steps = Steps(dve, dve_step)

                def normalise(j, i):
                    dve.wait_ge(rstd_ready, j + 1)
                    wait(dve, out_stored[i % 2], (j - i) * 8 + i // 2 * 16)
                    for t in range(2):
                        ins = V.tensor_scalar(out[i % 2][:, t, :], y[i][0][:, t, :], mv[i % 2][:, t, 0:1],
                                              rstd[i % 2][:, t:t + 1], ALU.subtract, ALU.mult)
                        if t == 0:
                            steps.mark(ins)
                    ins.then_inc(out_ready, 1)

                def step(turn, j, i):
                    dve.wait_ge(sum_0, j + 1)
                    V.tensor_tensor(y[i][0][:, :, :], y[i][0][:, :, :], y[i][1][:, :, :], ALU.add).then_inc(sum_1, 1)
                    dve.wait_ge(sum_1, j + 1)
                    layer_norm_stats(steps, nc, y[i][0], stats[i % 2], mv[i % 2], var_ready)
                    if not isinstance(j, int) or j > 0:
                        normalise(j - 1, (i - 1) % DEPTH)

                turns(step, lambda count: steps.repeat(count, 4 * DEPTH))
                normalise(TILES // 2 - 1, DEPTH - 1)


def constants(nc, m, dram):
    const = {
        "identity": m.sb("identity", [P, P]),
        "head_mask": m.sb("head_mask", [P, 8]),
        "minus_half": m.sb("minus_half", [P, NI]),
    }
    step = m.sem("const_step")
    with nc.Block() as block:

        @block.gpsimd
        def _(pool):
            nc.gpsimd.memset(const["identity"][:, :], 0.0).then_inc(step, 1)
            nc.gpsimd.memset(const["head_mask"][:, :], 1.0).then_inc(step, 1)
            nc.gpsimd.memset(const["minus_half"][:, :], -0.5).then_inc(step, 1)
            pool.wait_ge(step, 3)
            nc.gpsimd.affine_select(out=const["identity"][:, :], in_=const["identity"][:, :], compare_op=ALU.not_equal,
                                    fill=1.0, base=0, pattern=[[-1, P]], channel_multiplier=1).then_inc(step, 1)
            nc.gpsimd.affine_select(out=const["head_mask"][:, :], in_=const["head_mask"][:, :], compare_op=ALU.is_ge,
                                    fill=0.0, base=0, pattern=[[-HD, 8]], channel_multiplier=1).then_inc(step, 1)
            pool.wait_ge(step, 5)
            nc.gpsimd.affine_select(out=const["head_mask"][:, :], in_=const["head_mask"][:, :], compare_op=ALU.is_ge,
                                    fill=0.0, base=HD - 1, pattern=[[HD, 8]], channel_multiplier=-1).then_inc(step, 1)
            pool.wait_ge(step, 6)
    return const


def decoder_kernel(nc, dram):
    with ExitStack() as stack:
        m = Memory(nc, stack, "all")
        def scratch(name, shape):
            return nc.dram_tensor(name, shape, F32, kind="Internal").ap()
        rows = "(t p) d -> p t d"
        dram = dict(dram)
        dram["x_rows"] = dram["x"].rearrange(rows, p=P)
        x2 = scratch("x2_rows", [TOKENS, D])
        dram["x2"] = x2.rearrange(rows, p=P)
        dram["x2_group"] = x2.rearrange("(p i) d -> p i d", p=P)
        dram["dispatched"] = scratch("dispatched", [E * SEGMENT, ROW])
        dram["results"] = scratch("results", [2 * TOKENS + 2 * P, D])
        dram["results_of"] = [dram["results"][k * TOKENS:(k + 1) * TOKENS, :].rearrange("(p i) d -> p i d", p=P)
                              for k in range(2)]
        dram["out_group"] = dram["out"].rearrange("(p i) d -> p i d", p=P)
        const = constants(nc, m, dram)
        keep = {"resid": m.sb("resid", [P, TILES, D]), "x2_in": m.sem("x2_in")}
        with ExitStack() as attention_stack:
            n = Memory(nc, attention_stack, "shared")
            kept = {"w_qkv": n.sb("w_qkv", [P, C, 3 * D]), "w_out": n.sb("w_out", [P, C, D]), "w_v": n.sb("w_v", [P, C, D]),
                    "b_out": n.sb("b_out", [P, D]), "b_v": n.sb("b_v", [P, D]), "qk": n.sb("qk", [P, C, B * CTX]),
                    "k_bias": n.sb("k_bias", [P, B * CTX]), "weights_in": n.sem("weights_in")}
            context_keys(nc, m, dram, const, kept)
            two_attentions(nc, m, dram, const, kept, keep)
        keep |= {
            "w1": m.sb("w1", [P, E * C, F]),
            "w2": m.sb("w2", [P, E * K4, D]),
            "ln2_w": m.sb("ln2_w", [P, C]),
            "ln2_b": m.sb("ln2_b", [P, C]),
            "expert_i": m.sb("expert_i", [P, MOE_TILES], I32),
            "expert_f": m.sb("expert_f", [P, MOE_TILES]),
            "first_i": m.sb("first_i", [P, MOE_TILES], I32),
            "experts_in": m.sem("experts_in"),
        }
        batch_axis_attention(nc, m, dram, const, keep)
        experts(nc, m, dram, const, keep)
        add_up_and_end(nc, m, dram, const, keep)


def kernel(x, ctx_1024, L0_attn_w_qkv, L0_attn_w_out, L0_attn_b_out, L0_xattn_Wq, L0_xattn_bq, L0_xattn_Wk, L0_xattn_bk,
           L0_xattn_Wv, L0_xattn_bv, L0_ffn_ln1_weight, L0_ffn_ln1_bias, L0_ffn_ln2_weight, L0_ffn_ln2_bias,
           L0_ffn_qkv_weight, L0_ffn_proj_weight, L0_ffn_router_weight, L0_ffn_moe_w1, L0_ffn_moe_w2):
    from concourse import bacc
    from concourse.bass_utils import run_bass_kernel_spmd

    def dense(a):
        return np.ascontiguousarray(a)

    def features_first(a):
        return dense(np.asarray(a).T.reshape(C, P, -1).transpose(1, 0, 2))

    def columns(a):
        return dense(np.asarray(a).reshape(C, P).T)

    x_rows = np.asarray(x).reshape(TOKENS, D)
    qk_rows = (H + KV) * HD
    arrays = {
        "x": dense(x_rows),
        "x_t": features_first(x_rows),
        "w_qkv": features_first(L0_attn_w_qkv),
        "w_out": features_first(L0_attn_w_out),
        "b_out": dense(L0_attn_b_out),
        "ctx_t": features_first(np.asarray(ctx_1024).reshape(-1, D)),
        "xw_q": dense(np.asarray(L0_xattn_Wq).reshape(C, P, D).transpose(1, 0, 2)),
        "xw_k": features_first(L0_xattn_Wk),
        "xw_v": features_first(L0_xattn_Wv),
        "xb_q": columns(L0_xattn_bq),
        "xb_k": columns(L0_xattn_bk),
        "xb_v": dense(L0_xattn_bv),
        "w_qk": features_first(np.asarray(L0_ffn_qkv_weight)[:qk_rows]),
        "w_v": features_first(np.asarray(L0_ffn_qkv_weight)[qk_rows:]),
        "w_proj": features_first(L0_ffn_proj_weight),
        "w_router": features_first(L0_ffn_router_weight),
        "moe_w1": dense(np.asarray(L0_ffn_moe_w1).reshape(E, C, P, F).transpose(2, 0, 1, 3)),
        "moe_w2": dense(np.asarray(L0_ffn_moe_w2).reshape(E, K4, P, D).transpose(2, 0, 1, 3)),
        "ln1_w": columns(L0_ffn_ln1_weight),
        "ln1_b": columns(L0_ffn_ln1_bias),
        "ln2_w": columns(L0_ffn_ln2_weight),
        "ln2_b": columns(L0_ffn_ln2_bias),
    }
    nc = bacc.Bacc("TRN2", target_bir_lowering=False, num_devices=1)
    dram = {
        name: nc.dram_tensor(f"in_{name}_dram", a.shape, mybir.dt.from_np(a.dtype), kind="ExternalInput").ap()
        for name, a in arrays.items()
    }
    dram["out"] = nc.dram_tensor("out_0_dram", (TOKENS, D), F32, kind="ExternalOutput").ap()
    decoder_kernel(nc, dram)
    r = run_bass_kernel_spmd(nc, [{f"in_{name}_dram": a for name, a in arrays.items()}], core_ids=[0])
    return r.results[0]["out_0_dram"].reshape(B, N, D)
```

```python
from contextlib import ExitStack

import numpy as np

import concourse.bass as bass
from concourse import mybir

F32 = mybir.dt.float32
F32R = mybir.dt.float32r
BF16 = mybir.dt.bfloat16
I32 = mybir.dt.int32
U32 = mybir.dt.uint32
ALU = mybir.AluOpType
ACT = mybir.ActivationFunctionType
AX = mybir.AxisListType.X

P = 128
B, N, D = 16, 256, 256
TOKENS = B * N
C = D // P
T = N // P
HD = 16
CTX = 77
H, KV = 16, 4
REP = H // KV
NI = 8
GROUPS = TOKENS // P // NI
TILES = TOKENS // P
E, F = 8, 512
K4 = F // P
SEGMENT = TOKENS + 2 * P
ROW = D + 5
MOE_TILES = 2 * TOKENS // P + E - 1
EPS = 1e-5
BIG = 3.4028234663852886e38


class Steps:

    def __init__(self, eng, sem):
        self.eng, self.sem, self.base, self.n = eng, sem, 0, 0

    def mark(self, ins):
        ins.then_inc(self.sem, 1)
        self.n += 1
        return self.base + self.n

    def need(self, value):
        self.eng.wait_ge(self.sem, value)

    def need_apart(self, value):
        wait_apart(self.eng, self.sem, value)

    def chain(self, ins):
        self.need(self.mark(ins))

    def repeat(self, count, per):
        entry = self.base + self.n
        with self.eng.Fori(0, count) as j:
            self.base, self.n = j * per + entry, 0
            yield j
            assert self.n == per, f"{self.n} steps a turn"
        self.base, self.n = entry + count * per, 0


def wait(eng, sem, value):
    if not isinstance(value, int) or value > 0:
        eng.wait_ge(sem, value)


def wait_apart(eng, sem, value):
    eng.wait_ge(sem, value)
    eng.nop(nofuse=True)


def bcast(ap, shape):
    return ap.to_broadcast(shape)


class Batch:

    def __init__(self, turn, par):
        self.turn, self.par, self.n = turn, par, turn * 2 + par

    def off(self, d):
        return Batch(self.turn + (self.par + d) // 2, (self.par + d) % 2)

    @property
    def there(self):
        return not isinstance(self.n, int) or 0 <= self.n < B


def upto(n):
    return min(n, B) if isinstance(n, int) else n


class Memory:
    def __init__(self, nc, stack, prefix):
        self.nc, self.stack, self.prefix = nc, stack, prefix

    def sb(self, name, shape, dt=F32):
        return self.stack.enter_context(self.nc.sbuf_tensor(f"{self.prefix}_{name}", shape, dt))

    def ps(self, name, shape):
        return self.stack.enter_context(self.nc.psum_tensor(f"{self.prefix}_{name}", shape, F32))

    def sem(self, name):
        return self.stack.enter_context(self.nc.semaphore(f"{self.prefix}_{name}"))


def split_products(nc, out, pairs, start=True, stop=True):
    for i, ((a_hi, a_lo), (b_hi, b_lo)) in enumerate(pairs):
        nc.tensor.matmul(out, a_hi, b_hi, start=(start and i == 0), stop=False)
        nc.tensor.matmul(out, a_hi, b_lo, start=False, stop=False)
        ins = nc.tensor.matmul(out, a_lo, b_hi, start=False, stop=(stop and i == len(pairs) - 1))
    return ins


def layer_norm_stats(steps, nc, rows, stats, mv, to_pool):
    k = rows.shape[1]
    for t in range(k):
        last = steps.mark(nc.vector.bn_stats(stats[:, t, :], rows[:, t, :]))
    steps.need_apart(last)
    for t in range(k):
        ins = nc.vector.bn_aggr(mv[:, t, :], stats[:, t, :])
        if t < k - 1:
            steps.mark(ins)
    ins.then_inc(to_pool, 1)


def context_keys(nc, mem_all, dram, const, kept):
    KEYS = B * CTX
    PIECES = 4
    CH = KEYS // PIECES
    SPLIT_AFTER = PIECES * C + 4
    qk, k_bias = kept["qk"], kept["k_bias"]
    with ExitStack() as stack:
        m = Memory(nc, stack, "ck")
        w_q, w_k = m.sb("w_q", [P, C, D]), m.sb("w_k", [P, C, D])
        whole = {name: m.sb(name, list(kept[name + "_hi"].shape)) for name in ("w_qkv", "w_out")}
        b_q, b_k = m.sb("b_q", [P, C]), m.sb("b_k", [P, C])
        b_q_cols = m.sb("b_q_cols", [P, C, P])
        ctx_t = m.sb("ctx_t", [P, C, KEYS])
        k_t = m.sb("k_t", [P, C, KEYS])
        p_set = [m.ps(f"p_set{i}", [P, 512]) for i in range(4)]
        wk_in, wq_in, biases_in = m.sem("wk_in"), m.sem("wq_in"), m.sem("biases_in")
        ctx_in = [m.sem(f"ctx_in{i}") for i in range(PIECES)]
        bq_cols, piece_mm = m.sem("bq_cols"), m.sem("piece_mm")
        weights_high, weights_split = m.sem("weights_high"), m.sem("weights_split")
        act_read, dve_read = m.sem("act_read"), m.sem("dve_read")

        w_parts = {SPLIT_AFTER + 2 * c: ("w_qkv", slice(c, c + 1)) for c in range(C)} | {SPLIT_AFTER + 2 * C: ("w_out", slice(0, C))}
        part_in = [m.sem(f"part_in{i}") for i in range(C + 1)]

        pieces = [("k", o, ch) for ch in range(PIECES) for o in range(C)]
        for ch in range(PIECES):
            pieces += [("qk", o, ch) for o in range(C)] + [("bias", 0, ch)]

        def wait_read(eng, n):
            eng.wait_ge(dve_read if n % 2 else act_read, n // 2 + 1)

        with nc.Block() as block:

            @block.sync
            def _(sp):
                sp.dma_start(w_k[:, :, :], dram["xw_k"]).then_inc(wk_in, 16)
                for ch in range(PIECES):
                    cols = slice(ch * CH, (ch + 1) * CH)
                    sp.dma_start(ctx_t[:, :, cols], dram["ctx_t"][:, :, cols]).then_inc(ctx_in[ch], 16)
                sp.dma_start(w_q[:, :, :], dram["xw_q"]).then_inc(wq_in, 16)
                for c in range(C):
                    sp.dma_start(whole["w_qkv"][:, c, :], dram["w_qkv"][:, c, :]).then_inc(part_in[c], 16)
                sp.dma_start(whole["w_out"][:, :, :], dram["w_out"]).then_inc(part_in[C], 16)
                for i in range(2):
                    sp.dma_start(kept["x_t"][i][:, :, :], dram["x_t"][:, :, i * N:(i + 1) * N]).then_inc(kept["x_t_in"][i], 16)
                sp.dma_start(kept["w_v"][:, :, :], dram["xw_v"]).then_inc(kept["weights_in"], 16)

            @block.scalar
            def _(act):
                act.dma_start(b_k[:, :], dram["xb_k"]).then_inc(biases_in, 16)
                act.dma_start(b_q[:, :], dram["xb_q"]).then_inc(biases_in, 16)
                act.dma_start(kept["b_out"][:, :], dram["b_out"].partition_broadcast(P)).then_inc(kept["weights_in"], 16)
                act.dma_start(kept["b_v"][:, :], dram["xb_v"].partition_broadcast(P)).then_inc(kept["weights_in"], 16)
                act.wait_ge(biases_in, 32)
                for n in range(0, len(pieces), 2):
                    kind, o, ch = pieces[n]
                    cols = slice(ch * CH, (ch + 1) * CH)
                    act.wait_ge(piece_mm, n + 1)
                    src = p_set[n % 4][:, 0:CH]
                    if kind == "k":
                        ins = nc.scalar.activation(k_t[:, o, cols], src, ACT.Identity, bias=b_k[:, o:o + 1])
                    else:
                        ins = nc.scalar.activation(qk[:, o, cols] if kind == "qk" else k_bias[:, cols], src, ACT.Copy)
                    ins.then_inc(act_read, 1)
                    if n in w_parts:
                        name, cs = w_parts[n]
                        act.wait_ge(part_in[(n - SPLIT_AFTER) // 2], 16)
                        nc.scalar.activation(kept[name + "_hi"][:, cs, :], whole[name][:, cs, :], ACT.Copy)\
                            .then_inc(weights_high, 1)

            @block.vector
            def _(dve):
                dve.wait_ge(biases_in, 32)
                nc.vector.tensor_copy(b_q_cols[:, :, :], bcast(b_q[:, :].unsqueeze(2), [P, C, P])).then_inc(bq_cols, 1)
                for n in range(1, len(pieces), 2):
                    kind, o, ch = pieces[n]
                    cols = slice(ch * CH, (ch + 1) * CH)
                    dve.wait_ge(piece_mm, n + 1)
                    src = p_set[n % 4][:, 0:CH]
                    if kind == "k":
                        ins = nc.vector.tensor_scalar(k_t[:, o, cols], src, b_k[:, o:o + 1], None, ALU.add)
                    else:
                        ins = nc.vector.tensor_copy(qk[:, o, cols] if kind == "qk" else k_bias[:, cols], src)
                    ins.then_inc(dve_read, 1)
                    if n - 1 in w_parts:
                        name, cs = w_parts[n - 1]
                        dve.wait_ge(weights_high, (n - 1 - SPLIT_AFTER) // 2 + 1)
                        nc.vector.tensor_tensor(kept[name + "_lo"][:, cs, :], whole[name][:, cs, :],
                                                kept[name + "_hi"][:, cs, :].bitcast(F32), ALU.subtract).then_inc(weights_split, 1)
                dve.wait_ge(weights_split, C + 1)

            @block.tensor
            def _(pe):
                pe.wait_ge(wk_in, 16)
                for n, (kind, o, ch) in enumerate(pieces):
                    cols = slice(ch * CH, (ch + 1) * CH)
                    if n >= 4:
                        wait_read(pe, n - 4)
                    if kind == "k":
                        pe.wait_ge(ctx_in[ch], 16)
                        pairs = [(w_k[:, c, o * P:(o + 1) * P], ctx_t[:, c, cols]) for c in range(C)]
                    else:
                        if kind == "qk" and o == 0:
                            pe.wait_ge(wq_in, 16)
                            pe.wait_ge(bq_cols, 1)
                            for c in range(C):
                                wait_read(pe, ch * C + c)
                        pairs = [(w_q[:, c, o * P:(o + 1) * P] if kind == "qk" else b_q_cols[:, c, :], k_t[:, c, cols])
                                 for c in range(C)]
                    for i, (lhs, rhs) in enumerate(pairs):
                        ins = nc.tensor.matmul(p_set[n % 4][:, 0:CH], lhs, rhs, start=(i == 0), stop=(i == C - 1))
                    ins.then_inc(piece_mm, 1)
                wait_read(pe, len(pieces) - 1)
                wait_read(pe, len(pieces) - 2)


def two_attentions(nc, mem_all, dram, const, kept, keep):
    with ExitStack() as stack:
        m = Memory(nc, stack, "at")
        w_qkv_hi, w_out_hi, b_out, w_v, b_v = (kept[n] for n in ("w_qkv_hi", "w_out_hi", "b_out", "w_v", "b_v"))
        w_qkv_lo, w_out_lo = kept["w_qkv_lo"], kept["w_out_lo"]
        qk, k_bias, weights_in = kept["qk"], kept["k_bias"], kept["weights_in"]
        resid, x2_in = keep["resid"], keep["x2_in"]
        x_t = kept["x_t"]
        x_hi = [m.sb(f"x_hi{i}", [P, C, N], F32R) for i in range(2)]
        x_lo = [m.sb(f"x_lo{i}", [P, C, N], F32R) for i in range(2)]
        x_tok = [m.sb(f"x_tok{i}", [P, T, D]) for i in range(2)]
        e_q, r_q = m.sb("e_q", [P, C * N]), m.sb("r_q", [P, C * N])
        e_k, r_k = m.sb("e_k", [P, T, D]), m.sb("r_k", [P, T, D])
        q = [m.sb(f"q{i}", [P, C, N]) for i in range(2)]
        k = [m.sb(f"k{i}", [P, T, D]) for i in range(2)]
        v = [m.sb(f"v{i}", [P, T, C, P + 1]) for i in range(2)]
        kv_sum = m.sb("kv_sum", [P, C, P + P // HD])
        den = m.sb("den", [P, T, H])
        rec = m.sb("rec", [P, T, H])
        att = m.sb("att", [P, T, D])
        att_hi, att_lo = m.sb("att_hi", [P, C, N], F32R), m.sb("att_lo", [P, C, N], F32R)
        x1 = [m.sb(f"x1_{i}", [P, T, D]) for i in range(2)]
        x1_bv = [m.sb(f"x1_bv{i}", [P, T, D]) for i in range(2)]
        ctx_b = [m.sb(f"ctx_b{i}", [P, C, CTX]) for i in range(2)]
        x1_t = m.sb("x1_t", [P, C, N])
        xv = m.sb("xv", [CTX, D])
        sc = m.sb("sc", [P, T, CTX])
        top = m.sb("top", [P, T])
        prob = m.sb("prob", [P, T, CTX])
        total = [m.sb(f"total{i}", [P, T]) for i in range(2)]
        total_rec = m.sb("total_rec", [P, T])
        prob_t = m.sb("prob_t", [CTX, T, P])
        x2 = [m.sb(f"x2_{i}", [P, T, D]) for i in range(2)]
        s = [m.sb(f"s{i}", [P, T, D]) for i in range(2)]
        stats = [m.sb(f"stats{i}", [P, T, 6]) for i in range(2)]
        mv = [m.sb(f"mv{i}", [P, T, 2]) for i in range(2)]
        var = [m.sb(f"var{i}", [P, T]) for i in range(2)]
        scaled_mean, shift = m.sb("scaled_mean", [P, T]), m.sb("shift", [P, T])
        rstd = [m.sb(f"rstd{i}", [P, T]) for i in range(2)]

        p_sum = p_x1 = m.ps("p_sum_x1", [P, C, N])
        p_q = p_s = m.ps("p_q_s", [P, C, N])
        p_kv = [m.ps(f"p_kv{t}", [P, 2 * D]) for t in range(T)]
        p_num = [m.ps("p_num_v", [P, 2 * D]), m.ps("p_num_p", [P, 2 * D])]
        p_v, p_p = p_num
        p_out = p_att = m.ps("p_out_att", [P, 2, D])
        p_o = m.ps("p_o", [P, T, D])

        x_t_in = kept["x_t_in"]
        x_tok_in, ctx_in, x2_out = ([m.sem(f"{n}{i}") for i in range(2)] for n in ("x_tok_in", "ctx_in", "x2_out"))
        s_ready, var_ready, var_done, rstd_ready = (
            [m.sem(f"{n}{i}") for i in range(2)] for n in ("s_ready", "var_ready", "var_done", "rstd_ready"))
        (ones_set, q_mm, kv_mm, sum_mm, num_mm, out_mm, q_exp, kv_act, att_mm, q_ready, k_ready, diag_ready, att_ready, att_high, att_split, x_high,
         x_split,
         bias_added, x1_ready, x1_bv_ready, x1_t_mm, s_mm, p_t_mm, v_mm, o_mm, x1_t_ready, sc_ready, exp_done,
         prob_t_ready, xv_ready, x2_ready, mean_scaled, shift_ready, dve_step) = (m.sem(n) for n in (
             "ones_set", "q_mm", "kv_mm", "sum_mm", "num_mm", "out_mm", "q_exp", "kv_act", "att_mm", "q_ready", "k_ready",
             "diag_ready", "att_ready", "att_high", "att_split", "x_high", "x_split", "bias_added", "x1_ready", "x1_bv_ready", "x1_t_mm", "s_mm", "p_t_mm", "v_mm",
             "o_mm", "x1_t_ready", "sc_ready", "exp_done", "prob_t_ready", "xv_ready", "x2_ready", "mean_scaled", "shift_ready", "dve_step"))

        def pipeline(step, repeat):
            for b in range(-1, 4):
                step(Batch(b // 2, b % 2))
            for j in repeat(B // 2 - 3):
                step(Batch(j + 2, 0))
                step(Batch(j + 2, 1))
            for b in range(B - 2, B + 3):
                step(Batch(b // 2, b % 2))

        def plain_repeat(eng):
            def repeat(count):
                with eng.Fori(0, count) as j:
                    yield j
            return repeat

        with nc.Block() as block:

            @block.sync
            def _(sp):
                def load_x_t(k):
                    wait(sp, x_split, k.n - 1)
                    sp.dma_start(x_t[k.par][:, :, :], dram["x_t"][:, :, bass.ds(k.n * N, N)]).then_inc(x_t_in[k.par], 16)

                def load(k):
                    if k.off(2).there:
                        load_x_t(k.off(2))
                    wait(sp, s_ready[0], k.n - 1)
                    sp.dma_start(x_tok[k.par][:, :, :], dram["x_rows"][:, bass.ds(k.n * T, T), :])\
                      .then_inc(x_tok_in[k.par], 16)
                    wait(sp, v_mm, k.n - 1)
                    sp.dma_start(ctx_b[k.par][:, :, :], dram["ctx_t"][:, :, bass.ds(k.n * CTX, CTX)])\
                      .then_inc(ctx_in[k.par], 16)

                load(Batch(0, 0))
                load(Batch(0, 1))
                with sp.Fori(0, B // 2 - 2) as j:
                    load(Batch(j + 1, 0))
                    load(Batch(j + 1, 1))
                load(Batch(B // 2 - 1, 0))
                load(Batch(B // 2 - 1, 1))
                for first, end in ((0, B - 2), (B - 2, B - 1), (B - 1, B)):
                    for par in range(2):
                        sp.wait_ge(x2_out[par], (end + 1 - par) // 2 * 16)
                    rows = slice(first * P // B, end * P // B)
                    sp.dma_start(resid[rows, :, :], dram["x2_group"][rows, :, :]).then_inc(x2_in, 16)

            @block.gpsimd
            def _(pool):
                for i in range(2):
                    ins = nc.gpsimd.memset(v[i][:, :, :, P:P + 1], 1.0)
                ins.then_inc(ones_set, 1)
                pool.wait_ge(weights_in, 48)

                def root(which, turns):
                    wait_apart(pool, var_ready[which], turns)
                    nc.gpsimd.tensor_scalar(var[which][:, :], mv[which][:, :, 1], EPS, None, ALU.add).then_inc(var_done[which], 1)
                    pool.wait_ge(var_done[which], turns)
                    nc.gpsimd.tensor_tensor(rstd[which][:, :], var[which][:, :], const["minus_half"][:, 0:T], ALU.pow)\
                      .then_inc(rstd_ready[which], 1)

                def x_low(k):
                    pool.wait_ge(x_high, k.n + 1)
                    nc.gpsimd.tensor_tensor(x_lo[k.par][:, :, :], x_t[k.par][:, :, :], x_hi[k.par][:, :, :].bitcast(F32),
                                            ALU.subtract).then_inc(x_split, 1)

                def step(k):
                    ahead, nxt, pre, old = k.off(2), k.off(1), k.off(-1), k.off(-2)
                    if pre.there:
                        root(0, pre.n + 1)
                        pool.wait_ge(x1_ready, pre.n + 1)
                        wait(pool, s_ready[1], pre.n - 1)
                        nc.gpsimd.tensor_tensor(x1_bv[pre.par][:, :, :], x1[pre.par][:, :, :],
                                                bcast(b_v[:, :].unsqueeze(1), [P, T, D]), ALU.add).then_inc(x1_bv_ready, 1)
                    if nxt.there:
                        pool.wait_ge(x_tok_in[nxt.par], nxt.turn * 16 + 16)
                        nc.gpsimd.tensor_tensor(x_tok[nxt.par][:, :, :], x_tok[nxt.par][:, :, :],
                                                bcast(b_out[:, :].unsqueeze(1), [P, T, D]), ALU.add).then_inc(bias_added, 1)
                    if ahead.there:
                        x_low(ahead)
                    if old.there:
                        root(1, old.n + 1)
                        pool.wait_ge(rstd_ready[1], old.n + 1)
                        nc.gpsimd.tensor_tensor(scaled_mean[:, :], mv[1][:, :, 0], rstd[1][:, :], ALU.mult).then_inc(mean_scaled, 1)
                        wait_apart(pool, mean_scaled, old.n + 1)
                        nc.gpsimd.tensor_scalar(shift[:, :], scaled_mean[:, :], -1.0, None, ALU.mult).then_inc(shift_ready, 1)

                x_low(Batch(0, 0))
                pipeline(step, plain_repeat(pool))

            @block.scalar
            def _(act):
                def q_features(k):
                    act.wait_ge(q_mm, k.n + 1)
                    wait(act, q_ready, k.n)
                    nc.scalar.activation(e_q[:, :], p_q[:, :, :].rearrange("p c n -> p (c n)"), ACT.Exp)
                    nc.scalar.activation(r_q[:, :], p_q[:, :, :].rearrange("p c n -> p (c n)"), ACT.Relu).then_inc(q_exp, 1)

                def kv_features(k, t):
                    act.wait_ge(kv_mm, k.n * T + t + 1)
                    if t == 0:
                        wait(act, k_ready, k.n)
                        wait(act, sum_mm, k.n - 1)
                    nc.scalar.activation(e_k[:, t, :], p_kv[t][:, 0:D], ACT.Exp)
                    nc.scalar.activation(r_k[:, t, :], p_kv[t][:, 0:D], ACT.Relu)
                    nc.scalar.activation(v[k.par][:, t, :, 0:P], p_kv[t][:, D:2 * D].rearrange("p (c e) -> p c e", c=C),
                                         ACT.Copy).then_inc(kv_act, 1)

                def high_x(k):
                    act.wait_ge(x_t_in[k.par], k.turn * 16 + 16)
                    wait(act, kv_mm, (k.n - 1) * T)
                    nc.scalar.activation(x_hi[k.par][:, :, :], x_t[k.par][:, :, :], ACT.Copy).then_inc(x_high, 1)

                def high_att(k):
                    act.wait_ge(att_mm, k.n + 1)
                    wait(act, out_mm, k.n)
                    nc.scalar.activation(att_hi[:, :, :], p_att[:, :, :], ACT.Copy).then_inc(att_high, 1)

                def x1_t_copy(k):
                    act.wait_ge(x1_t_mm, k.n + 1)
                    wait(act, s_mm, k.n)
                    nc.scalar.activation(x1_t[:, :, :], p_x1[:, :, :], ACT.Copy).then_inc(x1_t_ready, 1)

                def exponentials(k):
                    act.wait_ge(sc_ready, k.n + 1)
                    wait(act, p_t_mm, k.n)
                    for t in range(T):
                        nc.scalar.activation(prob[:, t, :], sc[:, t, :], ACT.Exp, bias=top[:, t:t + 1],
                                             accum_out=total[k.par][:, t:t + 1]).then_inc(exp_done, 1)

                def prob_t_copy(k):
                    act.wait_ge(p_t_mm, k.n + 1)
                    wait(act, o_mm, k.n)
                    nc.scalar.activation(prob_t[:, :, :], p_p[0:CTX, 0:T * P].rearrange("p (t n) -> p t n", t=T),
                                         ACT.Copy).then_inc(prob_t_ready, 1)

                def xv_copy(k):
                    act.wait_ge(v_mm, k.n + 1)
                    nc.scalar.activation(xv[:, :], p_v[0:CTX, 0:D], ACT.Copy).then_inc(xv_ready, 1)

                def normalise_and_store(k):
                    wait(act, x2_out[k.par], k.turn * 16)
                    act.wait_ge(shift_ready, k.n + 1)
                    for t in range(T):
                        ins = nc.scalar.activation(x2[k.par][:, t, :], s[1][:, t, :], ACT.Identity,
                                                   bias=shift[:, t:t + 1], scale=rstd[1][:, t:t + 1])
                    ins.then_inc(x2_ready, 1)
                    act.wait_ge(x2_ready, k.n + 1)
                    act.dma_start(dram["x2"][:, bass.ds(k.n * T, T), :], x2[k.par][:, :, :]).then_inc(x2_out[k.par], 16)

                def step(k):
                    ahead, nxt, pre, old, older = k.off(2), k.off(1), k.off(-1), k.off(-2), k.off(-3)
                    if old.there:
                        prob_t_copy(old)
                        xv_copy(old)
                    if older.there:
                        normalise_and_store(older)
                    if nxt.there:
                        q_features(nxt)
                    if pre.there:
                        x1_t_copy(pre)
                    if nxt.there:
                        kv_features(nxt, 0)
                    if k.there:
                        high_att(k)
                    if ahead.there:
                        high_x(ahead)
                    if pre.there:
                        exponentials(pre)
                    if nxt.there:
                        kv_features(nxt, 1)

                high_x(Batch(0, 0))
                pipeline(step, plain_repeat(act))
                for i in range(2):
                    act.wait_ge(x2_out[i], 16 * B // 2)

            @block.vector
            def _(dve):
                steps = Steps(dve, dve_step)

                def q_combine(k):
                    dve.wait_ge(q_exp, k.n + 1)
                    wait(dve, num_mm, k.n - 1)
                    nc.vector.scalar_tensor_tensor(q[k.par][:, :, :].rearrange("p c n -> p (c n)"), e_q[:, :], 1.0, r_q[:, :],
                                                   ALU.min, ALU.add).then_inc(q_ready, 1)

                def k_combine(n):
                    dve.wait_ge(kv_act, n.n * T + T)
                    wait(dve, sum_mm, n.n - 1)
                    nc.vector.scalar_tensor_tensor(k[n.par][:, :, :], e_k[:, :, :], 1.0, r_k[:, :, :],
                                                   ALU.min, ALU.add).then_inc(k_ready, 1)

                def diagonal(n):
                    dve.wait_ge(sum_mm, n.n + 1)
                    wait(dve, num_mm, n.n)
                    blocks = bcast(const["head_mask"][:, :].unsqueeze(2), [P, 8, HD])
                    for c in range(C):
                        steps.mark(nc.vector.tensor_tensor(kv_sum[:, c, 0:P].rearrange("p (h d) -> p h d", d=HD),
                                                           p_sum[:, c, 0:P].rearrange("p (h d) -> p h d", d=HD),
                                                           blocks, ALU.mult))
                    for c in range(C):
                        ins = nc.vector.tensor_scalar(kv_sum[:, c, P:], const["head_mask"][:, :], p_sum[:, c, P:P + 1],
                                                      None, ALU.mult)
                    ins.then_inc(diag_ready, 1)

                def divide(n):
                    dve.wait_ge(num_mm, n.n + 1)
                    products = [p_num[t][:, 0:C * (P + P // HD)].rearrange("p (c e) -> p c e", c=C) for t in range(T)]
                    for t in range(T):
                        last = steps.mark(nc.vector.tensor_scalar(den[:, t, :].rearrange("p (c h) -> p c h", c=C),
                                                                  products[t][:, :, P:], 1e-6, None, ALU.add))
                    steps.need(last)
                    steps.chain(nc.vector.reciprocal(rec[:, :, :], den[:, :, :]))
                    wait(dve, att_mm, n.n)
                    for t in range(T):
                        for c in range(C):
                            ins = nc.vector.tensor_tensor(
                                att[:, t, c * P:(c + 1) * P].rearrange("p (h d) -> p h d", d=HD),
                                products[t][:, c, 0:P].rearrange("p (h d) -> p h d", d=HD),
                                bcast(rec[:, t, c * 8:(c + 1) * 8].unsqueeze(2), [P, 8, HD]), ALU.mult)
                            if (t, c) != (T - 1, C - 1):
                                steps.mark(ins)
                    ins.then_inc(att_ready, 1)

                def low_att(n):
                    dve.wait_ge(att_high, n.n + 1)
                    nc.vector.tensor_tensor(att_lo[:, :, :], p_att[:, :, :], att_hi[:, :, :].bitcast(F32), ALU.subtract)\
                        .then_inc(att_split, 1)

                def sum_1(n):
                    dve.wait_ge(out_mm, n.n + 1)
                    dve.wait_ge(bias_added, n.n + 1)
                    nc.vector.tensor_tensor(s[0][:, :, :], p_out[:, :, :], x_tok[n.par][:, :, :], ALU.add)\
                      .then_inc(s_ready[0], 1)
                    dve.wait_ge(s_ready[0], n.n + 1)
                    layer_norm_stats(steps, nc, s[0], stats[0], mv[0], var_ready[0])

                def sum_2(n):
                    dve.wait_ge(exp_done, n.n * T + T)
                    steps.chain(nc.vector.reciprocal(total_rec[:, :], total[n.par][:, :]))
                    dve.wait_ge(o_mm, n.n + 1)
                    dve.wait_ge(x1_bv_ready, n.n + 1)
                    wait(dve, x2_ready, n.n)
                    for t in range(T):
                        ins = nc.vector.scalar_tensor_tensor(s[1][:, t, :], p_o[:, t, :], total_rec[:, t:t + 1],
                                                             x1_bv[n.par][:, t, :], ALU.mult, ALU.add)
                        if t < T - 1:
                            steps.mark(ins)
                    ins.then_inc(s_ready[1], 1)

                def moments_2(n):
                    dve.wait_ge(s_ready[1], n.n + 1)
                    layer_norm_stats(steps, nc, s[1], stats[1], mv[1], var_ready[1])

                def normalise_1(n):
                    dve.wait_ge(rstd_ready[0], n.n + 1)
                    wait(dve, x1_t_mm, n.n - 1)
                    wait(dve, x1_bv_ready, n.n - 1)
                    for t in range(T):
                        ins = nc.vector.tensor_scalar(x1[n.par][:, t, :], s[0][:, t, :], mv[0][:, t, 0:1],
                                                      rstd[0][:, t:t + 1], ALU.subtract, ALU.mult)
                        if t < T - 1:
                            steps.mark(ins)
                    ins.then_inc(x1_ready, 1)

                def scores(n):
                    dve.wait_ge(s_mm, n.n + 1)
                    wait(dve, exp_done, n.n * T)
                    steps.chain(nc.vector.tensor_tensor(
                        sc[:, :, :], p_s[:, :, 0:CTX],
                        bcast(k_bias[:, bass.ds(n.n * CTX, CTX)].unsqueeze(1), [P, T, CTX]), ALU.add))
                    steps.chain(nc.vector.tensor_reduce(top[:, :], sc[:, :, :], AX, ALU.max))
                    nc.vector.tensor_scalar(top[:, :], top[:, :], -1.0, None, ALU.mult).then_inc(sc_ready, 1)

                def step(n):
                    nxt, pre, old = n.off(1), n.off(-1), n.off(-2)
                    if pre.there:
                        sum_1(pre)
                    if n.there:
                        diagonal(n)
                    if pre.there:
                        normalise_1(pre)
                    if nxt.there:
                        q_combine(nxt)
                    if n.there:
                        divide(n)
                    if old.there:
                        sum_2(old)
                    if pre.there:
                        scores(pre)
                    if n.there:
                        low_att(n)
                    if old.there:
                        moments_2(old)
                    if nxt.there:
                        k_combine(nxt)

                pipeline(step, lambda count: steps.repeat(count, 2 * 19))

            @block.tensor
            def _(pe):
                def project_q(n):
                    pe.wait_ge(x_split, n.n + 1)
                    wait(pe, q_exp, n.n)
                    wait(pe, sc_ready, n.n - 2)
                    for o in range(C):
                        cols = slice(o * P, (o + 1) * P)
                        ins = split_products(nc, p_q[:, o, :], [
                            ((w_qkv_hi[:, c, cols], w_qkv_lo[:, c, cols]), (x_hi[n.par][:, c, :], x_lo[n.par][:, c, :]))
                            for c in range(C)])
                    ins.then_inc(q_mm, 1)

                def project_kv(n, t):
                    wait(pe, kv_act, (n.n - 1) * T + t + 1)
                    rows = slice(t * P, (t + 1) * P)
                    split_products(nc, p_kv[t][:, :], [
                        ((x_hi[n.par][:, c, rows], x_lo[n.par][:, c, rows]), (w_qkv_hi[:, c, D:], w_qkv_lo[:, c, D:]))
                        for c in range(C)]).then_inc(kv_mm, 1)

                def sum_kv(n):
                    pe.wait_ge(k_ready, n.n + 1)
                    pe.wait_ge(kv_act, n.n * T + T)
                    wait(pe, diag_ready, n.n)
                    wait(pe, x1_t_ready, n.n - 1)
                    for c in range(C):
                        for t in range(T):
                            ins = nc.tensor.matmul(p_sum[:, c, 0:P + 1], k[n.par][:, t, c * P:(c + 1) * P],
                                                   v[n.par][:, t, c, :], start=(t == 0), stop=(t == T - 1))
                    ins.then_inc(sum_mm, 1)

                def numerators(n):
                    pe.wait_ge(diag_ready, n.n + 1)
                    pe.wait_ge(q_ready, n.n + 1)
                    wait(pe, att_ready, n.n)
                    wait(pe, xv_ready, n.n - 1)
                    wait(pe, prob_t_ready, n.n - 1)
                    for t in range(T):
                        for c in range(C):
                            ins = nc.tensor.matmul(p_num[t][:, c * (P + P // HD):(c + 1) * (P + P // HD)],
                                                   q[n.par][:, c, t * P:(t + 1) * P], kv_sum[:, c, :], start=True, stop=True)
                    ins.then_inc(num_mm, 1)

                def turn_att(n):
                    pe.wait_ge(att_ready, n.n + 1)
                    wait(pe, s_ready[0], n.n)
                    for t in range(T):
                        for c in range(C):
                            ins = nc.tensor.transpose(p_att[:, c, t * P:(t + 1) * P], att[:, t, c * P:(c + 1) * P],
                                                      const["identity"][:, :])
                    ins.then_inc(att_mm, 1)

                def project_out(n):
                    pe.wait_ge(att_split, n.n + 1)
                    for t in range(T):
                        rows = slice(t * P, (t + 1) * P)
                        ins = split_products(nc, p_out[:, t, :], [
                            ((att_hi[:, c, rows], att_lo[:, c, rows]), (w_out_hi[:, c, :], w_out_lo[:, c, :]))
                            for c in range(C)])
                    ins.then_inc(out_mm, 1)

                def turn_x1(n):
                    pe.wait_ge(x1_ready, n.n + 1)
                    pe.wait_ge(diag_ready, upto(n.n + 2))
                    for t in range(T):
                        for c in range(C):
                            ins = nc.tensor.transpose(p_x1[:, c, t * P:(t + 1) * P], x1[n.par][:, t, c * P:(c + 1) * P],
                                                      const["identity"][:, :])
                    ins.then_inc(x1_t_mm, 1)

                def scores(n):
                    pe.wait_ge(x1_t_ready, n.n + 1)
                    pe.wait_ge(q_exp, upto(n.n + 3))
                    wait(pe, sc_ready, n.n)
                    for t in range(T):
                        for c in range(C):
                            ins = nc.tensor.matmul(p_s[:, t, 0:CTX], x1_t[:, c, t * P:(t + 1) * P],
                                                   qk[:, c, bass.ds(n.n * CTX, CTX)], start=(c == 0), stop=(c == C - 1))
                    ins.then_inc(s_mm, 1)

                def turn_prob(n):
                    pe.wait_ge(exp_done, n.n * T + T)
                    pe.wait_ge(att_ready, upto(n.n + 2))
                    wait(pe, prob_t_ready, n.n)
                    for t in range(T):
                        ins = nc.tensor.transpose(p_p[0:CTX, t * P:(t + 1) * P], prob[:, t, :], const["identity"][:, :])
                    ins.then_inc(p_t_mm, 1)

                def project_v(n):
                    pe.wait_ge(ctx_in[n.par], n.turn * 16 + 16)
                    pe.wait_ge(att_ready, upto(n.n + 2))
                    wait(pe, xv_ready, n.n)
                    for c in range(C):
                        ins = nc.tensor.matmul(p_v[0:CTX, 0:D], ctx_b[n.par][:, c, :], w_v[:, c, :],
                                               start=(c == 0), stop=(c == C - 1))
                    ins.then_inc(v_mm, 1)

                def outputs(n):
                    pe.wait_ge(prob_t_ready, n.n + 1)
                    pe.wait_ge(xv_ready, n.n + 1)
                    wait(pe, s_ready[1], n.n)
                    for t in range(T):
                        ins = nc.tensor.matmul(p_o[:, t, :], prob_t[:, t, :], xv[:, :], start=True, stop=True)
                    ins.then_inc(o_mm, 1)

                def step(n):
                    nxt, pre, old = n.off(1), n.off(-1), n.off(-2)
                    if n.there:
                        sum_kv(n)
                    if nxt.there:
                        project_q(nxt)
                    if old.there:
                        outputs(old)
                    if n.there:
                        numerators(n)
                    if pre.there:
                        turn_x1(pre)
                    if nxt.there:
                        project_kv(nxt, 0)
                    if pre.there:
                        scores(pre)
                    if n.there:
                        turn_att(n)
                    if nxt.there:
                        project_kv(nxt, 1)
                    if pre.there:
                        project_v(pre)
                    if n.there:
                        project_out(n)
                    if pre.there:
                        turn_prob(pre)

                pe.wait_ge(weights_in, 48)
                pe.wait_ge(ones_set, 1)
                pipeline(step, plain_repeat(pe))


class Ring:

    def __init__(self, m, name, banks, body, ahead):
        self.banks = [m.ps(f"{name}{i}", [P, 512]) for i in range(banks)]
        self.full = [m.sem(f"{name}_full{i}") for i in range(banks)]
        self.free = [m.sem(f"{name}_free{i}") for i in range(banks)]
        before = [what for what in body if what[0] in ahead]
        after = [what for what in body if what[0] not in ahead]
        assert len(body) % banks == 0
        self.first = {what: i for i, what in enumerate(before)}
        self.at = {what: len(before) + i for i, what in enumerate(body)}
        self.last = {what: len(before) + (GROUPS - 1) * len(body) + i for i, what in enumerate(after)}
        self.ahead, self.per = ahead, len(body) // banks

    def open(self, eng):
        for sem in self.free:
            eng.sem_inc(sem, 1)

    def turn(self, g, what):
        count = len(self.banks)
        if what[0] in self.ahead:
            if isinstance(g, int) and g == 0:
                return self.first[what] % count, self.first[what] // count
            return self.at[what] % count, (g - 1) * self.per + self.at[what] // count
        if isinstance(g, int) and g == GROUPS - 1:
            return self.last[what] % count, self.last[what] // count
        return self.at[what] % count, g * self.per + self.at[what] // count

    def fill(self, pe, g, what):
        bank, turn = self.turn(g, what)
        pe.wait_ge(self.free[bank], turn + 1)
        return self.banks[bank], self.full[bank]

    def read(self, eng, g, what):
        self.wait_full(eng, g, what)
        bank, _ = self.turn(g, what)
        return self.banks[bank], self.free[bank]

    def wait_full(self, eng, g, what):
        bank, turn = self.turn(g, what)
        eng.wait_ge(self.full[bank], turn + 1)

    def wait_read(self, eng, g, what):
        bank, turn = self.turn(g, what)
        eng.wait_ge(self.free[bank], turn + 2)


def send_rows(nc, dram, keep):
    for u in range(NI):
        for k in range(2):
            nc.gpsimd.indirect_dma_start(
                out=dram["dispatched"], out_offset=bass.IndirectOffsetOnAxis(ap=keep["slot_u"][:, u, k:k + 1], axis=0),
                in_=keep["xh2"][:, u, :], in_offset=None).then_inc(keep["scattered"], 16)


def batch_axis_attention(nc, mem_all, dram, const, keep):
    PAIRS = NI // 2
    BLK = P // B
    QK = (H + KV) * HD
    with ExitStack() as stack:
        m = Memory(nc, stack, "ba")
        w_qk = m.sb("w_qk", [P, C, QK])
        w_v = m.sb("w_v", [P, C, KV * HD])
        w_proj = m.sb("w_proj", [P, C, D])
        w_router = m.sb("w_router", [P, C, E])
        ln1_w, ln1_b = m.sb("ln1_w", [P, C]), m.sb("ln1_b", [P, C])
        limit = m.sb("limit", [P, B])
        prefix = m.sb("prefix", [P, P], BF16)
        ones = m.sb("ones", [P, P], BF16)
        zero = m.sb("zero", [P, 1])
        row_i, row_f, col_f = m.sb("row_i", [P, 1], I32), m.sb("row_f", [P, 1]), m.sb("col_f", [P, B])
        lim_a, lim_b = m.sb("lim_a", [P, B]), m.sb("lim_b", [P, B])
        stats = m.sb("stats", [P, NI, 6])
        mv = m.sb("mv", [P, NI, 2])
        var = m.sb("var", [P, NI])
        rstd = m.sb("rstd", [P, NI])
        xh1 = m.sb("xh1", [P, NI, D])
        att = m.sb("att", [P, NI, D])
        xn_t = m.sb("xn_t", [P, C, NI * P])
        qk = m.sb("qk", [P, H + KV, NI, HD])
        v_diag = m.sb("v_diag", [P, BLK * KV, P])
        k_diag = m.sb("k_diag", [P, KV, BLK, P])
        q_t = m.sb("q_t", [P, H, P])
        prob = [m.sb(f"prob{i}", [P, 4 * NI, B]) for i in range(2)]
        prob += [xh1[:, i * NI // 4:(i + 1) * NI // 4, :].rearrange("p i d -> p (i d)").rearrange("p (n t) -> p n t", t=B)
                 for i in range(2)]
        top = [m.sb(f"top{i}", [P, 4 * NI]) for i in range(2)]
        total = [m.sb(f"total{i}", [P, 4 * NI]) for i in range(2)]
        rec = [m.sb(f"rec{i}", [P, 4 * NI]) for i in range(2)]
        prob_t = [m.sb(f"prob_t{i}", [P, 4, P]) for i in range(2)]
        o_t = qk[:, 0:H, :, :].rearrange("p h i d -> p (h i d)").rearrange("p (n b) -> p n b", b=BLK)
        h_rows = att
        att_t = [m.sb(f"att_t{i}", [P, 2, C, P]) for i in range(2)]
        xh2_t = att_t
        logits = m.sb("logits", [P, NI, E])
        best = m.sb("best", [P, NI, 8])
        best_at = m.sb("best_at", [P, NI, 8], U32)
        shifted = m.sb("shifted", [P, NI, E + 2])
        gate_sum = m.sb("gate_sum", [P, NI])
        gate_rec = m.sb("gate_rec", [P, NI])
        picked = m.sb("picked", [P, NI + 1, E], BF16)
        place = m.sb("place", [P, NI, E])
        masked = m.sb("masked", [P, NI, E])
        hot = m.sb("hot", [P, 2, NI, E])
        slot = m.sb("slot", [P, NI, 2])
        tokens = m.sb("tokens", [P, TILES])
        tail_no = m.sb("tail_no", [P, 2])
        xh2, slot_u, count, experts, segments, one_e, tile_no, tail = (
            keep[n] for n in ("xh2", "slot_u", "count", "experts", "segments", "one_e", "tile_no", "tail"))

        turn = Ring(m, "turn", 3, [(n, i) for n in ("p", "o", "a", "x", "q", "h") for i in range(4)], ("x", "q"))
        prod = Ring(m, "prod", 3, [("s", 2), ("s", 3), ("o", 0), ("o", 1), ("o", 2), ("o", 3)] + [("a", i) for i in range(4)]
                    + [("qk", i) for i in range(8)] + [("k", 0), ("early s", 0), ("early s", 1)], ("qk", "k", "early s"))
        p_v = m.ps("p_v", [P, BLK * KV, HD])
        p_r = m.ps("p_r", [P, 512])

        names = ("weights_in biases_in pool_const xh1_ready xh2_ready "
                 "v_mm v_diag_ready shift_done exp_done prob_ready prob_t_ready "
                 "h_ready keep_done logits_mm shifted_ready gates_exp "
                 "picked_ready place_mm slots_ready dve_step").split()
        s = {n: m.sem(n) for n in names}
        var_ready, var_done, rstd_ready = ([m.sem(f"{n}{i}") for i in range(2)] for n in ("var_ready", "var_done", "rstd_ready"))
        resid = keep["resid"]

        def groups(first, body, repeat):
            first(0)
            body(0)
            for j in repeat(GROUPS - 2):
                body(j + 1)
            body(GROUPS - 1)

        def score(i):
            return ("early s" if i < 2 else "s", i)

        def there(g):
            return not isinstance(g, int) or 0 <= g < GROUPS

        def plain_repeat(eng):
            def repeat(count):
                with eng.Fori(0, count) as j:
                    yield j
            return repeat

        with nc.Block() as block:

            @block.sync
            def _(sp):
                for t, name in ((ln1_w, "ln1_w"), (ln1_b, "ln1_b"), (keep["ln2_w"], "ln2_w"), (keep["ln2_b"], "ln2_b")):
                    sp.dma_start(t[:, :], dram[name]).then_inc(s["biases_in"], 16)
                for t, name in ((w_qk, "w_qk"), (w_v, "w_v"), (w_proj, "w_proj"), (w_router, "w_router")):
                    sp.dma_start(t[:, :, :], dram[name]).then_inc(s["weights_in"], 16)
                sp.dma_start(keep["w1"][:, :, :].rearrange("p (e c) f -> p e c f", c=C), dram["moe_w1"])\
                  .then_inc(keep["experts_in"], 16)
                sp.dma_start(keep["w2"][:, :, :].rearrange("p (e k) h -> p e k h", k=K4), dram["moe_w2"])\
                  .then_inc(keep["experts_in"], 16)

            @block.gpsimd
            def _(pool):
                done = s["pool_const"]
                nc.gpsimd.iota(row_i[:, :], [[0, 1]], base=0, channel_multiplier=1).then_inc(done, 1)
                nc.gpsimd.iota(col_f[:, :], [[1, B]], base=0, channel_multiplier=0,
                               allow_small_or_imprecise_dtypes=True).then_inc(done, 1)
                nc.gpsimd.iota(experts[:, :], [[1, E]], base=0, channel_multiplier=0,
                               allow_small_or_imprecise_dtypes=True).then_inc(done, 1)
                nc.gpsimd.iota(segments[:, :], [[SEGMENT, E]], base=0, channel_multiplier=0,
                               allow_small_or_imprecise_dtypes=True).then_inc(done, 1)
                nc.gpsimd.memset(ones[:, :], 1.0).then_inc(done, 1)
                nc.gpsimd.memset(zero[:, :], 0.0).then_inc(done, 1)
                nc.gpsimd.memset(prefix[:, :], 1.0).then_inc(done, 1)
                nc.gpsimd.memset(picked[:, NI, :], 0.0).then_inc(done, 1)
                nc.gpsimd.memset(count[:, :], 0.0).then_inc(done, 1)
                nc.gpsimd.memset(one_e[:, :], 1.0).then_inc(done, 1)
                nc.gpsimd.memset(tail[:, :, :], 0.0).then_inc(done, 1)
                nc.gpsimd.iota(tail_no[:, :], [[P, 2]], base=2 * TOKENS, channel_multiplier=1,
                               allow_small_or_imprecise_dtypes=True).then_inc(done, 1)
                nc.gpsimd.iota(tile_no[:, :], [[1, MOE_TILES]], base=0, channel_multiplier=0,
                               allow_small_or_imprecise_dtypes=True).then_inc(done, 1)
                nc.gpsimd.iota(tokens[:, :], [[1, TILES]], base=0, channel_multiplier=TILES,
                               allow_small_or_imprecise_dtypes=True).then_inc(done, 1)
                pool.wait_ge(done, 14)
                nc.gpsimd.memset(tail[:, :, D + 1:D + 3], -1.0).then_inc(done, 1)
                nc.gpsimd.tensor_copy(tail[:, :, D:D + 1], tail_no[:, :].unsqueeze(2)).then_inc(done, 1)
                nc.gpsimd.affine_select(out=prefix[:, :], in_=prefix[:, :], compare_op=ALU.is_gt, fill=0.0, base=0,
                                        pattern=[[1, P]], channel_multiplier=-1).then_inc(done, 1)

                def rstd_of(which, g):
                    wait_apart(pool, var_ready[which], g + 1)
                    nc.gpsimd.tensor_scalar(var[:, :], mv[:, :, 1], EPS, None, ALU.add).then_inc(var_done[which], 1)
                    pool.wait_ge(var_done[which], g + 1)
                    nc.gpsimd.tensor_tensor(rstd[:, :], var[:, :], const["minus_half"][:, :], ALU.pow)\
                      .then_inc(rstd_ready[which], 1)

                def scatter(g):
                    wait_apart(pool, s["slots_ready"], g + 1)
                    send_rows(nc, dram, keep)

                def residual(g):
                    for i in range(PAIRS):
                        pool.wait_ge(s["h_ready"], g * PAIRS + i + 1)
                        rows = resid[:, bass.ds(g * NI + 2 * i, 2), :]
                        nc.gpsimd.tensor_tensor(rows, rows, h_rows[:, 2 * i:2 * i + 2, :], ALU.add).then_inc(s["keep_done"], 1)

                def body(g):
                    if there(g + 1):
                        rstd_of(0, g + 1)
                    if there(g - 1):
                        scatter(g - 1)
                    rstd_of(1, g)
                    residual(g)

                groups(lambda g: rstd_of(0, g), body, plain_repeat(pool))
                pool.wait_ge(s["keep_done"], GROUPS * PAIRS)

            @block.scalar
            def _(act):
                act.wait_ge(s["biases_in"], 64)
                act.wait_ge(s["pool_const"], 17)

                def turned(g, what, out, scale=None, bias=None):
                    bank, free = turn.read(act, g, what)
                    src = bank[:, :].rearrange("p (u c n) -> p u c n", u=2, c=C)
                    if scale is None:
                        nc.scalar.activation(out, src, ACT.Copy).then_inc(free, 1)
                        return
                    for c in range(C):
                        ins = nc.scalar.activation(out[:, :, c, :], src[:, :, c, :], ACT.Identity,
                                                   bias=bias[:, c:c + 1], scale=scale[:, c:c + 1])
                    ins.then_inc(free, 1)

                def qk_copy(g, u):
                    bank, free = prod.read(act, g, ("qk", u))
                    nc.scalar.activation(qk[:, :, u, :], bank[:, 0:QK].rearrange("p (h d) -> p h d", d=HD), ACT.Copy)\
                      .then_inc(free, 1)

                def first(g):
                    xn_pairs = xn_t[:, :, :].rearrange("p c (u n) -> p u c n", n=P)
                    for i in range(PAIRS):
                        turned(g, ("x", i), xn_pairs[:, 2 * i:2 * i + 2, :, :], ln1_w, ln1_b)
                        if i >= 1:
                            qk_copy(g, 2 * i - 2)
                            qk_copy(g, 2 * i - 1)
                    qk_copy(g, NI - 2)
                    qk_copy(g, NI - 1)
                    for i in range(4):
                        bank, free = turn.read(act, g, ("q", i))
                        nc.scalar.activation(q_t[:, 4 * i:4 * i + 4, :], bank[:, :].rearrange("p (h n) -> p h n", n=P),
                                             ACT.Copy).then_inc(free, 1)

                def value_blocks(g, pair):
                    act.wait_ge(s["v_mm"], g + 1)
                    for i in (2 * pair, 2 * pair + 1):
                        ins = nc.scalar.activation(v_diag[:, :, i * HD:(i + 1) * HD], p_v[:, :, :], ACT.Identity,
                                                   bias=zero[:, 0:1], scale=const["head_mask"][:, i:i + 1])
                    ins.then_inc(s["v_diag_ready"], 1)

                def exponential(g, i):
                    act.wait_ge(s["shift_done"], g * 4 + i + 1)
                    nc.scalar.activation(prob[i][:, :, :], prob[i][:, :, :], ACT.Exp).then_inc(s["exp_done"], 1)

                def prob_t_copy(g, i):
                    bank, free = turn.read(act, g, ("p", i))
                    if i >= 2:
                        prod.wait_full(act, g, ("o", i - 2))
                    nc.scalar.activation(prob_t[i % 2][:, :, :], bank[:, :].rearrange("p (u n) -> p u n", n=P),
                                         ACT.Copy).then_inc(free, 1)

                def o_t_copy(g, i):
                    bank, free = prod.read(act, g, ("o", i))
                    nc.scalar.activation(o_t[:, :, 2 * i:2 * i + 2], bank[:, :].rearrange("p (b n) -> p n b", b=2),
                                         ACT.Copy).then_inc(free, 1)

                def body(g):
                    exponential(g, 1)
                    prob_t_copy(g, 0)
                    prob_t_copy(g, 1)
                    exponential(g, 2)
                    o_t_copy(g, 0)
                    exponential(g, 3)
                    o_t_copy(g, 1)
                    prob_t_copy(g, 2)
                    prob_t_copy(g, 3)
                    if there(g - 1):
                        act.wait_ge(s["shifted_ready"], g)
                        nc.scalar.activation(shifted[:, :, :], shifted[:, :, :], ACT.Exp).then_inc(s["gates_exp"], 1)
                    o_t_copy(g, 2)
                    o_t_copy(g, 3)
                    wait(act, s["xh2_ready"], g * NI)
                    wait(act, s["keep_done"], g * PAIRS)
                    for i in range(4):
                        bank, free = turn.read(act, g, ("o", i))
                        nc.scalar.activation(
                            att[:, :, i * 4 * HD:(i + 1) * 4 * HD].rearrange("p i (h d) -> p h i d", d=HD),
                            bank[:, :].rearrange("p (h i d) -> p h i d", h=4, d=HD), ACT.Copy).then_inc(free, 1)
                    for i in range(PAIRS):
                        if i >= 2:
                            prod.wait_full(act, g, ("a", i - 2))
                        turned(g, ("a", i), att_t[i % 2][:, :, :, :])
                    if there(g + 1):
                        first(g + 1)
                    for i in range(PAIRS):
                        if i >= 2:
                            act.wait_ge(s["logits_mm"], g * PAIRS + i - 1)
                        if there(g + 1) and i == PAIRS - 1:
                            exponential(g + 1, 0)
                        turned(g, ("h", i), xh2_t[i % 2][:, :, :, :], keep["ln2_w"], keep["ln2_b"])
                        if there(g + 1):
                            value_blocks(g + 1, i)

                def start(g):
                    first(g)
                    for pair in range(PAIRS):
                        value_blocks(g, pair)
                    exponential(g, 0)

                groups(start, body, plain_repeat(act))
                act.wait_ge(s["shifted_ready"], GROUPS)
                nc.scalar.activation(shifted[:, :, :], shifted[:, :, :], ACT.Exp).then_inc(s["gates_exp"], 1)

            @block.vector
            def _(dve):
                steps = Steps(dve, s["dve_step"])
                turn.open(dve)
                prod.open(dve)
                dve.wait_ge(s["pool_const"], 17)
                steps.chain(nc.vector.tensor_scalar(row_i[:, :], row_i[:, :], B - 1, None, ALU.bitwise_and))
                steps.chain(nc.vector.tensor_copy(row_f[:, :], row_i[:, :]))
                steps.chain(nc.vector.tensor_scalar(limit[:, :], col_f[:, :], row_f[:, 0:1], None, ALU.is_le))
                steps.mark(nc.vector.tensor_scalar(lim_a[:, :], limit[:, :], BIG, None, ALU.mult))
                steps.chain(nc.vector.tensor_scalar(lim_b[:, :], limit[:, :], -1.0, BIG, ALU.add, ALU.mult))
                steps.chain(nc.vector.tensor_tensor(limit[:, :], lim_a[:, :], lim_b[:, :], ALU.add))
                dve.wait_ge(s["biases_in"], 64)
                dve.wait_ge(keep["x2_in"], 48)


                def statistics(rows, ready):
                    for u in range(NI):
                        last = steps.mark(nc.vector.bn_stats(stats[:, u, :], rows(u)))
                    steps.need_apart(last)
                    for u in range(NI):
                        ins = nc.vector.bn_aggr(mv[:, u, :], stats[:, u, :])
                        if u < NI - 1:
                            steps.mark(ins)
                    ins.then_inc(ready, 1)

                def normalise(rows, g, which, out, ready):
                    dve.wait_ge(rstd_ready[which], g + 1)
                    for u in range(NI):
                        nc.vector.tensor_scalar(out[:, u, :], rows(u), mv[:, u, 0:1], rstd[:, u:u + 1],
                                                ALU.subtract, ALU.mult).then_inc(ready, 1)

                def x2_rows(g):
                    return lambda u: resid[:, bass.ds(g * NI + u, 1), :]

                def first(g):
                    bank, free = prod.read(dve, g, ("k", 0))
                    for kv in range(KV):
                        src = bank[:, kv * P:(kv + 1) * P].rearrange("p (t b) -> p b t", b=BLK).unsqueeze(2)
                        ins = nc.vector.tensor_tensor(
                            k_diag[:, kv, :, :].rearrange("p b (i t) -> p b i t", t=B),
                            bcast(src, [P, BLK, NI, B]),
                            bcast(const["head_mask"][:, :].unsqueeze(1).unsqueeze(3), [P, BLK, NI, B]), ALU.mult)
                        if kv < KV - 1:
                            steps.mark(ins)
                    ins.then_inc(free, 1)

                def score_top(g, i):
                    bank, free = prod.read(dve, g, score(i))
                    nc.vector.scalar_tensor_tensor(prob[i][:, :, :], bank[:, :].rearrange("p (n t) -> p n t", t=B),
                                                   HD ** -0.5, bcast(limit[:, :].unsqueeze(1), [P, 4 * NI, B]),
                                                   ALU.mult, ALU.min).then_inc(free, 1)
                    prod.wait_read(dve, g, score(i))
                    steps.chain(nc.vector.tensor_reduce(top[i % 2][:, :], prob[i][:, :, :], AX, ALU.max))
                    nc.vector.tensor_tensor(prob[i][:, :, :], prob[i][:, :, :],
                                            bcast(top[i % 2][:, :].unsqueeze(2), [P, 4 * NI, B]), ALU.subtract)\
                        .then_inc(s["shift_done"], 1)

                def normalise_prob(g, i):
                    dve.wait_ge(s["exp_done"], g * 4 + i + 1)
                    steps.chain(nc.vector.tensor_reduce(total[i % 2][:, :], prob[i][:, :, :], AX, ALU.add))
                    steps.chain(nc.vector.reciprocal(rec[i % 2][:, :], total[i % 2][:, :]))
                    nc.vector.tensor_tensor(prob[i][:, :, :], prob[i][:, :, :],
                                            bcast(rec[i % 2][:, :].unsqueeze(2), [P, 4 * NI, B]), ALU.mult)\
                        .then_inc(s["prob_ready"], 1)

                def route_best(g):
                    dve.wait_ge(s["logits_mm"], g * PAIRS + PAIRS)
                    steps.need_apart(steps.mark(nc.vector.tensor_copy(logits[:, :, :],
                                                                      p_r[:, 0:NI * E].rearrange("p (u e) -> p u e", e=E))))
                    for u in range(NI):
                        last = steps.mark(nc.vector.max(best[:, u, :], logits[:, u, :]))
                    return last

                def route_shift(last):
                    steps.need_apart(last)
                    leader = best[:, :, 0:1]
                    steps.mark(nc.vector.tensor_tensor(shifted[:, :, 0:E], logits[:, :, :], bcast(leader, [P, NI, E]),
                                                       ALU.subtract))
                    nc.vector.tensor_tensor(shifted[:, :, E:E + 2], best[:, :, 0:2], bcast(leader, [P, NI, 2]),
                                            ALU.subtract).then_inc(s["shifted_ready"], 1)
                    for u in range(NI):
                        last = steps.mark(nc.vector.max_index(best_at[:, u, :], best[:, u, :], logits[:, u, :]))
                    return last

                def route_pick(g, last):
                    steps.need(last)
                    chosen = xh2[:, :, D + 1:D + 3]
                    steps.mark(nc.vector.tensor_copy(xh2[:, :, D:D + 1], tokens[:, bass.ds(g * NI, NI)].unsqueeze(2)))
                    steps.chain(nc.vector.tensor_copy(chosen, best_at[:, :, 0:2]))
                    for k in range(2):
                        last = steps.mark(nc.vector.tensor_tensor(hot[:, k, :, :], bcast(chosen[:, :, k:k + 1], [P, NI, E]),
                                                                  bcast(experts[:, :].unsqueeze(1), [P, NI, E]), ALU.is_equal))
                    steps.need(last)
                    nc.vector.tensor_tensor(picked[:, 0:NI, :], hot[:, 0, :, :], hot[:, 1, :, :], ALU.add)\
                        .then_inc(s["picked_ready"], 1)

                def route_slots(g):
                    dve.wait_ge(s["gates_exp"], g + 1)
                    steps.chain(nc.vector.tensor_reduce(gate_sum[:, :], shifted[:, :, 0:E], AX, ALU.add))
                    steps.chain(nc.vector.reciprocal(gate_rec[:, :], gate_sum[:, :]))
                    steps.mark(nc.vector.tensor_tensor(xh2[:, :, D + 3:D + 5], shifted[:, :, E:E + 2],
                                                       bcast(gate_rec[:, :].unsqueeze(2), [P, NI, 2]), ALU.mult))
                    dve.wait_ge(s["place_mm"], g + 1)
                    places = p_r[:, NI * E:(2 * NI + 1) * E].rearrange("p (u e) -> p u e", e=E)
                    steps.chain(nc.vector.tensor_tensor(place[:, :, :], places[:, 0:NI, :],
                                                        bcast(count[:, :].unsqueeze(1), [P, NI, E]), ALU.add))
                    steps.mark(nc.vector.tensor_tensor(count[:, :], places[:, NI, :], count[:, :], ALU.add))
                    steps.chain(nc.vector.tensor_tensor(place[:, :, :], place[:, :, :],
                                                        bcast(segments[:, :].unsqueeze(1), [P, NI, E]), ALU.add))
                    for k in range(2):
                        steps.chain(nc.vector.tensor_tensor(masked[:, :, :], place[:, :, :], hot[:, k, :, :], ALU.mult))
                        summed = steps.mark(nc.vector.tensor_reduce(slot[:, :, k:k + 1], masked[:, :, :], AX, ALU.add))
                        steps.need(summed)
                    nc.vector.tensor_copy(slot_u[:, :, :], slot[:, :, :]).then_inc(s["slots_ready"], 1)

                def body(g):
                    score_top(g, 0)
                    score_top(g, 1)
                    normalise_prob(g, 0)
                    normalise_prob(g, 1)
                    score_top(g, 2)
                    score_top(g, 3)
                    normalise_prob(g, 2)
                    normalise_prob(g, 3)
                    if there(g - 1):
                        route_pick(g - 1, route_shift(route_best(g - 1)))
                    if there(g + 1):
                        statistics(x2_rows(g + 1), var_ready[0])
                    if there(g - 1):
                        route_slots(g - 1)
                    if there(g + 1):
                        turn.wait_full(dve, g, ("p", 3))
                        normalise(x2_rows(g + 1), g + 1, 0, xh1, s["xh1_ready"])
                    for i in range(PAIRS):
                        bank, free = prod.read(dve, g, ("a", i))
                        added = steps.mark(nc.vector.tensor_tensor(
                            h_rows[:, 2 * i:2 * i + 2, :], bank[:, :].rearrange("p (u d) -> p u d", u=2),
                            resid[:, bass.ds(g * NI + 2 * i, 2), :], ALU.add))
                        steps.need(added)
                        dve.sem_inc(free, 1)
                        dve.sem_inc(s["h_ready"], 1)
                    statistics(lambda u: h_rows[:, u, :], var_ready[1])
                    wait(dve, keep["scattered"], g * (NI * 2 * 16))
                    normalise(lambda u: h_rows[:, u, :], g, 1, xh2[:, :, 0:D], s["xh2_ready"])
                    if there(g + 1):
                        first(g + 1)

                def start(g):
                    dve.wait_ge(keep["x2_in"], 48)
                    statistics(x2_rows(g), var_ready[0])
                    normalise(x2_rows(g), g, 0, xh1, s["xh1_ready"])
                    first(g)

                groups(start, body, lambda count: steps.repeat(count, 81))
                route_pick(GROUPS - 1, route_shift(route_best(GROUPS - 1)))
                route_slots(GROUPS - 1)
                dve.wait_ge(s["keep_done"], GROUPS * PAIRS)

            @block.tensor
            def _(pe):
                ident = const["identity"]
                pe.wait_ge(s["weights_in"], 64)
                pe.wait_ge(s["pool_const"], 17)

                def turn_pair(g, what, ready, rows, i):
                    pe.wait_ge(ready, g * NI + 2 * i + 2)
                    bank, full = turn.fill(pe, g, (what, i))
                    for u in range(2):
                        for c in range(C):
                            ins = nc.tensor.transpose(bank[:, (u * C + c) * P:(u * C + c + 1) * P],
                                                      rows[:, 2 * i + u, c * P:(c + 1) * P], ident[:, :])
                    ins.then_inc(full, 1)

                def project_qk(g, i):
                    turn.wait_read(pe, g, ("x", i))
                    for u in (2 * i, 2 * i + 1):
                        bank, full = prod.fill(pe, g, ("qk", u))
                        for c in range(C):
                            ins = nc.tensor.matmul(bank[:, 0:QK], xn_t[:, c, u * P:(u + 1) * P], w_qk[:, c, :],
                                                   start=(c == 0), stop=(c == C - 1))
                        ins.then_inc(full, 1)

                def first(g):
                    turn_pair(g, "x", s["xh1_ready"], xh1, 0)
                    for i in range(1, PAIRS):
                        turn_pair(g, "x", s["xh1_ready"], xh1, i)
                        project_qk(g, i - 1)
                    project_qk(g, PAIRS - 1)
                    wait(pe, s["v_diag_ready"], g * PAIRS)
                    for b in range(BLK):
                        for c in range(C):
                            tokens = xn_t[:, c, :].rearrange("p (n b) -> p n b", b=BLK)[:, :, b]
                            ins = nc.tensor.matmul(p_v[:, b * KV:(b + 1) * KV, :].rearrange("p k d -> p (k d)"), tokens,
                                                   w_v[:, c, :], start=(c == 0), stop=(c == C - 1))
                    ins.then_inc(s["v_mm"], 1)
                    for u in range(NI):
                        prod.wait_read(pe, g, ("qk", u))
                    bank, full = prod.fill(pe, g, ("k", 0))
                    for kv in range(KV):
                        ins = nc.tensor.transpose(bank[:, kv * P:(kv + 1) * P],
                                                  qk[:, H + kv, :, :].rearrange("p i d -> p (i d)"), ident[:, :])
                    ins.then_inc(full, 1)
                    for i in range(4):
                        bank, full = turn.fill(pe, g, ("q", i))
                        for h in range(4):
                            ins = nc.tensor.transpose(bank[:, h * P:(h + 1) * P],
                                                      qk[:, 4 * i + h, :, :].rearrange("p i d -> p (i d)"), ident[:, :])
                        ins.then_inc(full, 1)

                def scores(g, i):
                    if i == 0:
                        for h4 in range(4):
                            turn.wait_read(pe, g, ("q", h4))
                        prod.wait_read(pe, g, ("k", 0))
                    bank, full = prod.fill(pe, g, score(i))
                    for b2 in range(2):
                        for kv in range(KV):
                            b = 2 * i + b2
                            tile = 2 * b2 + kv // 2
                            rows = slice(64 * (kv % 2), 64 * (kv % 2) + 64)
                            queries = q_t[:, kv * REP:(kv + 1) * REP, :].rearrange("p h n -> p (h n)")\
                                .rearrange("p (n b) -> p n b", b=BLK)[:, :, b]
                            ins = nc.tensor.matmul(bank[rows, tile * P:(tile + 1) * P], queries, k_diag[:, kv, b, :],
                                                   start=True, stop=True)
                    ins.then_inc(full, 1)

                def turn_prob(g, i):
                    pe.wait_ge(s["prob_ready"], g * 4 + i + 1)
                    bank, full = turn.fill(pe, g, ("p", i))
                    for t in range(4):
                        ins = nc.tensor.transpose(bank[:, t * P:(t + 1) * P],
                                                  prob[i][:, t * NI:(t + 1) * NI, :].rearrange("p n t -> p (n t)"),
                                                  ident[:, :])
                    ins.then_inc(full, 1)

                def outputs(g, i):
                    turn.wait_read(pe, g, ("p", i))
                    bank, full = prod.fill(pe, g, ("o", i))
                    for b2 in range(2):
                        for kv in range(KV):
                            tile = 2 * b2 + kv // 2
                            ins = nc.tensor.matmul(bank[:, (b2 * KV + kv) * 64:(b2 * KV + kv + 1) * 64],
                                                   v_diag[:, (2 * i + b2) * KV + kv, :],
                                                   prob_t[i % 2][:, tile, 64 * (kv % 2):64 * (kv % 2) + 64],
                                                   start=True, stop=True)
                    ins.then_inc(full, 1)

                def turn_att(g, i):
                    bank, full = turn.fill(pe, g, ("a", i))
                    for u in range(2):
                        for c in range(C):
                            ins = nc.tensor.transpose(bank[:, (u * C + c) * P:(u * C + c + 1) * P],
                                                      att[:, 2 * i + u, c * P:(c + 1) * P], ident[:, :])
                    ins.then_inc(full, 1)

                def project(g, i):
                    turn.wait_read(pe, g, ("a", i))
                    bank, full = prod.fill(pe, g, ("a", i))
                    for u in range(2):
                        for c in range(C):
                            ins = nc.tensor.matmul(bank[:, u * D:(u + 1) * D], att_t[i % 2][:, u, c, :], w_proj[:, c, :],
                                                   start=(c == 0), stop=(c == C - 1))
                    ins.then_inc(full, 1)

                def route(g, i):
                    turn.wait_read(pe, g, ("h", i))
                    for u in range(2):
                        for c in range(C):
                            ins = nc.tensor.matmul(p_r[:, (2 * i + u) * E:(2 * i + u + 1) * E], xh2_t[i % 2][:, u, c, :],
                                                   w_router[:, c, :], start=(c == 0), stop=(c == C - 1))
                    ins.then_inc(s["logits_mm"], 1)

                def count_places(g):
                    pe.wait_ge(s["picked_ready"], g + 1)
                    places = p_r[:, NI * E:(2 * NI + 1) * E]
                    nc.tensor.matmul(places, prefix[:, :], picked[:, :, :].rearrange("p u e -> p (u e)"), start=True, stop=False)
                    for u in range(NI):
                        ins = nc.tensor.matmul(places[:, (u + 1) * E:(NI + 1) * E], ones[:, :],
                                               bcast(picked[:, u:u + 1, :], [P, NI - u, E]), start=False, stop=(u == NI - 1))
                    ins.then_inc(s["place_mm"], 1)

                def body(g):
                    scores(g, 2)
                    scores(g, 3)
                    turn_prob(g, 0)
                    turn_prob(g, 1)
                    pe.wait_ge(s["v_diag_ready"], g * PAIRS + PAIRS)
                    outputs(g, 0)
                    outputs(g, 1)
                    turn_prob(g, 2)
                    turn_prob(g, 3)
                    outputs(g, 2)
                    outputs(g, 3)
                    if there(g - 1):
                        count_places(g - 1)
                    for i in range(4):
                        prod.wait_read(pe, g, ("o", i))
                    for i in range(4):
                        bank, full = turn.fill(pe, g, ("o", i))
                        for h in range(4):
                            head = o_t[:, (4 * i + h) * B:(4 * i + h + 1) * B, :].rearrange("p s b -> p (s b)")
                            ins = nc.tensor.transpose(bank[:, h * P:(h + 1) * P], head, ident[:, :])
                        ins.then_inc(full, 1)
                    for i in range(4):
                        turn.wait_read(pe, g, ("o", i))
                    turn_att(g, 0)
                    for i in range(1, PAIRS):
                        turn_att(g, i)
                        project(g, i - 1)
                    project(g, PAIRS - 1)
                    if there(g + 1):
                        first(g + 1)
                    turn_pair(g, "h", s["xh2_ready"], xh2, 0)
                    for i in range(1, PAIRS):
                        turn_pair(g, "h", s["xh2_ready"], xh2, i)
                        route(g, i - 1)
                        if there(g + 1) and i < PAIRS - 1:
                            scores(g + 1, i - 1)
                    route(g, PAIRS - 1)

                def start(g):
                    first(g)
                    scores(g, 0)
                    scores(g, 1)

                groups(start, body, plain_repeat(pe))
                count_places(GROUPS - 1)


def experts(nc, mem_all, dram, const, keep):
    with ExitStack() as stack:
        m = Memory(nc, stack, "ex")
        count, experts, segments, one_e, tile_no = (keep[n] for n in ("count", "experts", "segments", "one_e", "tile_no"))
        n_tiles, up_to, before = m.sb("n_tiles", [P, E]), m.sb("up_to", [P, E]), m.sb("before", [P, E])
        tail_row, tail_i = m.sb("tail_row", [P, E]), m.sb("tail_i", [P, E], I32)
        count_i, tiles_i = m.sb("count_i", [P, E], I32), m.sb("tiles_i", [P, E], I32)
        skip_f, own_f, row_at, expert_f = (m.sb(n, [P, MOE_TILES]) for n in ("skip_f", "own_f", "row_at", "expert_f"))
        expert_i, first_i = m.sb("expert_i", [P, MOE_TILES], I32), m.sb("first_i", [P, MOE_TILES], I32)
        wide, hot_t = m.sb("wide", [P, MOE_TILES, E]), m.sb("hot_t", [P, MOE_TILES, E])
        w1, w2 = keep["w1"], keep["w2"]
        w1_hi, w2_hi = m.sb("w1_hi", [P, E * C, F], F32R), m.sb("w2_hi", [P, E * K4, D], F32R)
        w1_lo, w2_lo = w1[:, :, :].bitcast(F32R), w2[:, :, :].bitcast(F32R)
        x_hi = [m.sb(f"x_hi{i}", [P, C, P], F32R) for i in range(2)]
        x_lo = [m.sb(f"x_lo{i}", [P, C, P], F32R) for i in range(2)]
        hid_hi = [m.sb(f"hid_hi{i}", [P, K4, P], F32R) for i in range(2)]
        hid_lo = [m.sb(f"hid_lo{i}", [P, K4, P], F32R) for i in range(2)]
        xm = [m.sb(f"xm{i}", [P, ROW]) for i in range(2)]
        xm_t = [m.sb(f"xm_t{i}", [P, C, P]) for i in range(2)]
        hid = [m.sb(f"hid{i}", [P, F]) for i in range(2)]
        ym = [m.sb(f"ym{i}", [P, D]) for i in range(2)]
        token = [m.sb(f"token{i}", [P, ROW - D]) for i in range(2)]
        hit = m.sb("hit", [P, 2])
        hit_gate = m.sb("hit_gate", [P, 2])
        gate = [m.sb(f"gate{i}", [P, 1]) for i in range(2)]
        home_f = [m.sb(f"home_f{i}", [P, 1]) for i in range(2)]
        home = [m.sb(f"home{i}", [P, 1], U32) for i in range(2)]

        p_x = m.ps("p_x", [P, C, P])
        p_h = [m.ps(f"p_h{i}", [P, F]) for i in range(2)]
        p_t = [m.ps(f"p_t{half}", [P, 512])[:, 0:K4 // 2 * P].rearrange("p (c n) -> p c n", n=P) for half in range(2)]
        p_y = [m.ps(f"p_y{i}", [P, 512]) for i in range(2)]

        names = ("table_ready token_ready tails_ready tails_out w1_high w2_high w1_split w2_split x_mm x_ready x_high x_split h_mm "
                 "hid_ready t_mm hid_high hid_split y_mm y_ready home_ready dve_step").split()
        s = {n: m.sem(n) for n in names}
        xm_in = [m.sem(f"xm_in{i}") for i in range(2)]
        ym_out = [m.sem(f"ym_out{i}") for i in range(2)]
        LAST = MOE_TILES - 1
        HALVES = (slice(0, K4 // 2), slice(K4 // 2, K4))
        assert MOE_TILES % 2 == 1

        def moe_pipeline(first, step, end, repeat):
            first(0, 0, 0)
            step(0, 1, 1)
            step(1, 2, 0)
            for j in repeat((MOE_TILES - 5) // 2):
                step(j + 1, j * 2 + 3, 1)
                step(j + 2, j * 2 + 4, 0)
            step(LAST // 2 - 1, LAST - 1, 1, more=False)
            end(LAST // 2, LAST, 0)

        def plain_repeat(eng):
            def repeat(count):
                with eng.Fori(0, count) as j:
                    yield j
            return repeat

        with nc.Block() as block:

            @block.sync
            def _(sp):
                sp.wait_ge(s["tails_ready"], 1)
                with sp.Fori(0, E) as e:
                    row = sp.value_load(tail_i[0:1, bass.ds(e, 1)], min_val=0, max_val=E * SEGMENT - 2 * P)
                    sp.dma_start(dram["dispatched"][bass.ds(row, 2 * P), :].rearrange("(t p) d -> p t d", p=P),
                                 keep["tail"][:, :, :]).then_inc(s["tails_out"], 16)
                sp.wait_ge(s["tails_out"], 16 * E)
                sp.wait_ge(keep["scattered"], GROUPS * NI * 2 * 16)
                sp.wait_ge(s["table_ready"], 1)

                def load(t, par):
                    row = sp.value_load(first_i[0:1, bass.ds(t, 1)], min_val=0, max_val=E * SEGMENT - P)
                    wait(sp, s["x_mm"], t - 1)
                    wait(sp, s["token_ready"], t - 1)
                    sp.dma_start(xm[par][:, :], dram["dispatched"][bass.ds(row, P), :]).then_inc(xm_in[par], 16)

                load(0, 0)
                load(1, 1)
                with sp.Fori(0, (MOE_TILES - 3) // 2) as j:
                    load(j * 2 + 2, 0)
                    load(j * 2 + 3, 1)
                load(LAST, 0)

            @block.gpsimd
            def _(pool):
                send_rows(nc, dram, keep)

                def send(turn, par):
                    wait(pool, ym_out[1 - par], (turn + par) * 16)
                    wait_apart(pool, s["y_ready"], turn * 2 + par + 1)
                    nc.gpsimd.indirect_dma_start(
                        out=dram["results"], out_offset=bass.IndirectOffsetOnAxis(ap=home[par][:, 0:1], axis=0),
                        in_=ym[par][:, :], in_offset=None).then_inc(ym_out[par], 16)

                send(0, 0)
                send(0, 1)
                with pool.Fori(0, LAST // 2 - 1) as j:
                    send(j + 1, 0)
                    send(j + 1, 1)
                send(LAST // 2, 0)
                pool.wait_ge(ym_out[0], 16 * (LAST // 2 + 1))
                pool.wait_ge(ym_out[1], 16 * (LAST // 2))

            @block.scalar
            def _(act):
                act.wait_ge(keep["experts_in"], 32)
                for e in range(E):
                    nc.scalar.activation(w1_hi[:, e * C:(e + 1) * C, :], w1[:, e * C:(e + 1) * C, :], ACT.Copy)\
                      .then_inc(s["w1_high"], 1)
                for e in range(E):
                    nc.scalar.activation(w2_hi[:, e * K4:(e + 1) * K4, :], w2[:, e * K4:(e + 1) * K4, :], ACT.Copy)\
                      .then_inc(s["w2_high"], 1)

                def x_copy(t, par):
                    act.wait_ge(s["x_mm"], t + 1)
                    wait(act, s["x_split"], t - 1)
                    for c in range(C):
                        ins = nc.scalar.activation(xm_t[par][:, c, :], p_x[:, c, :], ACT.Identity,
                                                   bias=keep["ln2_b"][:, c:c + 1], scale=keep["ln2_w"][:, c:c + 1])
                    ins.then_inc(s["x_ready"], 1)

                def gelu(t, par):
                    act.wait_ge(s["h_mm"], t + 1)
                    wait(act, s["t_mm"], 2 * (t - 1))
                    nc.scalar.activation(hid[par][:, :], p_h[par][:, :], ACT.Gelu_apprx_tanh).then_inc(s["hid_ready"], 1)

                def hid_high(t, par):
                    wait(act, s["y_mm"], t - 1)
                    for half, cs in enumerate(HALVES):
                        act.wait_ge(s["t_mm"], 2 * t + half + 1)
                        nc.scalar.activation(hid_hi[par][:, cs, :], p_t[half], ACT.Copy).then_inc(s["hid_high"], 1)

                def first(turn, t, par):
                    x_copy(0, 0)
                    x_copy(1, 1)
                    step(turn, t, par)

                def step(turn, t, par, more=True):
                    gelu(t, par)
                    hid_high(t, par)
                    if more:
                        x_copy(t + 2, par)

                def end(turn, t, par):
                    gelu(t, par)
                    hid_high(t, par)

                moe_pipeline(first, step, end, plain_repeat(act))

            @block.vector
            def _(dve):
                V = nc.vector
                steps = Steps(dve, s["dve_step"])

                def tile_table():
                    steps.chain(V.tensor_scalar(count_i[:, :], count[:, :], float(P - 1), None, ALU.add))
                    steps.chain(V.tensor_scalar(tiles_i[:, :], count_i[:, :], 7, None, ALU.logical_shift_right))
                    steps.chain(V.tensor_copy(n_tiles[:, :], tiles_i[:, :]))
                    steps.chain(V.tensor_tensor_scan(up_to[:, :], one_e[:, :], n_tiles[:, :], 0.0, ALU.mult, ALU.add))
                    steps.chain(V.tensor_tensor(before[:, :], up_to[:, :], n_tiles[:, :], ALU.subtract))
                    steps.chain(V.tensor_tensor(tail_row[:, :], count[:, :], segments[:, :], ALU.add))
                    V.tensor_copy(tail_i[:, :], tail_row[:, :]).then_inc(s["tails_ready"], 1)
                    wide_shape = [P, MOE_TILES, E]
                    steps.chain(V.tensor_tensor(wide[:, :, :], bcast(tile_no[:, :].unsqueeze(2), wide_shape),
                                                bcast(up_to[:, :].unsqueeze(1), wide_shape), ALU.is_ge))
                    steps.chain(V.tensor_reduce(expert_f[:, :], wide[:, :, :], AX, ALU.add))
                    steps.chain(V.tensor_scalar(expert_f[:, :], expert_f[:, :], float(E - 1), None, ALU.min))
                    steps.chain(V.tensor_tensor(hot_t[:, :, :], bcast(expert_f[:, :].unsqueeze(2), wide_shape),
                                                bcast(experts[:, :].unsqueeze(1), wide_shape), ALU.is_equal))
                    for table, out in ((before, skip_f), (n_tiles, own_f)):
                        steps.chain(V.tensor_tensor(wide[:, :, :], hot_t[:, :, :], bcast(table[:, :].unsqueeze(1), wide_shape), ALU.mult))
                        steps.chain(V.tensor_reduce(out[:, :], wide[:, :, :], AX, ALU.add))
                    steps.chain(V.tensor_tensor(skip_f[:, :], tile_no[:, :], skip_f[:, :], ALU.subtract))
                    steps.chain(V.tensor_tensor(skip_f[:, :], skip_f[:, :], own_f[:, :], ALU.min))
                    steps.chain(V.tensor_scalar(skip_f[:, :], skip_f[:, :], float(P), None, ALU.mult))
                    steps.chain(V.scalar_tensor_tensor(row_at[:, :], expert_f[:, :], float(SEGMENT), skip_f[:, :],
                                                       ALU.mult, ALU.add))
                    steps.mark(V.tensor_copy(expert_i[:, :], expert_f[:, :]))
                    V.tensor_copy(first_i[:, :], row_at[:, :]).then_inc(s["table_ready"], 1)

                def low_parts(w, hi, lo, per, experts, ready, done):
                    for e in experts:
                        dve.wait_ge(ready, e + 1)
                        part = slice(e * per, (e + 1) * per)
                        ins = V.tensor_tensor(lo[:, part, :], w[:, part, :], hi[:, part, :].bitcast(F32), ALU.subtract)
                    ins.then_inc(done, 1)

                tile_table()
                low_parts(w1, w1_hi, w1_lo, C, range(E), s["w1_high"], s["w1_split"])
                low_parts(w2, w2_hi, w2_lo, K4, range(E // 2), s["w2_high"], s["w2_split"])

                def gates_and_homes(t, par):
                    dve.wait_ge(s["token_ready"], t + 1)
                    steps.chain(V.tensor_tensor(hit[:, :], token[par][:, 1:3],
                                                bcast(expert_f[:, bass.ds(t, 1)], [P, 2]), ALU.is_equal))
                    steps.mark(V.tensor_tensor(hit_gate[:, :], hit[:, :], token[par][:, 3:5], ALU.mult))
                    steps.chain(V.scalar_tensor_tensor(home_f[par][:, :], hit[:, 1:2], float(TOKENS), token[par][:, 0:1],
                                                       ALU.mult, ALU.add))
                    V.tensor_tensor(gate[par][:, :], hit_gate[:, 0:1], hit_gate[:, 1:2], ALU.add)\
                     .then_inc(s["home_ready"], 1)

                def copy_token(turn, par):
                    dve.wait_ge(xm_in[par], turn * 16 + 16)
                    wait(dve, s["home_ready"], turn * 2 + par - 1)
                    V.tensor_copy(token[par][:, :], xm[par][:, D:ROW]).then_inc(s["token_ready"], 1)

                def split_x(t, par):
                    dve.wait_ge(s["x_ready"], t + 1)
                    wait(dve, s["h_mm"], t - 1)
                    V.tensor_copy(x_hi[par][:, :, :], xm_t[par][:, :, :]).then_inc(s["x_high"], 1)
                    dve.wait_ge(s["x_high"], t + 1)
                    V.tensor_tensor(x_lo[par][:, :, :], xm_t[par][:, :, :], x_hi[par][:, :, :].bitcast(F32), ALU.subtract)\
                     .then_inc(s["x_split"], 1)

                def split_hidden(t, par):
                    wait(dve, s["y_mm"], t - 1)
                    for half, cs in enumerate(HALVES):
                        dve.wait_ge(s["hid_high"], 2 * t + half + 1)
                        V.tensor_tensor(hid_lo[par][:, cs, :], p_t[half], hid_hi[par][:, cs, :].bitcast(F32),
                                        ALU.subtract).then_inc(s["hid_split"], 1)

                def y_gated(turn, t, par):
                    wait(dve, ym_out[par], turn * 16)
                    dve.wait_ge(s["home_ready"], t + 1)
                    steps.mark(V.tensor_copy(home[par][:, :], home_f[par][:, :]))
                    dve.wait_ge(s["y_mm"], t + 1)
                    V.tensor_scalar(ym[par][:, :], p_y[par][:, 0:D], gate[par][:, 0:1], None, ALU.mult)\
                     .then_inc(s["y_ready"], 1)

                def first(turn, t, par):
                    for i in range(2):
                        copy_token(0, i)
                        split_x(i, i)
                    low_parts(w2, w2_hi, w2_lo, K4, range(E // 2, E), s["w2_high"], s["w2_split"])
                    gates_and_homes(0, 0)
                    gates_and_homes(1, 1)
                    copy_token(1, 0)
                    split_hidden(t, par)
                    split_x(t + 2, par)

                def step(turn, t, par, more=True):
                    y_gated(turn if par else turn - 1, t - 1, 1 - par)
                    gates_and_homes(t + 1, 1 - par)
                    if more:
                        copy_token(turn + 1, par)
                    split_hidden(t, par)
                    if more:
                        split_x(t + 2, par)

                def end(turn, t, par):
                    y_gated(turn if par else turn - 1, t - 1, 1 - par)
                    split_hidden(t, par)
                    y_gated(turn, t, par)

                moe_pipeline(first, step, end, lambda count: steps.repeat(count, 2 * 4))

            @block.tensor
            def _(pe):
                def turn_x(turn, t, par):
                    pe.wait_ge(xm_in[par], turn * 16 + 16)
                    wait(pe, s["x_ready"], t)
                    for c in range(C):
                        ins = nc.tensor.transpose(p_x[:, c, :], xm[par][:, c * P:(c + 1) * P], const["identity"][:, :])
                    ins.then_inc(s["x_mm"], 1)

                def pairs(hi, lo, w_hi, w_lo, per, expert):
                    own_hi, own_lo = (w[:, bass.ds(expert * per, per), :] for w in (w_hi, w_lo))
                    return [((hi[:, c, :], lo[:, c, :]), (own_hi[:, c, :], own_lo[:, c, :])) for c in range(per)]

                def up(t, par, expert):
                    pe.wait_ge(s["x_split"], t + 1)
                    wait(pe, s["hid_ready"], t - 1)
                    split_products(nc, p_h[par][:, :], pairs(x_hi[par], x_lo[par], w1_hi, w1_lo, C, expert))\
                        .then_inc(s["h_mm"], 1)

                def turn_hidden(t, par):
                    pe.wait_ge(s["hid_ready"], t + 1)
                    wait(pe, s["hid_split"], 2 * t)
                    for half in range(2):
                        for c in range(K4 // 2):
                            cols = slice((half * K4 // 2 + c) * P, (half * K4 // 2 + c + 1) * P)
                            ins = nc.tensor.transpose(p_t[half][:, c, :], hid[par][:, cols], const["identity"][:, :])
                        ins.then_inc(s["t_mm"], 1)

                def down(t, par, expert):
                    wait(pe, s["y_ready"], t - 1)
                    parts = pairs(hid_hi[par], hid_lo[par], w2_hi, w2_lo, K4, expert)
                    for half, cs in enumerate(HALVES):
                        pe.wait_ge(s["hid_split"], 2 * t + half + 1)
                        ins = split_products(nc, p_y[par][:, 0:D], parts[cs], start=(half == 0), stop=(half == 1))
                    ins.then_inc(s["y_mm"], 1)

                expert_reg = [pe.alloc_register(f"expert{i}") for i in range(2)]

                def read_expert(t, par):
                    pe.reg_load(expert_reg[par], expert_i[0:1, bass.ds(t, 1)])

                def expert_of(par):
                    return pe.snap(expert_reg[par], min_val=0, max_val=E - 1)

                def first(turn, t, par):
                    turn_x(0, 0, 0)
                    turn_x(0, 1, 1)
                    read_expert(0, 0)
                    read_expert(1, 1)
                    pe.wait_ge(s["w1_split"], 1)
                    up(0, 0, expert_of(0))
                    turn_hidden(0, 0)
                    turn_x(1, 2, 0)
                    up(1, 1, expert_of(1))
                    pe.wait_ge(s["w2_split"], 2)

                def step(turn, t, par, more=True):
                    down(t - 1, 1 - par, expert_of(1 - par))
                    read_expert(t + 1, 1 - par)
                    turn_hidden(t, par)
                    if more:
                        turn_x(turn + 1, t + 2, par)
                    up(t + 1, 1 - par, expert_of(1 - par))

                def end(turn, t, par):
                    down(t - 1, 1 - par, expert_of(1 - par))
                    turn_hidden(t, par)
                    down(t, par, expert_of(par))

                pe.wait_ge(s["table_ready"], 1)
                moe_pipeline(first, step, end, plain_repeat(pe))


def add_up_and_end(nc, mem_all, dram, const, keep):
    DEPTH = 4
    TURNS = TILES // 2 // DEPTH
    with ExitStack() as stack:
        m = Memory(nc, stack, "en")
        y = [[m.sb(f"y{i}{k}", [P, 2, D]) for k in range(2)] for i in range(DEPTH)]
        out = [m.sb(f"out{i}", [P, 2, D]) for i in range(2)]
        stats, mv, var, rstd = ([m.sb(f"{n}{i}", shape) for i in range(2)] for n, shape in (
            ("stats", [P, 2, 6]), ("mv", [P, 2, 2]), ("var", [P, 2]), ("rstd", [P, 2])))
        sum_0, sum_1, var_ready, var_done, rstd_ready, out_ready, dve_step = (
            m.sem(n) for n in ("sum_0", "sum_1", "var_ready", "var_done", "rstd_ready", "out_ready", "dve_step"))
        y_in = [m.sem(f"y_in{i}") for i in range(DEPTH)]
        out_stored = [m.sem(f"out_stored{i}") for i in range(2)]
        resid = keep["resid"]

        def turns(step, repeat):
            for i in range(DEPTH):
                step(0, i, i)
            for turn in repeat(TURNS - 1):
                for i in range(DEPTH):
                    step(turn + 1, (turn + 1) * DEPTH + i, i)

        def plain_repeat(eng):
            def repeat(count):
                with eng.Fori(0, count) as j:
                    yield j
            return repeat

        with nc.Block() as block:

            @block.sync
            def _(sp):
                def load(turn, j, i):
                    wait(sp, out_ready, j - DEPTH + 1)
                    for k in range(2):
                        sp.dma_start(y[i][k][:, :, :], dram["results_of"][k][:, bass.ds(j * 2, 2), :]).then_inc(y_in[i], 16)

                turns(load, plain_repeat(sp))

            @block.scalar
            def _(act):
                def store(turn, j, i):
                    act.wait_ge(out_ready, j + 1)
                    act.dma_start(dram["out_group"][:, bass.ds(j * 2, 2), :], out[i % 2][:, :, :]).then_inc(out_stored[i % 2], 16)

                turns(store, plain_repeat(act))
                for i in range(2):
                    act.wait_ge(out_stored[i], TILES // 4 * 16)

            @block.gpsimd
            def _(pool):
                def root(j, par):
                    wait_apart(pool, var_ready, j + 1)
                    nc.gpsimd.tensor_scalar(var[par][:, :], mv[par][:, :, 1], EPS, None, ALU.add).then_inc(var_done, 1)
                    pool.wait_ge(var_done, j + 1)
                    nc.gpsimd.tensor_tensor(rstd[par][:, :], var[par][:, :], const["minus_half"][:, 0:2], ALU.pow)\
                      .then_inc(rstd_ready, 1)

                def step(turn, j, i):
                    pool.wait_ge(y_in[i], turn * 32 + 32)
                    nc.gpsimd.tensor_tensor(y[i][0][:, :, :], y[i][0][:, :, :], resid[:, bass.ds(j * 2, 2), :], ALU.add)\
                      .then_inc(sum_0, 1)
                    if not isinstance(j, int) or j > 0:
                        root(j - 1, (i - 1) % 2)

                turns(step, plain_repeat(pool))
                root(TILES // 2 - 1, 1)

            @block.vector
            def _(dve):
                V = nc.vector
                steps = Steps(dve, dve_step)

                def normalise(j, i):
                    dve.wait_ge(rstd_ready, j + 1)
                    wait(dve, out_stored[i % 2], (j - i) * 8 + i // 2 * 16)
                    for t in range(2):
                        ins = V.tensor_scalar(out[i % 2][:, t, :], y[i][0][:, t, :], mv[i % 2][:, t, 0:1],
                                              rstd[i % 2][:, t:t + 1], ALU.subtract, ALU.mult)
                        if t == 0:
                            steps.mark(ins)
                    ins.then_inc(out_ready, 1)

                def step(turn, j, i):
                    dve.wait_ge(sum_0, j + 1)
                    V.tensor_tensor(y[i][0][:, :, :], y[i][0][:, :, :], y[i][1][:, :, :], ALU.add).then_inc(sum_1, 1)
                    dve.wait_ge(sum_1, j + 1)
                    layer_norm_stats(steps, nc, y[i][0], stats[i % 2], mv[i % 2], var_ready)
                    if not isinstance(j, int) or j > 0:
                        normalise(j - 1, (i - 1) % DEPTH)

                turns(step, lambda count: steps.repeat(count, 4 * DEPTH))
                normalise(TILES // 2 - 1, DEPTH - 1)


def constants(nc, m, dram):
    const = {
        "identity": m.sb("identity", [P, P]),
        "head_mask": m.sb("head_mask", [P, 8]),
        "minus_half": m.sb("minus_half", [P, NI]),
    }
    step = m.sem("const_step")
    with nc.Block() as block:

        @block.gpsimd
        def _(pool):
            nc.gpsimd.memset(const["identity"][:, :], 0.0).then_inc(step, 1)
            nc.gpsimd.memset(const["head_mask"][:, :], 1.0).then_inc(step, 1)
            nc.gpsimd.memset(const["minus_half"][:, :], -0.5).then_inc(step, 1)
            pool.wait_ge(step, 3)
            nc.gpsimd.affine_select(out=const["identity"][:, :], in_=const["identity"][:, :], compare_op=ALU.not_equal,
                                    fill=1.0, base=0, pattern=[[-1, P]], channel_multiplier=1).then_inc(step, 1)
            nc.gpsimd.affine_select(out=const["head_mask"][:, :], in_=const["head_mask"][:, :], compare_op=ALU.is_ge,
                                    fill=0.0, base=0, pattern=[[-HD, 8]], channel_multiplier=1).then_inc(step, 1)
            pool.wait_ge(step, 5)
            nc.gpsimd.affine_select(out=const["head_mask"][:, :], in_=const["head_mask"][:, :], compare_op=ALU.is_ge,
                                    fill=0.0, base=HD - 1, pattern=[[HD, 8]], channel_multiplier=-1).then_inc(step, 1)
            pool.wait_ge(step, 6)
    return const


def decoder_kernel(nc, dram):
    with ExitStack() as stack:
        m = Memory(nc, stack, "all")
        def scratch(name, shape):
            return nc.dram_tensor(name, shape, F32, kind="Internal").ap()
        rows = "(t p) d -> p t d"
        dram = dict(dram)
        dram["x_rows"] = dram["x"].rearrange(rows, p=P)
        x2 = scratch("x2_rows", [TOKENS, D])
        dram["x2"] = x2.rearrange(rows, p=P)
        dram["x2_group"] = x2.rearrange("(p i) d -> p i d", p=P)
        dram["dispatched"] = scratch("dispatched", [E * SEGMENT, ROW])
        dram["results"] = scratch("results", [2 * TOKENS + 2 * P, D])
        dram["results_of"] = [dram["results"][k * TOKENS:(k + 1) * TOKENS, :].rearrange("(p i) d -> p i d", p=P)
                              for k in range(2)]
        dram["out_group"] = dram["out"].rearrange("(p i) d -> p i d", p=P)
        const = constants(nc, m, dram)
        keep = {"resid": m.sb("resid", [P, TILES, D]), "x2_in": m.sem("x2_in")}
        with ExitStack() as attention_stack:
            n = Memory(nc, attention_stack, "shared")
            kept = {"w_qkv_hi": n.sb("w_qkv_hi", [P, C, 3 * D], F32R), "w_qkv_lo": n.sb("w_qkv_lo", [P, C, 3 * D], F32R),
                    "w_out_hi": n.sb("w_out_hi", [P, C, D], F32R), "w_out_lo": n.sb("w_out_lo", [P, C, D], F32R),
                    "w_v": n.sb("w_v", [P, C, D]),
                    "x_t": [n.sb(f"x_t{i}", [P, C, N]) for i in range(2)], "x_t_in": [n.sem(f"x_t_in{i}") for i in range(2)],
                    "b_out": n.sb("b_out", [P, D]), "b_v": n.sb("b_v", [P, D]), "qk": n.sb("qk", [P, C, B * CTX]),
                    "k_bias": n.sb("k_bias", [P, B * CTX]), "weights_in": n.sem("weights_in")}
            context_keys(nc, m, dram, const, kept)
            two_attentions(nc, m, dram, const, kept, keep)
        keep |= {
            "w1": m.sb("w1", [P, E * C, F]),
            "w2": m.sb("w2", [P, E * K4, D]),
            "ln2_w": m.sb("ln2_w", [P, C]),
            "ln2_b": m.sb("ln2_b", [P, C]),
            "xh2": m.sb("xh2", [P, NI, ROW]),
            "slot_u": m.sb("slot_u", [P, NI, 2], U32),
            "count": m.sb("count", [P, E]),
            "experts": m.sb("experts", [P, E]),
            "segments": m.sb("segments", [P, E]),
            "one_e": m.sb("one_e", [P, E]),
            "tile_no": m.sb("tile_no", [P, MOE_TILES]),
            "tail": m.sb("tail", [P, 2, ROW]),
            "scattered": m.sem("scattered"),
            "experts_in": m.sem("experts_in"),
        }
        batch_axis_attention(nc, m, dram, const, keep)
        experts(nc, m, dram, const, keep)
        add_up_and_end(nc, m, dram, const, keep)


def kernel(x, ctx_1024, L0_attn_w_qkv, L0_attn_w_out, L0_attn_b_out, L0_xattn_Wq, L0_xattn_bq, L0_xattn_Wk, L0_xattn_bk,
           L0_xattn_Wv, L0_xattn_bv, L0_ffn_ln1_weight, L0_ffn_ln1_bias, L0_ffn_ln2_weight, L0_ffn_ln2_bias,
           L0_ffn_qkv_weight, L0_ffn_proj_weight, L0_ffn_router_weight, L0_ffn_moe_w1, L0_ffn_moe_w2):
    from concourse import bacc
    from concourse.bass_utils import run_bass_kernel_spmd

    def dense(a):
        return np.ascontiguousarray(a)

    def features_first(a):
        return dense(np.asarray(a).T.reshape(C, P, -1).transpose(1, 0, 2))

    def columns(a):
        return dense(np.asarray(a).reshape(C, P).T)

    x_rows = np.asarray(x).reshape(TOKENS, D)
    qk_rows = (H + KV) * HD
    arrays = {
        "x": dense(x_rows),
        "x_t": features_first(x_rows),
        "w_qkv": features_first(L0_attn_w_qkv),
        "w_out": features_first(L0_attn_w_out),
        "b_out": dense(L0_attn_b_out),
        "ctx_t": features_first(np.asarray(ctx_1024).reshape(-1, D)),
        "xw_q": dense(np.asarray(L0_xattn_Wq).reshape(C, P, D).transpose(1, 0, 2)),
        "xw_k": features_first(L0_xattn_Wk),
        "xw_v": features_first(L0_xattn_Wv),
        "xb_q": columns(L0_xattn_bq),
        "xb_k": columns(L0_xattn_bk),
        "xb_v": dense(L0_xattn_bv),
        "w_qk": features_first(np.asarray(L0_ffn_qkv_weight)[:qk_rows]),
        "w_v": features_first(np.asarray(L0_ffn_qkv_weight)[qk_rows:]),
        "w_proj": features_first(L0_ffn_proj_weight),
        "w_router": features_first(L0_ffn_router_weight),
        "moe_w1": dense(np.asarray(L0_ffn_moe_w1).reshape(E, C, P, F).transpose(2, 0, 1, 3)),
        "moe_w2": dense(np.asarray(L0_ffn_moe_w2).reshape(E, K4, P, D).transpose(2, 0, 1, 3)),
        "ln1_w": columns(L0_ffn_ln1_weight),
        "ln1_b": columns(L0_ffn_ln1_bias),
        "ln2_w": columns(L0_ffn_ln2_weight),
        "ln2_b": columns(L0_ffn_ln2_bias),
    }
    nc = bacc.Bacc("TRN2", target_bir_lowering=False, num_devices=1)
    dram = {
        name: nc.dram_tensor(f"in_{name}_dram", a.shape, mybir.dt.from_np(a.dtype), kind="ExternalInput").ap()
        for name, a in arrays.items()
    }
    dram["out"] = nc.dram_tensor("out_0_dram", (TOKENS, D), F32, kind="ExternalOutput").ap()
    decoder_kernel(nc, dram)
    r = run_bass_kernel_spmd(nc, [{f"in_{name}_dram": a for name, a in arrays.items()}], core_ids=[0])
    return r.results[0]["out_0_dram"].reshape(B, N, D)
```
